# Optimizing a Trainium2 kernel written in Bass

```python
import numpy as np
import jax
import jax.numpy as jnp

def _softmax(x, axis=-1):
    return jax.nn.softmax(x, axis=axis)

def _gelu(x):
    return jax.nn.gelu(x, approximate=True)

def _silu(x):
    return jax.nn.silu(x)

def _sigmoid(x):
    return jax.nn.sigmoid(x)

def _layernorm(x, axis=-1, eps=1e-05):
    m = jnp.mean(x, axis=axis, keepdims=True)
    v = jnp.var(x, axis=axis, keepdims=True)
    return (x - m) / jnp.sqrt(v + eps)

def _scatter_add(tgt, idx, src, axis=0):
    return tgt.at[idx].add(src)

def _segment_sum(src, seg, n):
    return jax.ops.segment_sum(src, seg, n)
kernel_name = 'mk_gnn_ffn_d4_gnn_r8_c44b4f'

def setup_inputs(seed: int=0):
    np.random.seed(seed)
    _w = jnp.asarray

    def _rec_inputs():
        import jax
        import jax.numpy as jnp
        _gk = jax.random.key(seed)
        x = -8.776e-05 + 1 * jax.random.normal(jax.random.fold_in(_gk, 1), (1250, 512), jnp.float32)
        src = jax.random.randint(jax.random.fold_in(_gk, 2), (40000,), 0, 1250, jnp.int32)
        dst = jax.random.randint(jax.random.fold_in(_gk, 3), (40000,), 0, 1250, jnp.int32)
        _o = jnp.argsort(dst, stable=True)
        src = src[_o]
        dst = dst[_o]
        edge_weight = jax.random.uniform(jax.random.fold_in(_gk, 12), (40000,), jnp.float32, 0.0, 0.999998)
        return (x, src, dst, edge_weight)
    x, src, dst, edge_weight = _rec_inputs()

    def _L0_gnn_setup():
        import jax, jax.numpy as jnp
        import numpy as np
        N_NODES = 1250

        def sage_conv(x, src, dst, Wl, bl, Wr):
            msg = x[src]
            summed = jax.ops.segment_sum(msg, dst, num_segments=N_NODES)
            cnt = jax.ops.segment_sum(jnp.ones((src.shape[0],), x.dtype), dst, num_segments=N_NODES)
            mean = summed / jnp.maximum(cnt, 1.0)[:, None]
            return mean @ Wl.T + bl + x @ Wr.T
        key = jax.random.key(seed)
        ks = jax.random.split(key, 7)
        d = 512
        E = 20000
        x = jax.random.normal(ks[0], (N_NODES, d), jnp.float32)
        edge_index = jax.random.randint(ks[1], (2, E), 0, N_NODES, jnp.int64)
        s = 1.0 / np.sqrt(d)
        Wl0 = jax.random.normal(ks[2], (d, d), jnp.float32) * s
        bl0 = jnp.zeros((d,), jnp.float32)
        Wr0 = jax.random.normal(ks[3], (d, d), jnp.float32) * s
        Wl1 = jax.random.normal(ks[4], (d, d), jnp.float32) * s
        bl1 = jnp.zeros((d,), jnp.float32)
        Wr1 = jax.random.normal(ks[5], (d, d), jnp.float32) * s
        return {'x': x, 'edge_index': edge_index, 'Wl0': Wl0, 'bl0': bl0, 'Wr0': Wr0, 'Wl1': Wl1, 'bl1': bl1, 'Wr1': Wr1}
    _L0_gnn_all = _L0_gnn_setup()
    _L0_gnn_in = {k: v for k, v in _L0_gnn_all.items() if k in ('Wl0', 'bl0', 'Wr0', 'Wl1', 'bl1', 'Wr1')}
    del _L0_gnn_all

    def _L0_ffn_setup():
        import jax, jax.numpy as jnp
        import numpy as np
        EPS = 1e-05
        NUM_HEADS = 8
        TOP_K = 2
        CAP_FACTOR = 2

        def layernorm(x, g, b):
            m = jnp.mean(x, axis=-1, keepdims=True)
            v = jnp.var(x, axis=-1, keepdims=True)
            return (x - m) * jax.lax.rsqrt(v + EPS) * g + b
        key = jax.random.key(seed)
        ks = jax.random.split(key, 16)
        B, S, H, E, F = (2, 256, 512, 64, 256)
        s = 0.02
        return {'x': jax.random.normal(ks[0], (B, S, H), jnp.float32), 'ln1_g': jnp.ones((H,), jnp.float32), 'ln1_b': jnp.zeros((H,), jnp.float32), 'wq': jax.random.normal(ks[1], (H, H), jnp.float32) * s, 'wk': jax.random.normal(ks[2], (H, H), jnp.float32) * s, 'wv': jax.random.normal(ks[3], (H, H), jnp.float32) * s, 'wo': jax.random.normal(ks[4], (H, H), jnp.float32) * s, 'ln2_g': jnp.ones((H,), jnp.float32), 'ln2_b': jnp.zeros((H,), jnp.float32), 'wr': jax.random.normal(ks[5], (H, E), jnp.float32) * s, 'w1': jax.random.normal(ks[6], (E, H, F), jnp.float32) * s, 'b1': jnp.zeros((E, F), jnp.float32), 'w2': jax.random.normal(ks[7], (E, F, H), jnp.float32) * s, 'b2': jnp.zeros((E, H), jnp.float32)}
    _L0_ffn_all = _L0_ffn_setup()
    _L0_ffn_in = {k: v for k, v in _L0_ffn_all.items() if k in ('ln1_g', 'ln1_b', 'wq', 'wk', 'wv', 'wo', 'ln2_g', 'ln2_b', 'wr', 'w1', 'b1', 'w2', 'b2')}
    del _L0_ffn_all

    def _L1_gnn_setup():
        import jax, jax.numpy as jnp
        import numpy as np
        N_NODES = 6250
        key = jax.random.key(seed)
        k1, k2, k3, k4, k5 = jax.random.split(key, 5)
        N, E, DIN, DOUT = (N_NODES, 200000, 512, 512)
        x = jax.random.normal(k1, (N, DIN), dtype=jnp.float32)
        weight = jax.random.normal(k2, (DIN, DOUT), dtype=jnp.float32) * (1.0 / np.sqrt(DIN))
        bias = jax.random.normal(k3, (DOUT,), dtype=jnp.float32) * 0.02
        edge_index = jax.random.randint(k4, (2, E), 0, N, dtype=jnp.int64)
        edge_vals = jax.random.uniform(k5, (E,), dtype=jnp.float32)
        return {'x': x, 'weight': weight, 'bias': bias, 'edge_index': edge_index, 'edge_vals': edge_vals}
    _L1_gnn_all = _L1_gnn_setup()
    _L1_gnn_in = {k: v for k, v in _L1_gnn_all.items() if k in ('weight', 'bias')}
    del _L1_gnn_all

    def _L1_ffn_setup():
        import jax, jax.numpy as jnp
        import numpy as np
        B, S, D, F, E = (8, 512, 512, 256, 8)
        INIT_LAMBDA = 0.2
        LN_EPS = 1e-05
        LN_MERGE = 0.03
        key = jax.random.key(seed)
        ks = jax.random.split(key, 12)
        n = lambda k, shp, s=1.0: jax.random.normal(k, shp, dtype=jnp.float32) * s
        return {'hidden_states': n(ks[0], (B, S, D)), 'gfc1_w': n(ks[1], (D, D), 0.01), 'gfc1_b': jnp.zeros((D,), jnp.float32), 'gfc2_w': n(ks[2], (E, D), 0.01), 'gfc2_b': jnp.full((E,), INIT_LAMBDA, dtype=jnp.float32), 'W1': n(ks[3], (F, D), 0.02), 'b1': jnp.zeros((F,), jnp.float32), 'W2': n(ks[4], (D, F), 0.02), 'b2': jnp.zeros((D,), jnp.float32), 'ln_g': jnp.ones((D,), jnp.float32), 'ln_b': jnp.zeros((D,), jnp.float32), 'tv_W1': n(ks[5], (E, F, D), 0.02), 'tv_b1': n(ks[6], (E, F), 0.02), 'tv_W2': n(ks[7], (E, D, F), 0.02), 'tv_b2': n(ks[8], (E, D), 0.02), 'tv_ln_g': n(ks[9], (E, D), 0.02), 'tv_ln_b': n(ks[10], (E, D), 0.02)}
    _L1_ffn_all = _L1_ffn_setup()
    _L1_ffn_in = {k: v for k, v in _L1_ffn_all.items() if k in ('gfc1_w', 'gfc1_b', 'gfc2_w', 'gfc2_b', 'W1', 'b1', 'W2', 'b2', 'ln_g', 'ln_b', 'tv_W1', 'tv_b1', 'tv_W2', 'tv_b2', 'tv_ln_g', 'tv_ln_b')}
    del _L1_ffn_all

    def _L2_gnn_setup():
        import jax, jax.numpy as jnp
        import numpy as np
        BN_EPS = 1e-05
        N_NODES, N_EDGES, D, N_LAYERS = (6250, 50000, 512, 3)
        key = jax.random.key(seed)
        k_x, k_e, k_w = jax.random.split(key, 3)
        x = jax.random.normal(k_x, (N_NODES, D), dtype=jnp.float32)
        edge_index = jax.random.randint(k_e, (2, N_EDGES), 0, N_NODES, dtype=jnp.int64)
        W = jax.random.normal(k_w, (N_LAYERS, D, D), dtype=jnp.float32) * (1.0 / np.sqrt(D))
        b = jnp.zeros((N_LAYERS, D), dtype=jnp.float32)
        gamma = jnp.ones((N_LAYERS, D), dtype=jnp.float32)
        beta = jnp.zeros((N_LAYERS, D), dtype=jnp.float32)
        return {'x': x, 'edge_index': edge_index, 'W': W, 'b': b, 'gamma': gamma, 'beta': beta}
    _L2_gnn_all = _L2_gnn_setup()
    _L2_gnn_in = {k: v for k, v in _L2_gnn_all.items() if k in ('W', 'b', 'gamma', 'beta')}
    del _L2_gnn_all

    def _L2_ffn_setup():
        import jax, jax.numpy as jnp
        import numpy as np
        B, S, H, E, F = (4, 256, 512, 8, 512)
        key = jax.random.key(seed)
        k = jax.random.split(key, 7)
        x = jax.random.normal(k[0], (B, S, H), dtype=jnp.float32)
        Wr = jax.random.normal(k[1], (H, E), dtype=jnp.float32) / np.sqrt(H)
        br = jnp.zeros((E,), dtype=jnp.float32)
        W1 = jax.random.normal(k[2], (E, H, F), dtype=jnp.float32) / np.sqrt(H)
        b1 = jnp.zeros((E, F), dtype=jnp.float32)
        W2 = jax.random.normal(k[3], (E, F, H), dtype=jnp.float32) / np.sqrt(F)
        b2 = jnp.zeros((E, H), dtype=jnp.float32)
        return {'x': x, 'Wr': Wr, 'br': br, 'W1': W1, 'b1': b1, 'W2': W2, 'b2': b2}
    _L2_ffn_all = _L2_ffn_setup()
    _L2_ffn_in = {k: v for k, v in _L2_ffn_all.items() if k in ('Wr', 'br', 'W1', 'b1', 'W2', 'b2')}
    del _L2_ffn_all

    def _L3_gnn_setup():
        import jax, jax.numpy as jnp
        import numpy as np
        N_NODES = 2500
        N_EDGES = 80000
        D_IN = 512
        D_OUT = 512
        key = jax.random.key(seed)
        kx, ke, kw, kb = jax.random.split(key, 4)
        X = jax.random.normal(kx, (N_NODES, D_IN), dtype=jnp.float32)
        edge_index = jax.random.randint(ke, (2, N_EDGES), 0, N_NODES, dtype=jnp.int32)
        W = jax.random.normal(kw, (D_IN, D_OUT), dtype=jnp.float32) / np.sqrt(D_IN)
        b = jax.random.normal(kb, (D_OUT,), dtype=jnp.float32) * 0.01
        return {'X': X, 'edge_index': edge_index, 'W': W, 'b': b}
    _L3_gnn_all = _L3_gnn_setup()
    _L3_gnn_in = {k: v for k, v in _L3_gnn_all.items() if k in ('W', 'b')}
    del _L3_gnn_all

    def _L3_ffn_setup():
        import jax, jax.numpy as jnp
        import numpy as np
        D_MODEL = 512
        D_FF = 256
        N_HEADS = 8
        N_EXPERTS = 8
        TOP_K = 2
        CAPACITY_FACTOR = 1.6
        BATCH = 512
        SEQ = 16
        LN_EPS = 1e-05

        def _layernorm(x, g, b):
            mu = x.mean(-1, keepdims=True)
            var = ((x - mu) ** 2).mean(-1, keepdims=True)
            return (x - mu) * jax.lax.rsqrt(var + LN_EPS) * g + b

        def _moe(xf, router_w, router_b, w1, b1, w2, b2):
            T = xf.shape[0]
            probs = jax.nn.softmax(xf @ router_w + router_b, axis=-1)
            _, topk_idx = jax.lax.top_k(probs, TOP_K)
            capacity = int(np.ceil(T * CAPACITY_FACTOR / N_EXPERTS))
            out = jnp.zeros_like(xf)
            tok = jnp.arange(T)
            for i in range(N_EXPERTS):
                mask = (topk_idx == i).any(-1)
                pos = jnp.where(mask, tok, T)
                sel = jnp.sort(pos)[:capacity]
                xi = xf[jnp.minimum(sel, T - 1)]
                hi = jax.nn.gelu(xi @ w1[i] + b1[i], approximate=False)
                yi = hi @ w2[i] + b2[i]
                out = out.at[sel].set(yi, mode='drop')
            return out
        key = jax.random.key(seed)
        ks = jax.random.split(key, 24)
        s = 0.02
        d, f, e = (D_MODEL, D_FF, N_EXPERTS)
        inp = {'x': jax.random.normal(ks[0], (BATCH, SEQ, d), dtype=jnp.float32), 'ln1_g': jnp.ones((d,), jnp.float32), 'ln1_b': jnp.zeros((d,), jnp.float32), 'ln2_g': jnp.ones((d,), jnp.float32), 'ln2_b': jnp.zeros((d,), jnp.float32), 'wq': jax.random.normal(ks[1], (d, d)) * s, 'bq': jnp.zeros((d,)), 'wk': jax.random.normal(ks[2], (d, d)) * s, 'bk': jnp.zeros((d,)), 'wv': jax.random.normal(ks[3], (d, d)) * s, 'bv': jnp.zeros((d,)), 'wo': jax.random.normal(ks[4], (d, d)) * s, 'bo': jnp.zeros((d,)), 'router_w': jax.random.normal(ks[5], (d, e)) * s, 'router_b': jnp.zeros((e,)), 'w1': jax.random.normal(ks[6], (e, d, f)) * s, 'b1': jnp.zeros((e, f)), 'w2': jax.random.normal(ks[7], (e, f, d)) * s, 'b2': jnp.zeros((e, d))}
        return inp
    _L3_ffn_all = _L3_ffn_setup()
    _L3_ffn_in = {k: v for k, v in _L3_ffn_all.items() if k in ('ln1_g', 'ln1_b', 'ln2_g', 'ln2_b', 'wq', 'bq', 'wk', 'bk', 'wv', 'bv', 'wo', 'bo', 'router_w', 'router_b', 'w1', 'b1', 'w2', 'b2')}
    del _L3_ffn_all
    return {'x': x, 'src': src, 'dst': dst, 'edge_weight': edge_weight, 'L0_gnn_Wl0': _L0_gnn_in['Wl0'], 'L0_gnn_bl0': _L0_gnn_in['bl0'], 'L0_gnn_Wr0': _L0_gnn_in['Wr0'], 'L0_gnn_Wl1': _L0_gnn_in['Wl1'], 'L0_gnn_bl1': _L0_gnn_in['bl1'], 'L0_gnn_Wr1': _L0_gnn_in['Wr1'], 'L0_ffn_ln1_g': _L0_ffn_in['ln1_g'], 'L0_ffn_ln1_b': _L0_ffn_in['ln1_b'], 'L0_ffn_wq': _L0_ffn_in['wq'], 'L0_ffn_wk': _L0_ffn_in['wk'], 'L0_ffn_wv': _L0_ffn_in['wv'], 'L0_ffn_wo': _L0_ffn_in['wo'], 'L0_ffn_ln2_g': _L0_ffn_in['ln2_g'], 'L0_ffn_ln2_b': _L0_ffn_in['ln2_b'], 'L0_ffn_wr': _L0_ffn_in['wr'], 'L0_ffn_w1': _L0_ffn_in['w1'], 'L0_ffn_b1': _L0_ffn_in['b1'], 'L0_ffn_w2': _L0_ffn_in['w2'], 'L0_ffn_b2': _L0_ffn_in['b2'], 'L1_gnn_weight': _L1_gnn_in['weight'], 'L1_gnn_bias': _L1_gnn_in['bias'], 'L1_ffn_gfc1_w': _L1_ffn_in['gfc1_w'], 'L1_ffn_gfc1_b': _L1_ffn_in['gfc1_b'], 'L1_ffn_gfc2_w': _L1_ffn_in['gfc2_w'], 'L1_ffn_gfc2_b': _L1_ffn_in['gfc2_b'], 'L1_ffn_W1': _L1_ffn_in['W1'], 'L1_ffn_b1': _L1_ffn_in['b1'], 'L1_ffn_W2': _L1_ffn_in['W2'], 'L1_ffn_b2': _L1_ffn_in['b2'], 'L1_ffn_ln_g': _L1_ffn_in['ln_g'], 'L1_ffn_ln_b': _L1_ffn_in['ln_b'], 'L1_ffn_tv_W1': _L1_ffn_in['tv_W1'], 'L1_ffn_tv_b1': _L1_ffn_in['tv_b1'], 'L1_ffn_tv_W2': _L1_ffn_in['tv_W2'], 'L1_ffn_tv_b2': _L1_ffn_in['tv_b2'], 'L1_ffn_tv_ln_g': _L1_ffn_in['tv_ln_g'], 'L1_ffn_tv_ln_b': _L1_ffn_in['tv_ln_b'], 'L2_gnn_W': _L2_gnn_in['W'], 'L2_gnn_b': _L2_gnn_in['b'], 'L2_gnn_gamma': _L2_gnn_in['gamma'], 'L2_gnn_beta': _L2_gnn_in['beta'], 'L2_ffn_Wr': _L2_ffn_in['Wr'], 'L2_ffn_br': _L2_ffn_in['br'], 'L2_ffn_W1': _L2_ffn_in['W1'], 'L2_ffn_b1': _L2_ffn_in['b1'], 'L2_ffn_W2': _L2_ffn_in['W2'], 'L2_ffn_b2': _L2_ffn_in['b2'], 'L3_gnn_W': _L3_gnn_in['W'], 'L3_gnn_b': _L3_gnn_in['b'], 'L3_ffn_ln1_g': _L3_ffn_in['ln1_g'], 'L3_ffn_ln1_b': _L3_ffn_in['ln1_b'], 'L3_ffn_ln2_g': _L3_ffn_in['ln2_g'], 'L3_ffn_ln2_b': _L3_ffn_in['ln2_b'], 'L3_ffn_wq': _L3_ffn_in['wq'], 'L3_ffn_bq': _L3_ffn_in['bq'], 'L3_ffn_wk': _L3_ffn_in['wk'], 'L3_ffn_bk': _L3_ffn_in['bk'], 'L3_ffn_wv': _L3_ffn_in['wv'], 'L3_ffn_bv': _L3_ffn_in['bv'], 'L3_ffn_wo': _L3_ffn_in['wo'], 'L3_ffn_bo': _L3_ffn_in['bo'], 'L3_ffn_router_w': _L3_ffn_in['router_w'], 'L3_ffn_router_b': _L3_ffn_in['router_b'], 'L3_ffn_w1': _L3_ffn_in['w1'], 'L3_ffn_b1': _L3_ffn_in['b1'], 'L3_ffn_w2': _L3_ffn_in['w2'], 'L3_ffn_b2': _L3_ffn_in['b2']}

def reference(x, src, dst, edge_weight, L0_gnn_Wl0, L0_gnn_bl0, L0_gnn_Wr0, L0_gnn_Wl1, L0_gnn_bl1, L0_gnn_Wr1, L0_ffn_ln1_g, L0_ffn_ln1_b, L0_ffn_wq, L0_ffn_wk, L0_ffn_wv, L0_ffn_wo, L0_ffn_ln2_g, L0_ffn_ln2_b, L0_ffn_wr, L0_ffn_w1, L0_ffn_b1, L0_ffn_w2, L0_ffn_b2, L1_gnn_weight, L1_gnn_bias, L1_ffn_gfc1_w, L1_ffn_gfc1_b, L1_ffn_gfc2_w, L1_ffn_gfc2_b, L1_ffn_W1, L1_ffn_b1, L1_ffn_W2, L1_ffn_b2, L1_ffn_ln_g, L1_ffn_ln_b, L1_ffn_tv_W1, L1_ffn_tv_b1, L1_ffn_tv_W2, L1_ffn_tv_b2, L1_ffn_tv_ln_g, L1_ffn_tv_ln_b, L2_gnn_W, L2_gnn_b, L2_gnn_gamma, L2_gnn_beta, L2_ffn_Wr, L2_ffn_br, L2_ffn_W1, L2_ffn_b1, L2_ffn_W2, L2_ffn_b2, L3_gnn_W, L3_gnn_b, L3_ffn_ln1_g, L3_ffn_ln1_b, L3_ffn_ln2_g, L3_ffn_ln2_b, L3_ffn_wq, L3_ffn_bq, L3_ffn_wk, L3_ffn_bk, L3_ffn_wv, L3_ffn_bv, L3_ffn_wo, L3_ffn_bo, L3_ffn_router_w, L3_ffn_router_b, L3_ffn_w1, L3_ffn_b1, L3_ffn_w2, L3_ffn_b2):
    import jax
    import jax.numpy as jnp

    def _L0_gnn_ref(x, edge_index, Wl0, bl0, Wr0, Wl1, bl1, Wr1):
        import jax, jax.numpy as jnp
        import numpy as np
        N_NODES = 1250

        def sage_conv(x, src, dst, Wl, bl, Wr):
            msg = x[src]
            summed = jax.ops.segment_sum(msg, dst, num_segments=N_NODES)
            cnt = jax.ops.segment_sum(jnp.ones((src.shape[0],), x.dtype), dst, num_segments=N_NODES)
            mean = summed / jnp.maximum(cnt, 1.0)[:, None]
            return mean @ Wl.T + bl + x @ Wr.T
        src, dst = (edge_index[0], edge_index[1])
        h = jax.nn.relu(sage_conv(x, src, dst, Wl0, bl0, Wr0))
        h = jax.nn.relu(sage_conv(h, src, dst, Wl1, bl1, Wr1))
        return h

    def _L0_ffn_ref(x, ln1_g, ln1_b, wq, wk, wv, wo, ln2_g, ln2_b, wr, w1, b1, w2, b2):
        import jax, jax.numpy as jnp
        import numpy as np
        EPS = 1e-05
        NUM_HEADS = 8
        TOP_K = 2
        CAP_FACTOR = 2

        def layernorm(x, g, b):
            m = jnp.mean(x, axis=-1, keepdims=True)
            v = jnp.var(x, axis=-1, keepdims=True)
            return (x - m) * jax.lax.rsqrt(v + EPS) * g + b
        B, S, H = x.shape
        NH = NUM_HEADS
        dh = H // NH
        x1 = layernorm(x, ln1_g, ln1_b)
        q = (x1 @ wq).reshape(B, S, NH, dh)
        k = (x1 @ wk).reshape(B, S, NH, dh)
        v = (x1 @ wv).reshape(B, S, NH, dh)
        scores = jnp.einsum('bqhd,bkhd->bhqk', q, k) * dh ** (-0.5)
        p = jax.nn.softmax(scores, axis=-1)
        attn_out = jnp.einsum('bhqk,bkhd->bqhd', p, v).reshape(B, S, H) @ wo
        x = x + attn_out
        x2 = layernorm(x, ln2_g, ln2_b).reshape(B * S, H)
        T = B * S
        E = wr.shape[1]
        C = CAP_FACTOR * (T * TOP_K // E)
        probs = jax.nn.softmax(x2 @ wr, axis=-1)
        gate_v, gate_i = jax.lax.top_k(probs, TOP_K)
        gate_v = gate_v / jnp.sum(gate_v, axis=-1, keepdims=True)
        ef = gate_i.reshape(-1)
        gf = gate_v.reshape(-1)
        oh = jax.nn.one_hot(ef, E, dtype=x2.dtype)
        pos = jnp.sum((jnp.cumsum(oh, axis=0) - oh) * oh, axis=1).astype(jnp.int32)
        keep = (pos < C).astype(x2.dtype)
        posc = jnp.minimum(pos, C - 1)
        tok = jnp.repeat(x2, TOP_K, axis=0) * keep[:, None]
        buf = jnp.zeros((E, C, H), x2.dtype).at[ef, posc].add(tok)
        h = jax.nn.gelu(jnp.einsum('ech,ehf->ecf', buf, w1) + b1[:, None, :])
        y = jnp.einsum('ecf,efh->ech', h, w2) + b2[:, None, :]
        ys = y[ef, posc] * (gf * keep)[:, None]
        moe_out = ys.reshape(T, TOP_K, H).sum(axis=1).reshape(B, S, H)
        return x + moe_out

    def _L1_gnn_ref(x, weight, bias, edge_index, edge_vals):
        import jax, jax.numpy as jnp
        import numpy as np
        N_NODES = 6250
        support = x @ weight
        dst, src = (edge_index[0], edge_index[1])
        msgs = support[src] * edge_vals[:, None]
        out = jax.ops.segment_sum(msgs, dst, num_segments=x.shape[0])
        return out + bias

    def _L1_ffn_ref(hidden_states, gfc1_w, gfc1_b, gfc2_w, gfc2_b, W1, b1, W2, b2, ln_g, ln_b, tv_W1, tv_b1, tv_W2, tv_b2, tv_ln_g, tv_ln_b):
        import jax, jax.numpy as jnp
        import numpy as np
        B, S, D, F, E = (8, 512, 512, 256, 8)
        INIT_LAMBDA = 0.2
        LN_EPS = 1e-05
        LN_MERGE = 0.03
        x = hidden_states
        gh = jax.nn.relu(jnp.einsum('bsd,hd->bsh', x, gfc1_w) + gfc1_b)
        g = (jnp.einsum('bsh,eh->bse', gh, gfc2_w) + gfc2_b).mean(axis=1)
        W1m = W1 + jnp.einsum('be,efd->bfd', g, tv_W1)
        b1m = b1 + g @ tv_b1
        W2m = W2 + jnp.einsum('be,edf->bdf', g, tv_W2)
        b2m = b2 + g @ tv_b2
        lng = ln_g + LN_MERGE * (tv_ln_g - ln_g).sum(axis=0)
        lnb = ln_b + LN_MERGE * (tv_ln_b - ln_b).sum(axis=0)
        h = jax.nn.relu(jnp.einsum('bsd,bfd->bsf', x, W1m) + b1m[:, None, :])
        out = jnp.einsum('bsf,bdf->bsd', h, W2m) + b2m[:, None, :]
        res = x + out
        mu = res.mean(axis=-1, keepdims=True)
        var = res.var(axis=-1, keepdims=True)
        return (res - mu) * jax.lax.rsqrt(var + LN_EPS) * lng + lnb

    def _L2_gnn_ref(x, W, b, gamma, beta, edge_index):
        import jax, jax.numpy as jnp
        import numpy as np
        BN_EPS = 1e-05
        N_NODES, N_EDGES, D, N_LAYERS = (6250, 50000, 512, 3)
        N = x.shape[0]
        loops = jnp.arange(N, dtype=edge_index.dtype)
        src = jnp.concatenate([edge_index[0], loops])
        dst = jnp.concatenate([edge_index[1], loops])
        deg = jax.ops.segment_sum(jnp.ones(src.shape, jnp.float32), dst, num_segments=N)
        dinv = jax.lax.rsqrt(deg)
        norm = dinv[src] * dinv[dst]
        for l in range(W.shape[0]):
            h = x @ W[l].T
            agg = jax.ops.segment_sum(h[src] * norm[:, None], dst, num_segments=N) + b[l]
            mean = jnp.mean(agg, axis=0)
            var = jnp.mean((agg - mean) ** 2, axis=0)
            xn = (agg - mean) * jax.lax.rsqrt(var + BN_EPS)
            x = jax.nn.relu(gamma[l] * xn + beta[l])
        return x

    def _L2_ffn_ref(x, Wr, br, W1, b1, W2, b2):
        import jax, jax.numpy as jnp
        import numpy as np
        B, S, H, E, F = (4, 256, 512, 8, 512)
        b, s, h = x.shape
        xt = x.reshape(-1, h)
        logits = xt @ Wr + br
        probs = jax.nn.softmax(logits, axis=-1)
        G = jnp.max(probs, axis=-1)
        idx = jnp.argmax(probs, axis=-1)
        h1 = jax.nn.relu(jnp.einsum('nh,ehf->nef', xt, W1) + b1)
        eo = jnp.einsum('nef,efh->neh', h1, W2) + b2
        Eout = jnp.take_along_axis(eo, idx[:, None, None], axis=1)[:, 0, :]
        y = G[:, None] * Eout
        return y.reshape(b, s, h)

    def _L3_gnn_ref(X, edge_index, W, b):
        import jax, jax.numpy as jnp
        import numpy as np
        N_NODES = 2500
        N_EDGES = 80000
        D_IN = 512
        D_OUT = 512
        n = X.shape[0]
        H = X @ W + b
        src, dst = (edge_index[0], edge_index[1])
        loops = jnp.arange(n, dtype=src.dtype)
        src_f = jnp.concatenate([src, loops])
        dst_f = jnp.concatenate([dst, loops])
        deg = jax.ops.segment_sum(jnp.ones_like(dst_f, dtype=H.dtype), dst_f, num_segments=n)
        inv_sqrt_deg = jax.lax.rsqrt(jnp.maximum(deg, 1.0))
        coef = inv_sqrt_deg[src_f] * inv_sqrt_deg[dst_f]
        msgs = H[src_f] * coef[:, None]
        out = jax.ops.segment_sum(msgs, dst_f, num_segments=n)
        return jax.nn.relu(out)

    def _L3_ffn_ref(x, ln1_g, ln1_b, ln2_g, ln2_b, wq, bq, wk, bk, wv, bv, wo, bo, router_w, router_b, w1, b1, w2, b2):
        import jax, jax.numpy as jnp
        import numpy as np
        D_MODEL = 512
        D_FF = 256
        N_HEADS = 8
        N_EXPERTS = 8
        TOP_K = 2
        CAPACITY_FACTOR = 1.6
        BATCH = 512
        SEQ = 16
        LN_EPS = 1e-05

        def _layernorm(x, g, b):
            mu = x.mean(-1, keepdims=True)
            var = ((x - mu) ** 2).mean(-1, keepdims=True)
            return (x - mu) * jax.lax.rsqrt(var + LN_EPS) * g + b

        def _moe(xf, router_w, router_b, w1, b1, w2, b2):
            T = xf.shape[0]
            probs = jax.nn.softmax(xf @ router_w + router_b, axis=-1)
            _, topk_idx = jax.lax.top_k(probs, TOP_K)
            capacity = int(np.ceil(T * CAPACITY_FACTOR / N_EXPERTS))
            out = jnp.zeros_like(xf)
            tok = jnp.arange(T)
            for i in range(N_EXPERTS):
                mask = (topk_idx == i).any(-1)
                pos = jnp.where(mask, tok, T)
                sel = jnp.sort(pos)[:capacity]
                xi = xf[jnp.minimum(sel, T - 1)]
                hi = jax.nn.gelu(xi @ w1[i] + b1[i], approximate=False)
                yi = hi @ w2[i] + b2[i]
                out = out.at[sel].set(yi, mode='drop')
            return out
        B, S, D = x.shape
        dk = D // N_HEADS
        h = _layernorm(x, ln1_g, ln1_b)
        q = (h @ wq + bq).reshape(B, S, N_HEADS, dk)
        k = (h @ wk + bk).reshape(B, S, N_HEADS, dk)
        v = (h @ wv + bv).reshape(B, S, N_HEADS, dk)
        scores = jnp.einsum('bqhd,bkhd->bhqk', q, k) / np.sqrt(dk).astype(np.float32)
        attn = jax.nn.softmax(scores, axis=-1)
        ctx = jnp.einsum('bhqk,bkhd->bqhd', attn, v).reshape(B, S, D)
        x = x + ctx @ wo + bo
        h2 = _layernorm(x, ln2_g, ln2_b)
        moe_out = _moe(h2.reshape(-1, D), router_w, router_b, w1, b1, w2, b2)
        return x + moe_out.reshape(B, S, D)
    edge_index = jnp.stack([src, dst])
    x = x + _L0_gnn_ref(_layernorm(x, axis=-1), edge_index, L0_gnn_Wl0, L0_gnn_bl0, L0_gnn_Wr0, L0_gnn_Wl1, L0_gnn_bl1, L0_gnn_Wr1)
    x = x + _L0_ffn_ref(_layernorm(x, axis=-1)[None], L0_ffn_ln1_g, L0_ffn_ln1_b, L0_ffn_wq, L0_ffn_wk, L0_ffn_wv, L0_ffn_wo, L0_ffn_ln2_g, L0_ffn_ln2_b, L0_ffn_wr, L0_ffn_w1, L0_ffn_b1, L0_ffn_w2, L0_ffn_b2)[0]
    x = x + _L1_gnn_ref(_layernorm(x, axis=-1), L1_gnn_weight, L1_gnn_bias, edge_index, edge_weight)
    x = x + _L1_ffn_ref(_layernorm(x, axis=-1)[None], L1_ffn_gfc1_w, L1_ffn_gfc1_b, L1_ffn_gfc2_w, L1_ffn_gfc2_b, L1_ffn_W1, L1_ffn_b1, L1_ffn_W2, L1_ffn_b2, L1_ffn_ln_g, L1_ffn_ln_b, L1_ffn_tv_W1, L1_ffn_tv_b1, L1_ffn_tv_W2, L1_ffn_tv_b2, L1_ffn_tv_ln_g, L1_ffn_tv_ln_b)[0]
    x = x + _L2_gnn_ref(_layernorm(x, axis=-1), L2_gnn_W, L2_gnn_b, L2_gnn_gamma, L2_gnn_beta, edge_index)
    x = x + _L2_ffn_ref(_layernorm(x, axis=-1)[None], L2_ffn_Wr, L2_ffn_br, L2_ffn_W1, L2_ffn_b1, L2_ffn_W2, L2_ffn_b2)[0]
    x = x + _L3_gnn_ref(_layernorm(x, axis=-1), edge_index, L3_gnn_W, L3_gnn_b)
    x = x + _L3_ffn_ref(_layernorm(x, axis=-1)[None], L3_ffn_ln1_g, L3_ffn_ln1_b, L3_ffn_ln2_g, L3_ffn_ln2_b, L3_ffn_wq, L3_ffn_bq, L3_ffn_wk, L3_ffn_bk, L3_ffn_wv, L3_ffn_bv, L3_ffn_wo, L3_ffn_bo, L3_ffn_router_w, L3_ffn_router_b, L3_ffn_w1, L3_ffn_b1, L3_ffn_w2, L3_ffn_b2)[0]
    return x

_drawn_inputs = setup_inputs


def setup_inputs(seed=0):
    import zlib

    import numpy as np

    out = dict(_drawn_inputs(seed))
    spreads = {'L0_gnn_bl0': (0.0, 0.1),
     'L0_gnn_bl1': (0.0, 0.1),
     'L0_ffn_ln1_g': (1.0, 0.6),
     'L0_ffn_ln1_b': (0.0, 0.3),
     'L0_ffn_ln2_g': (1.0, 0.6),
     'L0_ffn_ln2_b': (0.0, 0.621),
     'L0_ffn_b1': (0.0, 0.8),
     'L0_ffn_b2': (0.0, 0.299),
     'L1_ffn_gfc1_b': (0.0, 0.8),
     'L1_ffn_gfc2_b': (0.20000000298023224, 0.6),
     'L1_ffn_b1': (0.0, 0.8),
     'L1_ffn_b2': (0.0, 2.0),
     'L1_ffn_ln_g': (1.0, 0.6),
     'L1_ffn_ln_b': (0.0, 0.624),
     'L2_gnn_b': (0.0, 2.0),
     'L2_gnn_gamma': (1.0, 0.2),
     'L2_gnn_beta': (0.0, 0.447),
     'L2_ffn_br': (0.0, 0.749),
     'L2_ffn_b1': (0.0, 0.8),
     'L2_ffn_b2': (0.0, 0.8),
     'L3_ffn_ln1_g': (1.0, 0.6),
     'L3_ffn_ln1_b': (0.0, 0.8),
     'L3_ffn_ln2_g': (1.0, 0.6),
     'L3_ffn_ln2_b': (0.0, 0.8),
     'L3_ffn_bq': (0.0, 0.8),
     'L3_ffn_bk': (0.0, 2.0),
     'L3_ffn_bv': (0.0, 0.8),
     'L3_ffn_bo': (0.0, 0.562),
     'L3_ffn_router_b': (0.0, 0.65),
     'L3_ffn_b1': (0.0, 0.8),
     'L3_ffn_b2': (0.0, 0.717)}
    factors = {'L0_ffn_wq': 8.0,
     'L0_ffn_wk': 8.0,
     'L0_ffn_w1': 3.014,
     'L0_ffn_w2': 2.761,
     'L1_gnn_bias': 8.0,
     'L1_ffn_gfc1_w': 8.0,
     'L1_ffn_gfc2_w': 8.0,
     'L1_ffn_W1': 4.455,
     'L1_ffn_W2': 3.855,
     'L1_ffn_tv_W1': 6.107,
     'L1_ffn_tv_b1': 8.0,
     'L1_ffn_tv_W2': 5.364,
     'L1_ffn_tv_b2': 28.537,
     'L1_ffn_tv_ln_g': 8.0,
     'L1_ffn_tv_ln_b': 8.0,
     'L3_gnn_b': 8.0,
     'L3_ffn_wq': 8.0,
     'L3_ffn_wk': 8.0,
     'L3_ffn_router_w': 4.639,
     'L3_ffn_w1': 6.077,
     'L3_ffn_w2': 5.766}
    for name, (base, spread) in spreads.items():
        noise = np.random.default_rng([zlib.crc32(name.encode()), seed]).standard_normal(out[name].shape)
        drawn = base * np.exp(spread * noise) if base else spread * noise
        out[name] = jnp.asarray(drawn.astype(out[name].dtype))
    for name, factor in factors.items():
        out[name] = (out[name] * factor).astype(out[name].dtype)
    return out
```

```python
import concourse.bass as bass
from concourse import mybir
from contextlib import ExitStack, contextmanager
import numpy as np

N = 1250
D = 512
E = 40000
P = 125
T = N // P
C = D // 128
ET = E // P
ETP = ET + 2
WIN = 32
WPT = 4
NW = T * WPT
CH = [(0, 500), (500, 500), (1000, 250)]

fp32 = mybir.dt.float32
fp16 = mybir.dt.float16
bf16 = mybir.dt.bfloat16
i32 = mybir.dt.int32
u32 = mybir.dt.uint32
ALU = mybir.AluOpType
ACT = mybir.ActivationFunctionType
AX = mybir.AxisListType


class Steps:

    def __init__(self, eng, sem, base=0):
        self.eng, self.sem, self.base, self.n = eng, sem, base, 0

    def did(self, ins):
        ins.then_inc(self.sem, 1)
        self.n += 1
        return ins

    def wait(self):
        self.eng.wait_ge(self.sem, self.base + self.n)


def load_rows(eng, dst, src, sem):
    eng.dma_start(dst[0:120], src[0:120]).then_inc(sem, 16)
    eng.dma_start(dst[120:P], src[120:P]).then_inc(sem, 16)
def build_graph(nc, k, CT, WT, src_pt, dst_pt, w_pt, dst_rows, scr_minmax, scr_tab):
    with ExitStack() as ctx:
        def sb(name, shape, dt=fp32):
            return ctx.enter_context(nc.sbuf_tensor(name, shape, dt))

        def sem(name):
            return ctx.enter_context(k.semaphore(nc, name))

        ei = sb("edge_int", [P, 2, ET], i32)
        dF = sb("dst_f", [P, ETP])
        sF = sb("src_f", [P, ETP])
        wF = sb("w_f", [P, 3, ET])
        wp = sb("w_parts", [P, ETP, 4], bf16)
        dr = sb("dst_rows", [80, 4, P], i32)
        mm = sb("tile_minmax", [80, 2, 4])
        mb = sb("minmax_b", [NW, 2, ET])
        ov = sb("overlap", [NW, 3, ET])
        tl = sb("win_limits", [NW, 8])
        ti = sb("win_ints", [NW, 4], i32)
        tf = sb("win_tab", [NW, 4], i32)
        tab = sb("win_row", [1, NW * 4], i32)
        ioi = sb("iota_i", [P, N], i32)
        io16 = sb("iota16", [P, N + WIN], fp16)
        iot = sb("iota_t", [NW, ET])
        sel = sb("sel_parts", [128, 64])
        ohs = sb("onehot_src", [P, 3, N], bf16)
        ohd = sb("onehot_dst", [P, 3, 4, WIN], bf16)
        stage = sb("stage", [128, 2, N])
        ps = k.ps

        edges_in, consts_in, minmax_in, tab_in = (sem(n) for n in ("edges_in", "consts_in", "minmax_in", "tab_in"))
        steps, minmax_ready, iota_done = sem("table_steps"), sem("minmax_ready"), sem("iota_done")
        lens_ready, before_ready, table_ready = sem("lens_ready"), sem("before_ready"), sem("table_ready")

        with nc.Block() as block:
            @block.sync
            def _(sp):
                sp.dma_start(dr[:, :, :], dst_rows).then_inc(edges_in, 16)
                sp.dma_start(ei[:, 0, :], src_pt).then_inc(edges_in, 16)
                sp.dma_start(ei[:, 1, :], dst_pt).then_inc(edges_in, 16)
                sp.dma_start(wF[:, 0, :], w_pt).then_inc(edges_in, 16)
                sp.dma_start(sel[:, :], k.c_sel).then_inc(consts_in, 16)
                sp.dma_start(tl[:, 0:2], k.c_win).then_inc(consts_in, 16)
                sp.wait_ge(minmax_ready, 2)
                sp.dma_start(scr_minmax.rearrange("m (p q) -> p m q", q=4), mm[:, :, :]).then_inc(minmax_in, 16)
                sp.wait_ge(minmax_in, 16)
                sp.dma_start(mb[:, :, :], scr_minmax.partition_broadcast(NW)).then_inc(minmax_in, 16)
                sp.wait_ge(table_ready, 3)
                sp.dma_start(scr_tab, tf[:, :]).then_inc(tab_in, 16)
                sp.wait_ge(tab_in, 16)
                sp.dma_start(tab[:, :], scr_tab.rearrange("(o w) c -> o (w c)", o=1)).then_inc(tab_in, 16)
                sp.wait_ge(tab_in, 32)

            @block.gpsimd
            def _(pool):
                pool.iota(ioi[:, :], [[1, N]], base=0, channel_multiplier=0).then_inc(iota_done, 1)
                pool.iota(iot[:, :], [[1, ET]], base=0, channel_multiplier=0,
                          allow_small_or_imprecise_dtypes=True).then_inc(iota_done, 1)

            @block.tensor
            def _(pe):
                pe.wait_ge(lens_ready, 1)
                pe.matmul(ps[0:NW, 0, 0:1], k.tri[0:NW, 0:NW], tl[:, 6:7], start=True, stop=True)\
                    .then_inc(before_ready, 1)

            @block.vector
            def _(v):
                v.wait_ge(edges_in, 64)
                v.tensor_reduce(mm[:, 0, :], dr[:, :, :], AX.X, ALU.min).then_inc(minmax_ready, 1)
                v.tensor_reduce(mm[:, 1, :], dr[:, :, :], AX.X, ALU.max).then_inc(minmax_ready, 1)
                s = Steps(v, steps)
                s.did(v.memset(dF[:, ET:ETP], -1.0))
                s.did(v.memset(sF[:, ET:ETP], 0.0))
                s.did(v.memset(tf[:, 3:4], 0))
                s.did(v.memset(wp[:, :, :], 0.0))
                s.wait()
                s.did(v.memset(wp[:, 0:ET, 0:1], 1.0))
                s.did(v.tensor_copy(sF[:, 0:ET], ei[:, 0, :]))
                s.did(v.tensor_copy(dF[:, 0:ET], ei[:, 1, :]))
                s.did(v.tensor_copy(wp[:, 0:ET, 1], wF[:, 0, :]))
                s.wait()
                s.did(v.tensor_tensor(wF[:, 1, :], wF[:, 0, :], wp[:, 0:ET, 1], ALU.subtract))
                s.wait()
                s.did(v.tensor_copy(wp[:, 0:ET, 2], wF[:, 1, :]))
                s.wait()
                s.did(v.tensor_tensor(wF[:, 2, :], wF[:, 1, :], wp[:, 0:ET, 2], ALU.subtract))
                s.wait()
                s.did(v.tensor_copy(wp[:, 0:ET, 3], wF[:, 2, :]))
                v.wait_ge(iota_done, 2)
                s.did(v.memset(io16[:, N:], 2000.0))
                s.did(v.tensor_copy(io16[:, 0:N], ioi[:, :]))
                v.wait_ge(minmax_in, 32)
                v.wait_ge(consts_in, 32)
                s.did(v.tensor_scalar(ov[:, 0, :], mb[:, 0, :], tl[:, 1:2], None, ALU.is_le))
                s.wait()
                s.did(v.scalar_tensor_tensor(ov[:, 1, :], mb[:, 1, :], tl[:, 0:1], ov[:, 0, :],
                                             ALU.is_ge, ALU.mult))
                s.wait()
                s.did(v.scalar_tensor_tensor(ov[:, 2, :], ov[:, 1, :], -1000.0, iot[:, :], ALU.mult, ALU.add))
                s.did(v.scalar_tensor_tensor(ov[:, 0, :], iot[:, :], 1.0, ov[:, 1, :], ALU.add, ALU.mult))
                s.wait()
                s.did(v.tensor_reduce(tl[:, 2:3], ov[:, 2, :], AX.X, ALU.min))
                s.did(v.tensor_reduce(tl[:, 3:4], ov[:, 0, :], AX.X, ALU.max))
                s.wait()
                s.did(v.tensor_scalar(tl[:, 4:5], tl[:, 2:3], 1000.0, float(ET - 1), ALU.add, ALU.min))
                s.wait()
                s.did(v.tensor_tensor(tl[:, 5:6], tl[:, 3:4], tl[:, 4:5], ALU.subtract))
                s.wait()
                s.did(v.tensor_scalar(ti[:, 0:1], tl[:, 5:6], 1.0, None, ALU.max))
                s.wait()
                s.did(v.tensor_scalar(ti[:, 1:2], ti[:, 0:1], 1, None, ALU.arith_shift_right))
                s.wait()
                v.tensor_scalar(tf[:, 1:2], ti[:, 1:2], 1.0, None, ALU.max).then_inc(table_ready, 1)
                v.tensor_copy(tf[:, 0:1], tl[:, 4:5]).then_inc(table_ready, 1)
                v.wait_ge(table_ready, 2)
                v.tensor_scalar(tl[:, 6:7], tf[:, 1:2], 2.0, 1.0, ALU.mult, ALU.add).then_inc(lens_ready, 1)
                v.wait_ge(before_ready, 1)
                v.tensor_copy(tf[:, 2:3], ps[0:NW, 0, 0:1]).then_inc(table_ready, 1)

        onehots_ready, onehots_used = sem("onehots_ready"), sem("onehots_used")
        window_summed, window_staged = sem("window_summed"), sem("window_staged")
        parts_added, parts_out = sem("parts_added"), sem("parts_out")
        SPLIT = ((0, 5), (5, 5))

        def window(eng, w):
            return (eng.snap(eng.value_load(tab[0:1, bass.ds(w * 4, 1)], min_val=0, max_val=ET - 1)),
                    eng.snap(eng.value_load(tab[0:1, bass.ds(w * 4 + 1, 1)], min_val=1, max_val=ET // 2)),
                    eng.snap(eng.value_load(tab[0:1, bass.ds(w * 4 + 2, 1)], min_val=0, max_val=NW * (ET + 1))))

        with nc.Block() as block:
            @block.vector
            def _(v):
                def onehots(tile, nth, slot, base):
                    tile = nc.s_assert_within(tile, 0, ETP - 1, skip_runtime_bounds_check_because="a pair starts at tile ET at the latest")
                    v.wait_ge(onehots_used, nth + 1)
                    v.tensor_scalar(ohs[:, slot, :], io16[:, 0:N], sF[:, bass.ds(tile, 1)], None, ALU.is_equal)\
                        .then_inc(onehots_ready, 1)
                    v.scalar_tensor_tensor(
                        ohd[:, slot, :, :],
                        io16[:, bass.ds(base, WIN)].unsqueeze(1).broadcast_to([P, 4, WIN]),
                        dF[:, bass.ds(tile, 1)],
                        wp[:, bass.ds(tile, 1), :].rearrange("p o f -> p (o f)").unsqueeze(2).broadcast_to([P, 4, WIN]),
                        ALU.is_equal, ALU.mult).then_inc(onehots_ready, 1)

                with v.Fori(0, T) as i:
                    for j in range(WPT):
                        first, pairs, before = window(v, i * WPT + j)
                        base = i * P + j * WIN
                        onehots(first, before, 0, base)
                        with v.Fori(0, pairs) as q:
                            for h in range(2):
                                onehots(first + 2 * q + 1 + h, before + 2 * q + 1 + h, 1 + h, base)

            @block.tensor
            def _(pe):
                pe.sem_inc(onehots_used, 2)

                def add_tile(half, nth, slot, start):
                    pe.wait_ge(onehots_ready, (nth + 1) * 2)
                    for c, (c0, cn) in enumerate(CH):
                        mm_ = pe.matmul(ps[:, 3 * half + c, 0:cn], ohd[:, slot, :, :].rearrange("p a b -> p (a b)"),
                                        ohs[:, slot, c0:c0 + cn], start=start, stop=True, skip_group_check=True)
                    mm_.then_inc(onehots_used, 1)

                def add_parts(i, j):
                    w = i * WPT + j
                    pe.wait_ge(window_staged, w + 3)
                    pe.wait_ge(parts_out, w * 4 + 4)
                    for b, (s0, sn) in enumerate(SPLIT):
                        for s_ in range(sn):
                            t = s0 + s_
                            mm_ = pe.matmul(ps[0:P, 6 + b, 64 * s_:64 * s_ + 64],
                                            stage[:, j % 2, P * t:P * t + P], sel[:, :], start=True, stop=True,
                                            skip_group_check=True)
                    mm_.then_inc(parts_added, 1)

                with pe.Fori(0, T) as i:
                    for j in range(WPT):
                        w = i * WPT + j
                        first, pairs, before = window(pe, w)
                        pe.wait_ge(window_staged, w + 1)
                        add_tile(j % 2, before, 0, True)
                        with pe.Fori(0, pairs) as q:
                            for h in range(2):
                                add_tile(j % 2, before + 2 * q + 1 + h, 1 + h, False)
                        pe.drain().then_inc(window_summed, 1)
                        if j:
                            add_parts(i, j - 1)
                    add_parts(i, WPT - 1)

            @block.scalar
            def _(act):
                act.sem_inc(window_staged, 2)
                act.sem_inc(parts_out, 4)

                def stage_window(i, j):
                    act.wait_ge(window_summed, i * WPT + j + 1)
                    h = j % 2
                    act.activation(stage[:, h, 0:1000].rearrange("p (c n) -> p c n", c=2),
                                   ps[:, 3 * h:3 * h + 2, 0:500], ACT.Copy)
                    act.activation(stage[:, h, 1000:N], ps[:, 3 * h + 2, 0:250], ACT.Copy).then_inc(window_staged, 1)

                def parts_to_columns(i, j):
                    act.wait_ge(parts_added, i * WPT + j + 1)
                    n = min(WIN, P - j * WIN)
                    for b, (s0, sn) in enumerate(SPLIT):
                        for half, mat in enumerate((CT, WT)):
                            act.activation(mat[:, s0:s0 + sn, bass.ds(i * P + j * WIN, n)],
                                           ps[0:P, 6 + b, 0:64 * sn].rearrange("p (s n) -> p s n", n=64)
                                           [:, :, WIN * half:WIN * half + n], ACT.Copy).then_inc(parts_out, 1)

                with act.Fori(0, T) as i:
                    for j in range(WPT):
                        stage_window(i, j)
                        if j:
                            parts_to_columns(i, j - 1)
                    parts_to_columns(i, WPT - 1)
class Kit:

    def __init__(self):
        self.names = 0
        self.used_semaphores = []
        self.lasting = None

    def name(self, base):
        self.names += 1
        return f"{base}_{self.names}"


    def gpsimd_dma_semaphore(self, nc, name):
        return self.lasting.enter_context(nc.semaphore(self.name(name)))

    @contextmanager
    def semaphore(self, nc, name):
        with nc.semaphore(name) as s:
            yield s
        self.used_semaphores.append(s)

    def clear_semaphores(self, nc):
        todo, self.used_semaphores = self.used_semaphores, []
        with nc.Block() as block:
            @block.gpsimd
            def _(pool):
                for s in todo:
                    pool.sem_clear(s)
def norm_rows(nc, k, x, xn, xT=None, affine=None, eps=1e-5):
    with ExitStack() as ctx:
        def sb(name, shape, dt=fp32):
            return ctx.enter_context(nc.sbuf_tensor(k.name(name), shape, dt))

        def sem(name):
            return ctx.enter_context(k.semaphore(nc, k.name(name)))

        st = sb("bn_parts", [P, T, 6])
        mv = sb("mean_var", [P, T, 2])
        sd = sb("std", [P, T])
        rs = sb("rstd", [P, T])
        stats, var_ready, std_ready, inv_ready = sem("stats"), sem("var_ready"), sem("std_ready"), sem("inv_ready")
        rows_ready, transposed, copied = sem("rows_ready"), sem("transposed"), sem("copied")
        with nc.Block() as block:
            @block.vector
            def _(v):
                with v.Fori(0, T) as i:
                    v.bn_stats(st[:, bass.ds(i, 1), :].rearrange("p o n -> p (o n)"),
                               x[:, bass.ds(i, 1), :].rearrange("p o n -> p (o n)")).then_inc(stats, 1)
                v.wait_ge(stats, T)
                for i in range(T):
                    v.bn_aggr(mv[:, i, :], st[:, i, :]).then_inc(stats, 1)
                v.wait_ge(stats, 2 * T)
                v.tensor_scalar(sd[:, :], mv[:, :, 1], eps, None, ALU.add).then_inc(var_ready, 1)
                v.wait_ge(std_ready, 1)
                v.reciprocal(rs[:, :], sd[:, :]).then_inc(inv_ready, 1)
                v.wait_ge(inv_ready, 1)
                with v.Fori(0, T) as i:
                    v.tensor_scalar(xn[:, bass.ds(i, 1), :].rearrange("p o n -> p (o n)"),
                                    x[:, bass.ds(i, 1), :].rearrange("p o n -> p (o n)"),
                                    mv[:, bass.ds(i, 1), 0:1].rearrange("p o n -> p (o n)"), rs[:, bass.ds(i, 1)],
                                    ALU.subtract, ALU.mult).then_inc(rows_ready, 1)

            @block.scalar
            def _(act):
                act.wait_ge(var_ready, 1)
                act.activation(sd[:, :], sd[:, :], ACT.Sqrt).then_inc(std_ready, 1)
                if xT is not None:
                    copy_transposed(act, k, xT, transposed, copied, affine)

            if xT is not None:
                @block.tensor
                def _(pe):
                    transpose_rows(pe, k, xn, transposed, copied, rows_ready)


def transpose_rows(pe, k, xn, transposed, copied, rows_ready=None):
    g = 0
    for c0, cn in CH:
        if rows_ready is not None:
            pe.wait_ge(rows_ready, (c0 + cn) // P)
        for c in range(C):
            if g >= 8:
                pe.wait_ge(copied, g - 7)
            for t in range(c0 // P, (c0 + cn) // P):
                mm = pe.transpose(k.ps[:, g % 8, P * t - c0:P * t - c0 + P], xn[:, t, 128 * c:128 * c + 128],
                                  k.ident[0:P, 0:P])
            mm.then_inc(transposed, 1)
            g += 1


def copy_transposed(act, k, xT, transposed, copied, affine=None):
    g = 0
    for c0, cn in CH:
        for c in range(C):
            act.wait_ge(transposed, g + 1)
            if affine is None:
                act.activation(xT[:, c, c0:c0 + cn], k.ps[:, g % 8, 0:cn], ACT.Copy).then_inc(copied, 1)
            else:
                act.activation(xT[:, c, c0:c0 + cn], k.ps[:, g % 8, 0:cn], ACT.Identity,
                               bias=affine[1][:, c:c + 1], scale=affine[0][:, c:c + 1]).then_inc(copied, 1)
            g += 1


def transpose_only(nc, k, xn, xT):
    with k.semaphore(nc, k.name("transposed")) as transposed, k.semaphore(nc, k.name("copied")) as copied:
        with nc.Block() as block:
            @block.tensor
            def _(pe):
                transpose_rows(pe, k, xn, transposed, copied)

            @block.scalar
            def _(act):
                copy_transposed(act, k, xT, transposed, copied)


def load(nc, k, pairs):
    with k.semaphore(nc, k.name("loaded")) as loaded:
        with nc.Block() as block:
            @block.sync
            def _(sp):
                for dst, src in pairs:
                    sp.dma_start(dst, src).then_inc(loaded, 16)
                sp.wait_ge(loaded, 16 * len(pairs))


def rows_product(nc, k, terms, bias, finish):
    (engine, take), = finish.items()
    with k.semaphore(nc, k.name("summed")) as summed, k.semaphore(nc, k.name("taken")) as taken:
        with nc.Block() as block:
            @block.tensor
            def _(pe):
                for i in range(T):
                    if i >= 8:
                        pe.wait_ge(taken, i - 7)
                    todo = [(lhsT[:, c, P * i:P * i + P], rhs[:, c, :]) for lhsT, rhs, n in terms for c in range(n)]
                    if bias is not None:
                        todo.append((k.ones[0:1, 0:P], bias))
                    for n, (l, r) in enumerate(todo):
                        mm = pe.matmul(k.ps[0:P, i % 8, :], l, r, start=(n == 0), stop=(n == len(todo) - 1))
                    mm.then_inc(summed, 1)

            def takes(eng):
                for i in range(T):
                    eng.wait_ge(summed, i + 1)
                    take(eng, i, k.ps[0:P, i % 8, :]).then_inc(taken, 1)

            if engine == "scalar":
                block.scalar(takes)
            else:
                block.vector(takes)


def columns_product(nc, k, lhsT, rhs, chunks, mchunks, take, reuse=None):
    with k.semaphore(nc, k.name("summed")) as summed, k.semaphore(nc, k.name("taken")) as taken:
        with nc.Block() as block:
            @block.tensor
            def _(pe):
                g = 0
                for m in range(mchunks):
                    for c0, cn in CH:
                        if g >= 8:
                            pe.wait_ge(taken, g - 7)
                        for c in range(chunks):
                            mm = pe.matmul(k.ps[:, g % 8, 0:cn], lhsT[:, c, 128 * m:128 * m + 128],
                                           rhs[:, c, c0:c0 + cn], start=(c == 0), stop=(c == chunks - 1))
                        mm.then_inc(summed, 1)
                        g += 1

            @block.scalar
            def _(act):
                g = 0
                for m in range(mchunks):
                    for n, (c0, cn) in enumerate(CH):
                        if reuse is not None and g >= reuse:
                            act.wait_ge(taken, g - reuse + 1)
                        act.wait_ge(summed, g + 1)
                        take(act, m, (c0, cn), n, k.ps[:, g % 8, 0:cn]).then_inc(taken, 1)
                        g += 1


def copy_rows(out, func=None):
    return {"scalar": lambda act, i, psum: act.activation(out[:, i, :], psum, func or ACT.Copy)}


def add_rows(out, base=None):
    return {"vector": lambda v, i, psum: v.tensor_tensor(out[:, i, :], (out if base is None else base)[:, i, :],
                                                         psum, ALU.add)}


def add_into(nc, k, x, y):
    with k.semaphore(nc, k.name("added")) as added:
        with nc.Block() as block:
            @block.vector
            def _(v):
                v.tensor_tensor(x[:, :, :], x[:, :, :], y[:, :, :], ALU.add).then_inc(added, 1)


def attention(nc, k, x1T, w_qk, w_v, b_qk, b_v, ctxT):
    H, DH = 8, 64
    SCALE = DH ** -0.5
    RING = (0, 1, 2, 6, 7)
    with ExitStack() as ctx:
        def sb(name, shape, dt=fp32):
            return ctx.enter_context(nc.sbuf_tensor(k.name(name), shape, dt))

        def sem(name):
            return ctx.enter_context(k.semaphore(nc, k.name(name)))

        wqk = sb("wqk", [128, 2, C, 128])
        wv = sb("wv", [128, 2, C, DH])
        bqk = sb("bqk", [1, 2, 128])
        bv = sb("bv", [1, D])
        QT = sb("QT", [DH + 1, N])
        KT = sb("KT", [DH + 1, N])
        V = sb("V", [P, T, DH + 1])
        PT = sb("PT", [P, 2, N])
        cu = sb("ctx_sum", [DH + 1, N])
        mx = sb("mx", [P, T, 2])
        mr = sb("mr", [P, T])
        negm = sb("negm", [P, T])
        rc = sb("rc", [P, T])
        w_in, b_in = [sem("w_in0"), sem("w_in1")], sem("bv_in")
        w_used, ones_set = sem("w_used"), sem("ones_set")
        q_out, k_out, v_out = sem("q_out"), sem("k_out"), sem("v_out")
        max_out, max_steps, negm_ready, row_out = sem("max_out"), sem("max_steps"), sem("negm_ready"), sem("row_out")
        exp_out, ctx_out, recip_ready, norm_out = sem("exp_out"), sem("ctx_out"), sem("recip_ready"), sem("norm_out")
        proj_done, v_done, s_done, row_done = sem("proj_done"), sem("v_done"), sem("s_done"), sem("row_done")
        st_done, pt_used, acc_done = sem("st_done"), sem("pt_used"), sem("acc_done")
        sumcol_done, bc_done = sem("sumcol_done"), sem("bc_done")
        loads = 3 if b_qk is not None else 2
        ps = k.ps

        with nc.Block() as block:
            @block.sync
            def _(sp):
                if b_v is not None:
                    sp.dma_start(bv[:, :], b_v).then_inc(b_in, 16)
                with sp.Fori(0, H // 2) as i:
                    for j in range(2):
                        h = i * 2 + j
                        sp.wait_ge(w_used, h + 1)
                        sp.dma_start(wqk[:, j, :, :], w_qk[bass.ds(h, 1)].rearrange("o p c n -> p (o c) n"))\
                            .then_inc(w_in[j], 16)
                        sp.dma_start(wv[:, j, :, :], w_v[bass.ds(h, 1)].rearrange("o p c n -> p (o c) n"))\
                            .then_inc(w_in[j], 16)
                        if b_qk is not None:
                            sp.dma_start(bqk[:, j, :], b_qk[bass.ds(h, 1), :]).then_inc(w_in[j], 16)

            @block.tensor
            def _(pe):
                pe.sem_inc(w_used, 2)
                pe.sem_inc(pt_used, 2)
                pe.wait_ge(ones_set, 2)
                if b_v is not None:
                    pe.wait_ge(b_in, 16)
                with pe.Fori(0, H // 2) as i:
                    for j in range(2):
                        h = i * 2 + j
                        pe.wait_ge(w_in[j], (i + 1) * (16 * loads))
                        pe.wait_ge(norm_out, h * 3 + 1)
                        for n, (c0, cn) in enumerate(CH):
                            for c in range(C):
                                mm = pe.matmul(ps[:, n, 0:cn], wqk[:, j, c, :], x1T[:, c, c0:c0 + cn],
                                               start=(c == 0), stop=(c == C - 1 and b_qk is None))
                            if b_qk is not None:
                                mm = pe.matmul(ps[:, n, 0:cn], bqk[:, j, :], k.ones_row[0:1, 0:cn],
                                               start=False, stop=True)
                            mm.then_inc(proj_done, 1)
                        for half in range(2):
                            for t in range(5 * half, 5 * half + 5):
                                o = ps[0:P, 3 + half, DH * (t % 5):DH * (t % 5) + DH]
                                for c in range(C):
                                    mm = pe.matmul(o, x1T[:, c, P * t:P * t + P], wv[:, j, c, :], start=(c == 0),
                                                   stop=(c == C - 1 and b_v is None))
                                if b_v is not None:
                                    mm = pe.matmul(o, k.ones[0:1, 0:P], bv[0:1, bass.ds(h * DH, DH)],
                                                   start=False, stop=True)
                            mm.then_inc(v_done, 1)
                        pe.drain().then_inc(w_used, 1)
                        pe.wait_ge(q_out, h * 3 + 3)
                        pe.wait_ge(k_out, h * 3 + 3)
                        for t in range(T):
                            if t >= 2:
                                pe.wait_ge(max_out, h * T + (t - 1))
                            b0 = 5 if t % 2 == 0 else 0
                            for n, (c0, cn) in enumerate(CH):
                                mm = pe.matmul(ps[0:P, b0 + n, 0:cn], QT[0:DH, P * t:P * t + P],
                                               KT[0:DH, c0:c0 + cn], start=True, stop=True)
                            mm.then_inc(s_done, 1)
                        pe.wait_ge(negm_ready, h + 1)
                        pe.wait_ge(v_out, h * 2 + 2)
                        for n, (c0, cn) in enumerate(CH):
                            for t in range(c0 // P, (c0 + cn) // P):
                                mm = pe.matmul(ps[DH:DH + 1, 3 + n, P * t - c0:P * t - c0 + P], negm[:, t:t + 1],
                                               k.ident[0:P, 0:P], start=True, stop=True)
                            mm.then_inc(row_done, 1)
                        pe.wait_ge(row_out, h * 3 + 3)

                        def scores_t(t):
                            for n, (c0, cn) in enumerate(CH):
                                cc = 3 * t + n
                                if cc >= 5:
                                    pe.wait_ge(exp_out, h * 30 + (cc - 4))
                                pe.matmul(ps[0:P, RING[cc % 5], 0:cn], KT[:, P * t:P * t + P], QT[:, c0:c0 + cn],
                                          start=True, stop=True).then_inc(st_done, 1)

                        def times_v(t):
                            pe.wait_ge(exp_out, h * 30 + (3 * t + 3))
                            for n, (c0, cn) in enumerate(CH):
                                mm = pe.matmul(ps[0:DH + 1, 3 + n, 0:cn], V[:, t, :], PT[:, t % 2, c0:c0 + cn],
                                               start=(t == 0), stop=(t == T - 1))
                            mm.then_inc(pt_used, 1)

                        scores_t(0)
                        for t in range(1, T):
                            scores_t(t)
                            times_v(t - 1)
                        times_v(T - 1)
                        pe.drain().then_inc(acc_done, 1)
                        pe.wait_ge(ctx_out, h * 3 + 3)
                        for t in range(T):
                            mm = pe.matmul(ps[0:P, 6, t:t + 1], cu[DH:DH + 1, P * t:P * t + P],
                                           k.ones[DH:DH + 1, 0:1], start=True, stop=True, skip_group_check=True)
                        mm.then_inc(sumcol_done, 1)
                        pe.wait_ge(recip_ready, h + 1)
                        for n, (c0, cn) in enumerate(CH):
                            for t in range(c0 // P, (c0 + cn) // P):
                                mm = pe.matmul(ps[0:DH, n, P * t - c0:P * t - c0 + P],
                                               rc[:, t:t + 1].broadcast_to([P, DH]), k.ident[0:P, 0:P],
                                               start=True, stop=True)
                            mm.then_inc(bc_done, 1)

            @block.scalar
            def _(act):
                with act.Fori(0, H // 2) as i:
                    for j in range(2):
                        h = i * 2 + j
                        for n, (c0, cn) in enumerate(CH):
                            act.wait_ge(proj_done, h * 3 + (n + 1))
                            act.activation(QT[0:DH, c0:c0 + cn], ps[0:DH, n, 0:cn], ACT.Copy).then_inc(q_out, 1)
                        for half in range(2):
                            act.wait_ge(v_done, h * 2 + (half + 1))
                            act.activation(V[:, 5 * half:5 * half + 5, 0:DH],
                                           ps[0:P, 3 + half, 0:5 * DH].rearrange("p (t n) -> p t n", t=5),
                                           ACT.Copy).then_inc(v_out, 1)
                        for n, (c0, cn) in enumerate(CH):
                            act.wait_ge(row_done, h * 3 + (n + 1))
                            act.activation(QT[DH:DH + 1, c0:c0 + cn], ps[DH:DH + 1, 3 + n, 0:cn], ACT.Copy)\
                                .then_inc(row_out, 1)
                        for t in range(T):
                            act.wait_ge(pt_used, h * T + (t + 1))
                            for n, (c0, cn) in enumerate(CH):
                                cc = 3 * t + n
                                act.wait_ge(st_done, h * 30 + (cc + 1))
                                act.activation(PT[:, t % 2, c0:c0 + cn], ps[0:P, RING[cc % 5], 0:cn], ACT.Exp,
                                               scale=SCALE).then_inc(exp_out, 1)
                        act.wait_ge(acc_done, h + 1)
                        for n, (c0, cn) in enumerate(CH):
                            act.activation(cu[:, c0:c0 + cn], ps[0:DH + 1, 3 + n, 0:cn], ACT.Copy)\
                                .then_inc(ctx_out, 1)

            @block.vector
            def _(v):
                v.sem_inc(norm_out, 1)
                v.memset(KT[DH:DH + 1, :], 1.0).then_inc(ones_set, 1)
                v.memset(V[:, :, DH:DH + 1], 1.0).then_inc(ones_set, 1)
                with v.Fori(0, H // 2) as i:
                    for j in range(2):
                        h = i * 2 + j
                        for n, (c0, cn) in enumerate(CH):
                            v.wait_ge(proj_done, h * 3 + (n + 1))
                            v.tensor_copy(KT[0:DH, c0:c0 + cn], ps[DH:128, n, 0:cn]).then_inc(k_out, 1)
                        for t in range(T):
                            b0 = 5 if t % 2 == 0 else 0
                            v.wait_ge(s_done, h * T + (t + 1))
                            v.tensor_reduce(mx[:, t, 0:1], ps[0:P, b0:b0 + 2, 0:500], AX.XY, ALU.max)
                            v.tensor_reduce(mx[:, t, 1:2], ps[0:P, b0 + 2, 0:250], AX.X, ALU.max)\
                                .then_inc(max_out, 1)
                        v.wait_ge(max_out, h * T + T)
                        v.tensor_reduce(mr[:, :], mx[:, :, :], AX.X, ALU.max).then_inc(max_steps, 1)
                        v.wait_ge(max_steps, h + 1)
                        v.tensor_scalar(negm[:, :], mr[:, :], -1.0, None, ALU.mult).then_inc(negm_ready, 1)
                        v.wait_ge(sumcol_done, h + 1)
                        v.reciprocal(rc[:, :], ps[0:P, 6, 0:T]).then_inc(recip_ready, 1)
                        for n, (c0, cn) in enumerate(CH):
                            v.wait_ge(bc_done, h * 3 + (n + 1))
                            v.tensor_tensor(ctxT[DH * j:DH * j + DH, bass.ds(i, 1), c0:c0 + cn]
                                            .rearrange("p o n -> p (o n)"), cu[0:DH, c0:c0 + cn], ps[0:DH, n, 0:cn],
                                            ALU.mult).then_inc(norm_out, 1)
def route(nc, k, yT, wr, br, E_, topk, cap, keep_last, r):
    with ExitStack() as ctx:
        def sb(name, shape, dt=fp32):
            return ctx.enter_context(nc.sbuf_tensor(k.name(name), shape, dt))

        def sem(name):
            return ctx.enter_context(k.semaphore(nc, k.name(name)))

        L = sb("logits", [P, T, E_])
        W = sb("work", [P, T, E_])
        PR = sb("probs", [P, T, E_])
        OH = sb("onehot", [P, 2, T, E_])
        M16 = sb("mask16", [P, T, E_], bf16)
        POS = sb("pos", [P, T, E_])
        G = sb("gates_by_expert", [P, T, E_])
        m1 = sb("m1", [P, T])
        top = sb("top", [P, T, 8])
        idx = sb("idx", [P, T, 8], u32)
        ix = sb("ix", [P, 2, T])
        pk = sb("pk", [P, 2, T])
        keep = sb("keep", [P, 2, T])
        tmp = sb("tmp", [P, 4, T])
        spare = sb("spare", [P, 2, T])
        ioE = sb("iota_e", [P, E_])
        cnt = sb("cnt", [P, E_])
        cnti = sb("cnt_i", [P, 2, E_], i32)
        blk = sb("blk", [P, 3, E_])
        ps = k.ps
        iotas, logit_done, logit_out = sem("iotas"), sem("logit_done"), sem("logit_out")
        steps, shifted, exps, masks = sem("route_steps"), sem("shifted"), sem("exps"), sem("masks")
        pos_done, gates_ready, gT_done, gT_out = sem("pos_done"), sem("gates_ready"), sem("gT_done"), sem("gT_out")
        PB = T // 2

        def two(bank):
            return [(ps[0:P, bank + b, 0:PB * E_].rearrange("p (t e) -> p t e", e=E_), slice(PB * b, PB * b + PB))
                    for b in range(2)]

        def over_e(ap):
            return ap.unsqueeze(2).broadcast_to([P, T, E_])

        with nc.Block() as block:
            @block.gpsimd
            def _(pool):
                pool.iota(ioE[:, :], [[1, E_]], base=0, channel_multiplier=0,
                          allow_small_or_imprecise_dtypes=True).then_inc(iotas, 1)
                for c in range(topk):
                    pool.iota(spare[:, c, :], [[topk * P, T]], base=c + r.spare0, channel_multiplier=topk,
                              allow_small_or_imprecise_dtypes=True).then_inc(iotas, 1)

            @block.tensor
            def _(pe):
                for t in range(T):
                    o = ps[0:P, t // PB, E_ * (t % PB):E_ * (t % PB) + E_]
                    for c in range(C):
                        mm = pe.matmul(o, yT[:, c, P * t:P * t + P], wr[:, c, :], start=(c == 0),
                                       stop=(c == C - 1 and br is None))
                    if br is not None:
                        mm = pe.matmul(o, k.ones[0:1, 0:P], br, start=False, stop=True)
                mm.then_inc(logit_done, 1)
                pe.wait_ge(masks, 1)
                for t in range(T):
                    o = ps[0:P, 2 + t // PB, E_ * (t % PB):E_ * (t % PB) + E_]
                    for u in range(t):
                        pe.matmul(o, k.ones16[0:P, 0:P], M16[:, u, :], start=(u == 0), stop=False)
                    mm = pe.matmul(o, k.tri16[0:P, 0:P], M16[:, t, :], start=(t == 0), stop=True)
                if cap is None:
                    for u in range(T):
                        mm = pe.matmul(ps[0:P, 4, 0:E_], k.ones16[0:P, 0:P], M16[:, u, :], start=(u == 0),
                                       stop=(u == T - 1))
                mm.then_inc(pos_done, 1)
                pe.wait_ge(gates_ready, 1)
                for n, (c0, cn) in enumerate(CH):
                    for t in range(c0 // P, (c0 + cn) // P):
                        mm = pe.transpose(ps[0:E_, 5 + n, P * t - c0:P * t - c0 + P], G[:, t, :], k.ident[0:P, 0:P])
                mm.then_inc(gT_done, 1)

            @block.scalar
            def _(act):
                act.wait_ge(shifted, 1)
                act.activation(W[:, :, :], L[:, :, :], ACT.Exp).then_inc(exps, 1)
                act.wait_ge(gT_done, 1)
                for n, (c0, cn) in enumerate(CH):
                    act.activation(r.gateT[:, c0:c0 + cn], ps[0:E_, 5 + n, 0:cn], ACT.Copy).then_inc(gT_out, 1)

            @block.vector
            def _(v):
                s = Steps(v, steps)
                v.wait_ge(iotas, 1 + topk)
                v.wait_ge(logit_done, 1)
                for part, tt in two(0):
                    s.did(v.tensor_copy(POS[:, tt, :], part))
                s.wait()
                s.did(v.tensor_reduce(m1[:, :], POS[:, :, :], AX.X, ALU.max))
                s.wait()
                v.tensor_tensor(L[:, :, :], POS[:, :, :], over_e(m1[:, :]), ALU.subtract).then_inc(shifted, 1)
                v.wait_ge(exps, 1)
                s.did(v.tensor_reduce(m1[:, :], W[:, :, :], AX.X, ALU.add))
                s.wait()
                s.did(v.reciprocal(tmp[:, 0, :], m1[:, :]))
                s.wait()
                s.did(v.tensor_tensor(PR[:, :, :], W[:, :, :], over_e(tmp[:, 0, :]), ALU.mult))
                s.wait()
                for t in range(T):
                    s.did(v.max(top[:, t, :], PR[:, t, :]))
                s.wait()
                for t in range(T):
                    s.did(v.max_index(idx[:, t, :], top[:, t, :], PR[:, t, :]))
                s.wait()
                for c in range(topk):
                    s.did(v.tensor_copy(ix[:, c, :], idx[:, :, c]))
                s.wait()
                for c in range(topk):
                    s.did(v.tensor_tensor(OH[:, c, :, :], ioE[:, :].unsqueeze(1).broadcast_to([P, T, E_]),
                                          over_e(ix[:, c, :]), ALU.is_equal))
                s.wait()
                if topk == 2:
                    v.tensor_tensor(M16[:, :, :], OH[:, 0, :, :], OH[:, 1, :, :], ALU.add).then_inc(masks, 1)
                else:
                    v.tensor_copy(M16[:, :, :], OH[:, 0, :, :]).then_inc(masks, 1)
                v.wait_ge(pos_done, 1)
                for part, tt in two(2):
                    s.did(v.tensor_copy(POS[:, tt, :], part))
                s.wait()
                if cap is None:
                    s.did(v.tensor_copy(cnt[:, :], ps[0:P, 4, 0:E_]))
                    s.wait()
                    s.did(v.memset(blk[:, 0, :], 1.0))
                    s.wait()
                    for b in range(1, N // (2 * P)):
                        s.did(v.scalar_tensor_tensor(blk[:, 0, :], cnt[:, :], float(2 * P * b), blk[:, 0, :],
                                                     ALU.is_gt, ALU.add))
                        s.wait()
                    s.did(v.memset(blk[:, 1, :], 0.0))
                    s.did(v.memset(blk[:, 2, 0:1], 0.0))
                    s.wait()
                    for e in range(1, E_):
                        s.did(v.tensor_tensor(blk[:, 2, e:e + 1], blk[:, 2, e - 1:e], blk[:, 0, e - 1:e], ALU.add))
                        s.wait()
                    s.did(v.tensor_copy(r.tab[:, 0, :], blk[0:1, 0, :]))
                    s.did(v.tensor_copy(r.tab[:, 1, :], blk[0:1, 2, :]))
                    s.did(v.tensor_scalar(blk[:, 1, :], blk[:, 2, :], float(2 * P), None, ALU.mult))
                    s.wait()
                    s.did(v.tensor_tensor(POS[:, :, :], POS[:, :, :],
                                          blk[:, 1, :].unsqueeze(1).broadcast_to([P, T, E_]), ALU.add))
                    s.wait()
                for c in range(topk):
                    s.did(v.tensor_tensor(W[:, :, :], OH[:, c, :, :], POS[:, :, :], ALU.mult))
                    s.wait()
                    s.did(v.tensor_reduce(pk[:, c, :], W[:, :, :], AX.X, ALU.add))
                    s.wait()
                if cap is None:
                    s.did(v.tensor_copy(r.put[:, 0, :], pk[:, 0, :]))
                    s.did(v.tensor_copy(r.get[:, 0, :], pk[:, 0, :]))
                    s.did(v.tensor_copy(r.gate[:, 0, :], top[:, :, 0]))
                    s.wait()
                else:
                    for c in range(2):
                        s.did(v.tensor_scalar(keep[:, c, :], pk[:, c, :], float(cap), None, ALU.is_lt))
                        s.did(v.tensor_scalar(tmp[:, c, :], pk[:, c, :], float(cap - 1), None, ALU.min))
                    s.wait()
                    for c in range(2):
                        s.did(v.scalar_tensor_tensor(tmp[:, 2 + c, :], ix[:, c, :], float(cap), tmp[:, c, :],
                                                     ALU.mult, ALU.add))
                    s.wait()
                    for c in range(2):
                        s.did(v.tensor_copy(r.get[:, c, :], tmp[:, 2 + c, :]))
                        s.did(v.tensor_tensor(tmp[:, c, :], tmp[:, 2 + c, :], spare[:, c, :], ALU.subtract))
                    s.wait()
                    for c in range(2):
                        s.did(v.tensor_tensor(tmp[:, c, :], tmp[:, c, :], keep[:, c, :], ALU.mult))
                    s.wait()
                    for c in range(2):
                        s.did(v.tensor_tensor(r.put[:, c, :], tmp[:, c, :], spare[:, c, :], ALU.add))
                    s.wait()
                    if keep_last:
                        s.did(v.tensor_tensor(tmp[:, 0, :], ix[:, 1, :], ix[:, 0, :], ALU.is_gt))
                        s.did(v.tensor_tensor(tmp[:, 1, :], ix[:, 0, :], ix[:, 1, :], ALU.is_gt))
                        s.wait()
                        for c in range(2):
                            s.did(v.tensor_tensor(tmp[:, c, :], tmp[:, c, :], keep[:, 1 - c, :], ALU.mult))
                        s.wait()
                        for c in range(2):
                            s.did(v.tensor_scalar(tmp[:, c, :], tmp[:, c, :], -1.0, 1.0, ALU.mult, ALU.add))
                        s.wait()
                    else:
                        s.did(v.tensor_tensor(m1[:, :], top[:, :, 0], top[:, :, 1], ALU.add))
                        s.wait()
                        s.did(v.reciprocal(tmp[:, 2, :], m1[:, :]))
                        s.wait()
                        for c in range(2):
                            s.did(v.tensor_tensor(tmp[:, c, :], tmp[:, 2, :], top[:, :, c], ALU.mult))
                        s.wait()
                    for c in range(2):
                        s.did(v.tensor_tensor(r.gate[:, c, :], tmp[:, c, :], keep[:, c, :], ALU.mult))
                    s.wait()
                if topk == 2:
                    s.did(v.tensor_tensor(W[:, :, :], OH[:, 0, :, :], over_e(r.gate[:, 0, :]), ALU.mult))
                    s.did(v.tensor_tensor(PR[:, :, :], OH[:, 1, :, :], over_e(r.gate[:, 1, :]), ALU.mult))
                    s.wait()
                    v.tensor_tensor(G[:, :, :], W[:, :, :], PR[:, :, :], ALU.add).then_inc(gates_ready, 1)
                else:
                    v.tensor_tensor(G[:, :, :], OH[:, 0, :, :], over_e(r.gate[:, 0, :]), ALU.mult)\
                        .then_inc(gates_ready, 1)


def experts(nc, k, r, rows_in, E_, F, R, tiles, func, w1, b1, w2, affine, buf, ybuf, dynamic):
    FC = F // 128
    EPG = 2 if tiles == 1 else 1
    with ExitStack() as ctx:
        def sb(name, shape, dt=fp32):
            return ctx.enter_context(nc.sbuf_tensor(k.name(name), shape, dt))

        def sem(name):
            return ctx.enter_context(k.semaphore(nc, k.name(name)))

        w1s = sb("w1s", [128, 2 * EPG, C, F])
        w2s = sb("w2s", [128, 2 * EPG, FC, D])
        b1s = sb("b1s", [128, 2 * EPG, FC])
        xb = sb("xb", [R, 2, D])
        xbT = sb("xbT", [128, 2, C, R])
        hT = sb("hT", [128, 2, FC, R])
        yb = sb("yb", [R, 2, D])
        put_done = k.gpsimd_dma_semaphore(nc, "put_done")
        stored = [k.gpsimd_dma_semaphore(nc, "stored") for _ in range(2)]
        w_in, w_used = [sem("w_in0"), sem("w_in1")], [sem("w_used0"), sem("w_used1")]
        rows_loaded, turned = [sem("rows0"), sem("rows1")], [sem("turned0"), sem("turned1")]
        xT_out, h_done, h_out = [[sem(n + "0"), sem(n + "1")] for n in ("xT_out", "h_done", "h_out")]
        yb_free = [sem("yb_free0"), sem("yb_free1")]
        y_done, y_out = [[sem(n + "0"), sem(n + "1")] for n in ("y_done", "y_out")]
        ps = k.ps

        with nc.Block() as block:
            @block.gpsimd
            def _(pool):
                n = 0
                for c in range(r.topk):
                    for t in range(T):
                        pool.indirect_dma_start(buf, bass.IndirectOffsetOnAxis(ap=r.put[:, c, t:t + 1], axis=0),
                                                rows_in[:, t, :], None).then_inc(put_done, 16)
                        n += 16
                pool.wait_ge(put_done, n)

        def run(eng, body, before=None, after=None):
            with eng.Fori(0, E_ // (2 * EPG)) as i:
                for g in range(2):
                    if before is not None:
                        before(i, g)
                    e = i * 2 + g
                    if dynamic:
                        n = eng.snap(eng.value_load(r.tab[0:1, 0, bass.ds(e, 1)], min_val=1, max_val=N // (2 * P)))
                        first = eng.snap(eng.value_load(r.tab[0:1, 1, bass.ds(e, 1)], min_val=0,
                                                        max_val=r.max_blocks))
                        with eng.Fori(0, n) as q:
                            body(i, first + q, g)
                    else:
                        body(i, e, g)
                    if after is not None:
                        after(g)

        def rows_of(u, s):
            return bass.ds(nc.s_assert_within(u * (2 * R) + s * R, 0, r.rows - R,
                                              skip_runtime_bounds_check_because="the blocks fit the buffer"), R)

        def second(s):
            return s if EPG == 2 else 0

        with nc.Block() as block:
            @block.sync
            def _(sp):
                def weights(i, g):
                    sp.wait_ge(w_used[g], i + 1)
                    for x_ in range(EPG):
                        e = (i * 2 + g) * EPG + x_
                        sp.dma_start(w1s[:, g * EPG + x_, :, :], w1[bass.ds(e, 1)].rearrange("o p c f -> p (o c) f"))\
                            .then_inc(w_in[g], 16)
                        sp.dma_start(w2s[:, g * EPG + x_, :, :],
                                     w2[bass.ds(e, 1)].rearrange("o (c p) n -> p (o c) n", p=128))\
                            .then_inc(w_in[g], 16)
                        sp.dma_start(b1s[:, g * EPG + x_, :], b1[bass.ds(e, 1)].rearrange("o p f -> p (o f)"))\
                            .then_inc(w_in[g], 16)

                def rows(i, u, g):
                    for s in range(2):
                        sp.wait_ge(turned[s], u + 1)
                        sp.dma_start(xb[:, s, :], buf[rows_of(u, s), :]).then_inc(rows_loaded[s], 16)
                run(sp, rows, before=weights)

            @block.gpsimd
            def _(pool):
                pool.sem_inc(yb_free[0], 1)
                pool.sem_inc(yb_free[1], 1)

                def store(i, u, g):
                    for s in range(2):
                        pool.wait_ge(y_out[s], u + 2)
                        pool.dma_start(ybuf[rows_of(u, s), :], yb[:, s, :]).then_inc(stored[s], 16)
                    for s in range(2):
                        pool.wait_ge(stored[s], u * 16 + 16)
                        pool.sem_inc(yb_free[s], 1)
                run(pool, store)

            @block.tensor
            def _(pe):
                for g in range(2):
                    pe.sem_inc(w_used[g], 1)
                    pe.sem_inc(turned[g], 1)

                def products(i, u, g):
                    for s in range(2):
                        pe.wait_ge(rows_loaded[s], u * 16 + 16)
                        for c in range(C):
                            mm = pe.transpose(ps[:, 4 * s, R * c:R * c + R], xb[:, s, 128 * c:128 * c + 128],
                                              k.ident[0:R, 0:R])
                        mm.then_inc(turned[s], 1)
                    pe.wait_ge(w_in[g], (i + 1) * (48 * EPG))
                    for s in range(2):
                        w = g * EPG + second(s)
                        pe.wait_ge(xT_out[s], u * C + C)
                        for m in range(FC):
                            for c in range(C):
                                mm = pe.matmul(ps[:, 4 * s + 1, R * m:R * m + R],
                                               w1s[:, w, c, 128 * m:128 * m + 128],
                                               xbT[:, s, c, :], start=(c == 0), stop=(c == C - 1))
                        mm.then_inc(h_done[s], 1)
                    for s in range(2):
                        w = g * EPG + second(s)
                        pe.wait_ge(h_out[s], u * FC + FC)
                        pe.wait_ge(y_out[s], u + 1)
                        for m in range(FC):
                            mm = pe.matmul(ps[0:R, 4 * s + 2, :], hT[:, s, m, :], w2s[:, w, m, :],
                                           start=(m == 0), stop=(m == FC - 1))
                        mm.then_inc(y_done[s], 1)

                run(pe, products, after=lambda g: pe.drain().then_inc(w_used[g], 1))

            @block.scalar
            def _(act):
                def bend(i, u, g):
                    for s in range(2):
                        act.wait_ge(turned[s], u + 2)
                        for c in range(C):
                            o, in_ = xbT[:, s, c, :], ps[:, 4 * s, R * c:R * c + R]
                            if affine is None:
                                act.activation(o, in_, ACT.Copy).then_inc(xT_out[s], 1)
                            else:
                                act.activation(o, in_, ACT.Identity, bias=affine[1][:, c:c + 1],
                                               scale=affine[0][:, c:c + 1]).then_inc(xT_out[s], 1)
                    for s in range(2):
                        act.wait_ge(h_done[s], u + 1)
                        for m in range(FC):
                            act.activation(hT[:, s, m, :], ps[:, 4 * s + 1, R * m:R * m + R], func,
                                           bias=b1s[:, g * EPG + second(s), m:m + 1]).then_inc(h_out[s], 1)
                run(act, bend)

            @block.vector
            def _(v):
                v.sem_inc(y_out[0], 1)
                v.sem_inc(y_out[1], 1)

                def take(i, u, g):
                    for s in range(2):
                        v.wait_ge(y_done[s], u + 1)
                        v.wait_ge(yb_free[s], u + 1)
                        v.tensor_copy(yb[:, s, :], ps[0:R, 4 * s + 2, :]).then_inc(y_out[s], 1)
                run(v, take)


def combine(nc, k, r, x, res, b2, ybuf, E_):
    with ExitStack() as ctx:
        Y = ctx.enter_context(nc.sbuf_tensor(k.name("Y"), [P, 4, D], fp32))
        got = [k.gpsimd_dma_semaphore(nc, "got") for _ in range(4)]
        used, summed, taken = (ctx.enter_context(k.semaphore(nc, k.name(n))) for n in ("y_used", "summed", "taken"))
        K_ = r.topk
        with nc.Block() as block:
            @block.gpsimd
            def _(pool):
                for n in range(K_ * T):
                    t, c = n // K_, n % K_
                    if n >= 4:
                        pool.wait_ge(used, n - 3)
                    pool.indirect_dma_start(Y[:, n % 4, :], None, ybuf,
                                            bass.IndirectOffsetOnAxis(ap=r.get[:, c, t:t + 1], axis=0))\
                        .then_inc(got[n % 4], 16)

            @block.tensor
            def _(pe):
                for t in range(T):
                    if t >= 8:
                        pe.wait_ge(taken, 2 * (t - 7))
                    pe.matmul(k.ps[0:P, t % 8, :], r.gateT[:, P * t:P * t + P], b2, start=True, stop=True)\
                        .then_inc(summed, 1)

            @block.vector
            def _(v):
                for t in range(T):
                    v.wait_ge(summed, t + 1)
                    if res is not None:
                        v.tensor_tensor(x[:, t, :], x[:, t, :], res[:, t, :], ALU.add).then_inc(taken, 1)
                    else:
                        v.sem_inc(taken, 1)
                    v.wait_ge(taken, 2 * t + 1)
                    v.tensor_tensor(x[:, t, :], x[:, t, :], k.ps[0:P, t % 8, :], ALU.add).then_inc(taken, 1)
                    v.wait_ge(taken, 2 * t + 2)
                    for c in range(K_):
                        n = t * K_ + c
                        v.wait_ge(got[n % 4], 16 * (n // 4 + 1))
                        v.scalar_tensor_tensor(x[:, t, :], Y[:, n % 4, :], r.gate[:, c, t:t + 1], x[:, t, :],
                                               ALU.mult, ALU.add).then_inc(used, 1)
                        v.wait_ge(used, n + 1)
class Routing:

    def __init__(self, nc, k, ctx, E_, topk, cap):
        self.topk = topk
        blocks = None if cap else E_ + N // (2 * P) - 1
        self.max_blocks = blocks
        self.rows = E_ * cap if cap else blocks * 2 * P
        self.spare0 = self.rows
        self.put = ctx.enter_context(nc.sbuf_tensor(k.name("put"), [P, 2, T], u32))
        self.get = ctx.enter_context(nc.sbuf_tensor(k.name("get"), [P, 2, T], u32))
        self.gate = ctx.enter_context(nc.sbuf_tensor(k.name("gate"), [P, 2, T], fp32))
        self.gateT = ctx.enter_context(nc.sbuf_tensor(k.name("gateT"), [E_, N], fp32))
        self.tab = ctx.enter_context(nc.sbuf_tensor(k.name("tab"), [1, 2, E_], i32))


def rowtiles(ap):
    return ap.rearrange("(t p) n -> p t n", p=P)


def kchunks(ap):
    return ap.rearrange("(c p) n -> p c n", p=128)


def row(ap):
    return ap.rearrange("(o n) -> o n", o=1)


def l0_gnn(nc, k, a, x, G):
    with ExitStack() as ctx:
        def sb(name, shape):
            return ctx.enter_context(nc.sbuf_tensor(k.name(name), shape, fp32))
        h, hT, mT = sb("h", [P, T, D]), sb("hT", [128, C, N]), sb("meanT", [128, C, N])
        wl, wr, bl = sb("wl", [128, C, D]), sb("wr", [128, C, D]), sb("bl", [1, D])
        norm_rows(nc, k, x, h, hT)
        for l in range(2):
            load(nc, k, [(wl[:, :, :], kchunks(a[f"L0_gnn_Wl{l}T"])), (wr[:, :, :], kchunks(a[f"L0_gnn_Wr{l}T"])),
                         (bl[:, :], row(a[f"L0_gnn_bl{l}"]))])
            columns_product(nc, k, h, G, T, C, lambda act, m, ch, n, psum:
                            act.activation(mT[:, m, ch[0]:ch[0] + ch[1]], psum, ACT.Copy))
            rows_product(nc, k, [(mT, wl, C), (hT, wr, C)], bl[:, :], copy_rows(h, ACT.Relu))
            if l == 0:
                transpose_only(nc, k, h, hT)
        add_into(nc, k, x, h)


def transformer(nc, k, a, x, pre, E_, F, cap, func, keep_last, buf, ybuf):
    with ExitStack() as ctx:
        def sb(c_, name, shape):
            return c_.enter_context(nc.sbuf_tensor(k.name(name), shape, fp32))
        res, xnT = sb(ctx, "res", [P, T, D]), sb(ctx, "xnT", [128, C, N])
        g1, b1, g2, b2 = (sb(ctx, n, [128, C]) for n in ("g1", "b1", "g2", "b2"))
        load(nc, k, [(g1[:, :], a[pre + "ln1_g_c"]), (b1[:, :], a[pre + "ln1_b_c"]),
                     (g2[:, :], a[pre + "ln2_g_c"]), (b2[:, :], a[pre + "ln2_b_c"])])
        norm_rows(nc, k, x, res)
        bias = pre + "bo" in a
        with ExitStack() as c2:
            xn = sb(c2, "xn", [P, T, D])
            norm_rows(nc, k, res, xn, xnT, (g1, b1))
        with ExitStack() as c2:
            ctxT = sb(c2, "ctxT", [128, C, N])
            attention(nc, k, xnT, a[pre + "wqk"], a[pre + "wv_h"], a[pre + "bqk"] if bias else None,
                      row(a[pre + "bv"]) if bias else None, ctxT)
            wo, bo = sb(c2, "wo", [128, C, D]), sb(c2, "bo", [1, D])
            load(nc, k, [(wo[:, :, :], kchunks(a[pre + "wo"]))] + ([(bo[:, :], row(a[pre + "bo"]))] if bias else []))
            rows_product(nc, k, [(ctxT, wo, C)], bo[:, :] if bias else None, add_rows(res))
        yn = sb(ctx, "yn", [P, T, D])
        norm_rows(nc, k, res, yn, xnT, (g2, b2))
        r = Routing(nc, k, ctx, E_, 2, cap)
        with ExitStack() as c2:
            wr, br = sb(c2, "wr", [128, C, E_]), sb(c2, "br", [1, E_])
            load(nc, k, [(wr[:, :, :], kchunks(a[pre + ("router_w" if bias else "wr")]))]
                 + ([(br[:, :], row(a[pre + "router_b"]))] if bias else []))
            route(nc, k, xnT, wr, br[:, :] if bias else None, E_, 2, cap, keep_last, r)
        b2r = sb(ctx, "b2r", [E_, D])
        load(nc, k, [(b2r[:, :], a[pre + "b2"])])
        R = 78 if cap == 78 else P
        experts(nc, k, r, yn, E_, F, R, 1 if R == cap else 2, func, a[pre + "w1_p"], a[pre + "b1_p"], a[pre + "w2"],
                (g2, b2), buf, ybuf, False)
        combine(nc, k, r, x, res, b2r[:, :], ybuf, E_)


def l1_gnn(nc, k, a, x, G):
    with ExitStack() as ctx:
        def sb(name, shape):
            return ctx.enter_context(nc.sbuf_tensor(k.name(name), shape, fp32))
        xn, xT, w, b = sb("xn", [P, T, D]), sb("xT", [128, C, N]), sb("w", [128, C, D]), sb("b", [1, D])
        load(nc, k, [(w[:, :, :], kchunks(a["L1_gnn_weight"])), (b[:, :], row(a["L1_gnn_bias"]))])
        norm_rows(nc, k, x, xn, xT)
        rows_product(nc, k, [(xT, w, C)], None, copy_rows(xn))
        rows_product(nc, k, [(G, xn, T)], b[:, :], add_rows(x))


def l3_gnn(nc, k, a, x, G):
    with ExitStack() as ctx:
        def sb(name, shape):
            return ctx.enter_context(nc.sbuf_tensor(k.name(name), shape, fp32))
        xn, xT, w, b = sb("xn", [P, T, D]), sb("xT", [128, C, N]), sb("w", [128, C, D]), sb("b", [1, D])
        load(nc, k, [(w[:, :, :], kchunks(a["L3_gnn_W"])), (b[:, :], row(a["L3_gnn_b"]))])
        norm_rows(nc, k, x, xn, xT)
        rows_product(nc, k, [(xT, w, C)], b[:, :], copy_rows(xn))
        rows_product(nc, k, [(G, xn, T)], None,
                     {"vector": lambda v, i, psum: v.scalar_tensor_tensor(x[:, i, :], psum, 0.0, x[:, i, :],
                                                                          ALU.max, ALU.add)})


def l2_gnn(nc, k, a, x, G):
    with ExitStack() as ctx:
        def sb(name, shape):
            return ctx.enter_context(nc.sbuf_tensor(k.name(name), shape, fp32))

        def sem(name):
            return ctx.enter_context(k.semaphore(nc, k.name(name)))
        h, xT, aT = sb("h", [P, T, D]), sb("xT", [128, C, N]), sb("aggT", [128, C, N])
        w = sb("w", [128, C, D])
        cols = sb("bgb", [128, 3, 3, C])
        st, mv = sb("bn_parts", [128, C, 3, 6]), sb("mean_var", [128, C, 2])
        sc, sh = sb("scale", [128, C]), sb("shift", [128, C])
        norm_rows(nc, k, x, h, xT)
        for l in range(3):
            steps, var_ready, std_ready, scale_ready = sem("steps"), sem("var"), sem("std"), sem("scale_ready")
            load(nc, k, [(w[:, :, :], kchunks(a["L2_gnn_WT"][l]))] + ([(cols[:, :, :, :], a["L2_gnn_bgb"])] if l == 0 else []))
            rows_product(nc, k, [(xT, w, C)], None, copy_rows(h))
            columns_product(nc, k, h, G, T, C, lambda act, m, ch, n, psum:
                            act.activation(aT[:, m, ch[0]:ch[0] + ch[1]], psum, ACT.Identity,
                                           bias=cols[:, 0, l, m:m + 1]))
            with nc.Block() as block:
                @block.vector
                def _(v):
                    s = Steps(v, steps)
                    for m in range(C):
                        for n, (c0, cn) in enumerate(CH):
                            s.did(v.bn_stats(st[:, m, n, :], aT[:, m, c0:c0 + cn]))
                    s.wait()
                    for m in range(C):
                        s.did(v.bn_aggr(mv[:, m, :], st[:, m, :, :].rearrange("p a b -> p (a b)")))
                    s.wait()
                    v.tensor_scalar(sc[:, :], mv[:, :, 1], 1e-5, None, ALU.add).then_inc(var_ready, 1)
                    v.wait_ge(std_ready, 1)
                    s.did(v.reciprocal(sh[:, :], sc[:, :]))
                    s.wait()
                    s.did(v.tensor_tensor(sc[:, :], sh[:, :], cols[:, 1, l, :], ALU.mult))
                    s.wait()
                    s.did(v.tensor_tensor(sh[:, :], mv[:, :, 0], sc[:, :], ALU.mult))
                    s.wait()
                    v.tensor_tensor(sh[:, :], cols[:, 2, l, :], sh[:, :], ALU.subtract).then_inc(scale_ready, 1)

                @block.scalar
                def _(act):
                    act.wait_ge(var_ready, 1)
                    act.activation(sc[:, :], sc[:, :], ACT.Sqrt).then_inc(std_ready, 1)
                    act.wait_ge(scale_ready, 1)
                    for m in range(C):
                        act.activation(xT[:, m, :], aT[:, m, :], ACT.Relu, bias=sh[:, m:m + 1],
                                       scale=sc[:, m:m + 1])
        turned, taken = sem("turned"), sem("taken")
        with nc.Block() as block:
            @block.tensor
            def _(pe):
                for i in range(T):
                    if i >= 8:
                        pe.wait_ge(taken, i - 7)
                    for c in range(C):
                        mm = pe.transpose(k.ps[0:P, i % 8, 128 * c:128 * c + 128], xT[:, c, P * i:P * i + P],
                                          k.ident[:, :])
                    mm.then_inc(turned, 1)

            @block.vector
            def _(v):
                for i in range(T):
                    v.wait_ge(turned, i + 1)
                    v.tensor_tensor(x[:, i, :], x[:, i, :], k.ps[0:P, i % 8, :], ALU.add).then_inc(taken, 1)


def l2_ffn(nc, k, a, x, buf, ybuf):
    E_, F = 8, 512
    with ExitStack() as ctx:
        def sb(c_, name, shape):
            return c_.enter_context(nc.sbuf_tensor(k.name(name), shape, fp32))
        xn, xT = sb(ctx, "xn", [P, T, D]), sb(ctx, "xT", [128, C, N])
        norm_rows(nc, k, x, xn, xT)
        r = Routing(nc, k, ctx, E_, 1, None)
        with ExitStack() as c2:
            wr, br = sb(c2, "wr", [128, C, E_]), sb(c2, "br", [1, E_])
            load(nc, k, [(wr[:, :, :], kchunks(a["L2_ffn_Wr"])), (br[:, :], row(a["L2_ffn_br"]))])
            route(nc, k, xT, wr, br[:, :], E_, 1, None, False, r)
        b2r = sb(ctx, "b2r", [E_, D])
        load(nc, k, [(b2r[:, :], a["L2_ffn_b2"])])
        experts(nc, k, r, xn, E_, F, P, 2, ACT.Relu, a["L2_ffn_w1_p"], a["L2_ffn_b1_p"], a["L2_ffn_W2"], None, buf, ybuf, True)
        combine(nc, k, r, x, None, b2r[:, :], ybuf, E_)


def l1_ffn(nc, k, a, x, Gf):
    E_, F, FC = 8, 256, 2
    with ExitStack() as ctx:
        def sb(c_, name, shape):
            return c_.enter_context(nc.sbuf_tensor(k.name(name), shape, fp32))

        def sem(name):
            return ctx.enter_context(k.semaphore(nc, k.name(name)))
        xn, xT, hT = sb(ctx, "xn", [P, T, D]), sb(ctx, "xT", [128, C, N]), sb(ctx, "hT", [128, FC, N])
        W1m, W2m = sb(ctx, "W1m", [128, C, F]), sb(ctx, "W2m", [128, FC, D])
        b1m, b2b, lngb, lnbb = (sb(ctx, "b1m", [128, FC]), sb(ctx, "b2b", [P, D]), sb(ctx, "lngb", [P, D]),
                                sb(ctx, "lnbb", [P, D]))
        norm_rows(nc, k, x, xn, xT)
        with ExitStack() as c2:
            gw, gb = sb(c2, "gfc1", [128, C, D]), sb(c2, "gfc1_b", [128, C])
            g2w, g2b, g2c = sb(c2, "gfc2", [128, C, E_]), sb(c2, "gfc2_b", [128, E_]), sb(c2, "gfc2_bc", [E_, 1])
            tv1 = Gf[:, :, :].rearrange("p t n -> p (t n)")[:, 0:E_ * C * F].rearrange("p (e n) -> p e n", e=E_)
            tv2 = sb(c2, "tv2", [128, E_, FC * D])
            tb1, tb2 = sb(c2, "tb1", [E_, F]), sb(c2, "tb2", [E_, D])
            tg, tb, lg8, lb8 = (sb(c2, n, [E_, D]) for n in ("tg", "tb", "lg8", "lb8"))
            b1c, rows3 = sb(c2, "b1c", [128, FC]), sb(c2, "rows3", [1, 3, D])
            gh, ghs, ghb = sb(c2, "gh", [128, 4, 500]), sb(c2, "gh_sum", [128, C, 3]), sb(c2, "ghb", [128, C, 128])
            ghm, gB, gC = sb(c2, "gh_mean", [128, C]), sb(c2, "g_all", [128, E_]), sb(c2, "g_col", [E_, 1])
            load(nc, k, [(gw[:, :, :], kchunks(a["L1_ffn_gfc1_wT"])), (gb[:, :], a["L1_ffn_gfc1_b_c"]),
                         (g2w[:, :, :], kchunks(a["L1_ffn_gfc2_wT"])),
                         (g2b[:, :], a["L1_ffn_gfc2_b"].partition_broadcast(128)),
                         (g2c[:, :], a["L1_ffn_gfc2_b"].rearrange("(p o) -> p o", o=1)),
                         (tv1[:, :, :], a["L1_ffn_tv_W1_p"]), (tv2[:, :, :], a["L1_ffn_tv_W2_p"]),
                         (W1m[:, :, :], kchunks(a["L1_ffn_W1T"])), (W2m[:, :, :], kchunks(a["L1_ffn_W2T"])),
                         (tb1[:, :], a["L1_ffn_tv_b1"]), (tb2[:, :], a["L1_ffn_tv_b2"]),
                         (tg[:, :], a["L1_ffn_tv_ln_g"]), (tb[:, :], a["L1_ffn_tv_ln_b"]),
                         (lg8[:, :], a["L1_ffn_ln_g"].partition_broadcast(E_)),
                         (lb8[:, :], a["L1_ffn_ln_b"].partition_broadcast(E_)),
                         (b1c[:, :], a["L1_ffn_b1_c"]), (rows3[:, 0, :], row(a["L1_ffn_b2"])),
                         (rows3[:, 1, :], row(a["L1_ffn_ln_g"])), (rows3[:, 2, :], row(a["L1_ffn_ln_b"]))])
            columns_product(nc, k, gw, xT, C, C, lambda act, m, ch, n, psum:
                            act.activation(gh[:, (3 * m + n) % 4, 0:ch[1]], psum, ACT.Relu, bias=gb[:, m:m + 1],
                                           accum_out=ghs[:, m, n:n + 1]), reuse=4)
            steps, mean_ready, g_done, g_out = sem("steps"), sem("mean_ready"), sem("g_done"), sem("g_out")
            rows_ready, sums_done, accs = sem("rows_ready"), sem("sums_done"), sem("accs")
            with nc.Block() as block:
                @block.tensor
                def _(pe):
                    pe.wait_ge(mean_ready, C)
                    for c in range(C):
                        pe.matmul(k.ps[:, 0, 0:E_], ghb[:, c, :], g2w[:, c, :], start=(c == 0), stop=(c == C - 1))
                    for c in range(C):
                        mm = pe.matmul(k.ps[0:E_, 1, 0:1], g2w[:, c, :], ghm[:, c:c + 1], start=(c == 0),
                                       stop=(c == C - 1))
                    mm.then_inc(g_done, 1)
                    pe.wait_ge(rows_ready, 4)
                    for n, t_ in enumerate((tb2, tg, tb)):
                        pe.matmul(k.ps[0:P, 2 + n, :], k.ones[0:E_, 0:P], t_[:, :], start=True, stop=False)
                        pe.matmul(k.ps[0:P, 2 + n, :], k.ones[0:1, 0:P], rows3[:, n, :], start=False, stop=True)
                    for m in range(FC):
                        mm = pe.matmul(k.ps[:, 5, m:m + 1], tb1[:, 128 * m:128 * m + 128], gC[:, :], start=True,
                                       stop=True, skip_group_check=True)
                    mm.then_inc(sums_done, 1)

                @block.scalar
                def _(act):
                    act.wait_ge(sums_done, 1)
                    for n, o in enumerate((b2b, lngb, lnbb)):
                        act.activation(o[:, :], k.ps[0:P, 2 + n, :], ACT.Copy)

                @block.vector
                def _(v):
                    s = Steps(v, steps)
                    s.did(v.tensor_reduce(ghm[:, :], ghs[:, :, :], AX.X, ALU.add))
                    s.wait()
                    s.did(v.tensor_scalar(ghm[:, :], ghm[:, :], 1.0 / N, None, ALU.mult))
                    s.wait()
                    for c in range(C):
                        v.tensor_scalar(ghb[:, c, :], k.ones[:, :], ghm[:, c:c + 1], None, ALU.mult)\
                            .then_inc(mean_ready, 1)
                    s.did(v.tensor_tensor(tg[:, :], tg[:, :], lg8[:, :], ALU.subtract))
                    s.did(v.tensor_tensor(tb[:, :], tb[:, :], lb8[:, :], ALU.subtract))
                    s.wait()
                    v.tensor_scalar(tg[:, :], tg[:, :], 0.03, None, ALU.mult).then_inc(rows_ready, 1)
                    v.tensor_scalar(tb[:, :], tb[:, :], 0.03, None, ALU.mult).then_inc(rows_ready, 1)
                    v.wait_ge(g_done, 1)
                    s.did(v.tensor_tensor(gB[:, :], g2b[:, :], k.ps[:, 0, 0:E_], ALU.add))
                    v.tensor_tensor(gC[:, :], g2c[:, :], k.ps[0:E_, 1, 0:1], ALU.add).then_inc(rows_ready, 1)
                    v.wait_ge(rows_ready, 3)
                    s.wait()
                    v.tensor_scalar(tb2[:, :], tb2[:, :], gC[:, 0:1], None, ALU.mult).then_inc(rows_ready, 1)
                    W1f = W1m[:, :, :].rearrange("p c f -> p (c f)")
                    W2f = W2m[:, :, :].rearrange("p c f -> p (c f)")
                    for e in range(E_):
                        if e:
                            v.wait_ge(accs, 2 * e)
                        v.scalar_tensor_tensor(W1f, tv1[:, e, :], gB[:, e:e + 1], W1f, ALU.mult, ALU.add)\
                            .then_inc(accs, 1)
                        v.scalar_tensor_tensor(W2f, tv2[:, e, :], gB[:, e:e + 1], W2f, ALU.mult, ALU.add)\
                            .then_inc(accs, 1)
                    v.wait_ge(sums_done, 1)
                    v.tensor_tensor(b1m[:, :], b1c[:, :], k.ps[:, 5, 0:FC], ALU.add)
        columns_product(nc, k, W1m, xT, C, FC, lambda act, m, ch, n, psum:
                        act.activation(hT[:, m, ch[0]:ch[0] + ch[1]], psum, ACT.Relu, bias=b1m[:, m:m + 1]))
        rows_product(nc, k, [(hT, W2m, FC)], None, add_rows(xn))
        steps = sem("steps")
        with nc.Block() as block:
            @block.vector
            def _(v):
                v.tensor_tensor(xn[:, :, :], xn[:, :, :], b2b[:, :].unsqueeze(1).broadcast_to([P, T, D]), ALU.add)
        norm_rows(nc, k, xn, xn)
        with nc.Block() as block:
            @block.vector
            def _(v):
                s = Steps(v, steps)
                s.did(v.tensor_tensor(xn[:, :, :], xn[:, :, :], lngb[:, :].unsqueeze(1).broadcast_to([P, T, D]),
                                      ALU.mult))
                s.wait()
                s.did(v.tensor_tensor(xn[:, :, :], xn[:, :, :], lnbb[:, :].unsqueeze(1).broadcast_to([P, T, D]),
                                      ALU.add))
                s.wait()
                s.did(v.tensor_tensor(x[:, :, :], x[:, :, :], xn[:, :, :], ALU.add))


def finish_graph(nc, k, CT, WT, W, w_spill, ah_spill):
    with ExitStack() as ctx:
        def sb(name, shape):
            return ctx.enter_context(nc.sbuf_tensor(k.name(name), shape, fp32))

        def sem(name):
            return ctx.enter_context(k.semaphore(nc, k.name(name)))
        deg, rc, dr = sb("deg", [P, N]), sb("inv_deg", [P, N]), sb("dinv_row", [P, N])
        dc, junk = sb("dinv_col", [P, T]), sb("junk", [P, P])
        turned, taken, deg_done, steps = sem("turned"), sem("taken"), sem("deg_done"), sem("steps")
        deg1, root_done, spilled = sem("deg1"), sem("root_done"), sem("spilled")
        scaled, normed = sem("scaled"), sem("normed")
        with nc.Block() as block:
            @block.tensor
            def _(pe):
                for n, (c0, cn) in enumerate(CH):
                    for t in range(T):
                        mm = pe.matmul(k.ps[0:P, 5 + n, 0:cn], k.ones[0:P, 0:P], CT[:, t, c0:c0 + cn],
                                       start=(t == 0), stop=(t == T - 1))
                    mm.then_inc(deg_done, 1)
                g = 0
                for d in range(T):
                    for c0, cn in CH:
                        if g >= 5:
                            pe.wait_ge(taken, g - 4)
                        for s_ in range(c0 // P, (c0 + cn) // P):
                            mm = pe.transpose(k.ps[0:P, g % 5, P * s_ - c0:P * s_ - c0 + P],
                                              WT[:, s_, P * d:P * d + P], k.ident[0:P, 0:P])
                        mm.then_inc(turned, 1)
                        g += 1

            @block.scalar
            def _(act):
                g = 0
                for d in range(T):
                    for c0, cn in CH:
                        act.wait_ge(turned, g + 1)
                        act.activation(W[:, d, c0:c0 + cn], k.ps[0:P, g % 5, 0:cn], ACT.Copy).then_inc(taken, 1)
                        g += 1
                act.wait_ge(deg1, 1)
                act.activation(rc[:, :], dr[:, :], ACT.Sqrt).then_inc(root_done, 1)

            @block.vector
            def _(v):
                s = Steps(v, steps)
                v.wait_ge(deg_done, 3)
                for n, (c0, cn) in enumerate(CH):
                    s.did(v.tensor_copy(deg[:, c0:c0 + cn], k.ps[0:P, 5 + n, 0:cn]))
                s.wait()
                v.tensor_scalar(dr[:, :], deg[:, :], 1.0, None, ALU.add).then_inc(deg1, 1)
                v.wait_ge(root_done, 1)
                s.did(v.reciprocal(dr[:, :], rc[:, :]))
                s.did(v.tensor_scalar(deg[:, :], deg[:, :], 1.0, None, ALU.max))
                s.wait()
                s.did(v.reciprocal(rc[:, :], deg[:, :]))
                for t in range(T):
                    s.did(v.tensor_tensor(junk[:, :], dr[:, P * t:P * t + P], k.ident[0:P, 0:P], ALU.mult))
                    s.wait()
                    s.did(v.tensor_reduce(dc[:, t:t + 1], junk[:, :], AX.X, ALU.add))
                    s.wait()
        diag = sb("diag", [P, T, P])
        with nc.Block() as block:
            @block.sync
            def _(sp):
                spill_rows(sp, rowtiles(w_spill), W, spilled)
                sp.wait_ge(normed, T)
                spill_rows(sp, rowtiles(ah_spill), WT, spilled)
                sp.wait_ge(spilled, 64)

            @block.vector
            def _(v):
                for t in range(T):
                    v.scalar_tensor_tensor(WT[:, t, :], CT[:, t, :], dc[:, t:t + 1], dr[:, :], ALU.mult, ALU.mult)\
                        .then_inc(scaled, 1)
                    v.scalar_tensor_tensor(diag[:, t, :], k.ident[0:P, 0:P], dc[:, t:t + 1],
                                           dr[:, P * t:P * t + P], ALU.mult, ALU.mult).then_inc(scaled, 1)
                v.wait_ge(scaled, 2 * T)
                for t in range(T):
                    v.tensor_tensor(WT[:, t, P * t:P * t + P], WT[:, t, P * t:P * t + P], diag[:, t, :], ALU.add)\
                        .then_inc(normed, 1)
                for t in range(T):
                    v.tensor_tensor(CT[:, t, :], CT[:, t, :], rc[:, :], ALU.mult)


def spill_rows(sp, dram, sbuf, sem):
    sp.dma_start(dram[0:120], sbuf[0:120]).then_inc(sem, 16)
    sp.dma_start(dram[120:P], sbuf[120:P]).then_inc(sem, 16)




def program(nc, a, out):
    k = Kit()
    with ExitStack() as ctx:
        k.lasting = ctx
        k.ps = ctx.enter_context(nc.psum_tensor("ps", [128, 8, 512], fp32))
        k.ident = ctx.enter_context(nc.sbuf_tensor("ident", [128, 128], fp32))
        k.ones = ctx.enter_context(nc.sbuf_tensor("ones", [128, 128], fp32))
        k.tri = ctx.enter_context(nc.sbuf_tensor("tri", [128, 128], fp32))
        k.ones_row = ctx.enter_context(nc.sbuf_tensor("ones_row", [1, 512], fp32))
        k.ones16 = ctx.enter_context(nc.sbuf_tensor("ones16", [128, 128], bf16))
        k.tri16 = ctx.enter_context(nc.sbuf_tensor("tri16", [128, 128], bf16))
        k.c_sel, k.c_win = a["c_sel"], a["c_win"]
        Gf = ctx.enter_context(nc.sbuf_tensor("G", [128, T, N], fp32))
        x = ctx.enter_context(nc.sbuf_tensor("x", [P, T, D], fp32))
        G = Gf[0:P]
        zeroed = ctx.enter_context(k.semaphore(nc, "zeroed"))
        stored = ctx.enter_context(k.semaphore(nc, "stored"))

        def scratch(name, shape, dt=fp32):
            return nc.dram_tensor(name, shape, dt).ap()
        w_spill, ah_spill = scratch("w_spill", (N, N)), scratch("ah_spill", (N, N))
        NB0, NB3 = 64 * 78, 8 * 250
        NB2 = 12 * 250
        buf0, buf3, buf2 = (scratch("buf0", (NB0 + 2 * N, D)), scratch("buf3", (NB3 + 2 * N, D)),
                            scratch("buf2", (NB2, D)))
        yb0, yb3 = scratch("yb0", (NB0, D)), scratch("yb3", (NB3, D))
        scr1, scr2 = scratch("scr_minmax", (2, ET)), scratch("scr_tab", (NW, 4), i32)

        load(nc, k, [(k.ident[:, :], a["c_ident"]), (k.tri[:, :], a["c_tri"]), (x[:, :, :], rowtiles(a["x"]))])
        with nc.sbuf_tensor("zeros", [128, 2 * D], fp32) as zeros, k.semaphore(nc, "zero_set") as zero_set:
            with nc.Block() as block:
                @block.vector
                def _(v):
                    v.memset(k.ones[:, :], 1.0)
                    v.memset(k.ones_row[:, :], 1.0)
                    v.memset(k.ones16[:, :], 1.0)
                    v.tensor_copy(k.tri16[:, :], k.tri[:, :])
                    v.memset(zeros[:, :], 0.0).then_inc(zero_set, 1)

                @block.sync
                def _(sp):
                    sp.wait_ge(zero_set, 1)
                    n = 0
                    for b, rows in ((buf0, NB0), (buf3, NB3), (buf2, NB2)):
                        for r0 in range(0, rows, 256):
                            m = min(256, rows - r0)
                            m2 = m // 2
                            sp.dma_start(b[r0:r0 + m, :].rearrange("(p q) n -> p q n", q=2),
                                         zeros[0:m2, :].rearrange("p (q n) -> p q n", q=2)).then_inc(zeroed, 16)
                            n += 16
                    sp.wait_ge(zeroed, n)
        with ExitStack() as c2:
            WT = c2.enter_context(nc.sbuf_tensor("WT", [P, T, N], fp32))
            build_graph(nc, k, G, WT, a["src_pt"], a["dst_pt"], a["w_pt"], a["dst_rows"], scr1, scr2)
            W = c2.enter_context(nc.sbuf_tensor("W", [P, T, N], fp32))
            finish_graph(nc, k, G, WT, W, w_spill, ah_spill)

        def load_matrix(dram):
            with k.semaphore(nc, k.name("matrix_in")) as loaded:
                with nc.Block() as block:
                    @block.sync
                    def _(sp):
                        spill_rows(sp, G, rowtiles(dram), loaded)
                        sp.wait_ge(loaded, 32)
        k.clear_semaphores(nc)
        l0_gnn(nc, k, a, x, G)
        k.clear_semaphores(nc)
        transformer(nc, k, a, x, "L0_ffn_", 64, 256, 78, ACT.Gelu_apprx_tanh, False, buf0, yb0)
        k.clear_semaphores(nc)
        load_matrix(w_spill)
        l1_gnn(nc, k, a, x, G)
        l1_ffn(nc, k, a, x, Gf)
        k.clear_semaphores(nc)
        load_matrix(ah_spill)
        l2_gnn(nc, k, a, x, G)
        k.clear_semaphores(nc)
        l2_ffn(nc, k, a, x, buf2, buf2)
        k.clear_semaphores(nc)
        l3_gnn(nc, k, a, x, G)
        k.clear_semaphores(nc)
        transformer(nc, k, a, x, "L3_ffn_", 8, 256, 250, ACT.Gelu, True, buf3, yb3)
        with nc.Block() as block:
            @block.sync
            def _(sp):
                spill_rows(sp, rowtiles(out), x, stored)
                sp.wait_ge(stored, 32)


def layouts(inputs):
    import numpy as _np

    a = {n: _np.asarray(v) for n, v in inputs.items()}

    def heads(w):
        return w.reshape(C, 128, 8, 64).transpose(2, 1, 0, 3)

    def columns(b):
        return b.reshape(-1, 128).T

    w = _np.arange(NW)
    base = P * (w // WPT) + WIN * (w % WPT)
    p = _np.arange(128)
    sel = _np.zeros((128, 2 * WIN), _np.float32)
    sel[p[:WIN], p[:WIN]] = 1
    for m in (1, 2, 3):
        sel[WIN * m + p[:WIN], WIN + p[:WIN]] = 1
    o = {"c_sel": sel, "c_win": _np.stack([base, base + WIN - 1], 1).astype(_np.float32),
         "c_tri": (p[:, None] < p[None, :]).astype(_np.float32), "c_ident": _np.eye(128, dtype=_np.float32),
         "x": a["x"], "src_pt": a["src"].reshape(ET, P).T, "dst_pt": a["dst"].reshape(ET, P).T,
         "w_pt": a["edge_weight"].reshape(ET, P).T, "dst_rows": a["dst"].reshape(80, 4, P)}
    for l in range(2):
        o[f"L0_gnn_Wl{l}T"], o[f"L0_gnn_Wr{l}T"] = a[f"L0_gnn_Wl{l}"].T, a[f"L0_gnn_Wr{l}"].T
        o[f"L0_gnn_bl{l}"] = a[f"L0_gnn_bl{l}"]
    for pre, names in (("L0_ffn_", ("wo", "wr", "w2", "b2")),
                       ("L3_ffn_", ("wo", "bo", "bv", "router_w", "router_b", "w2", "b2"))):
        for n in names:
            o[pre + n] = a[pre + n]
        o[pre + "wqk"] = _np.concatenate([heads(a[pre + "wq"]), heads(a[pre + "wk"])], 3)
        o[pre + "wv_h"] = heads(a[pre + "wv"])
        for n in ("ln1_g", "ln1_b", "ln2_g", "ln2_b"):
            o[pre + n + "_c"] = columns(a[pre + n])
        e, d, f = a[pre + "w1"].shape
        o[pre + "w1_p"] = a[pre + "w1"].reshape(e, C, 128, f).transpose(0, 2, 1, 3)
        o[pre + "b1_p"] = a[pre + "b1"].reshape(e, f // 128, 128).transpose(0, 2, 1)
    o["L3_ffn_bqk"] = _np.concatenate([a["L3_ffn_bq"].reshape(8, 64), a["L3_ffn_bk"].reshape(8, 64)], 1)
    for n in ("L1_gnn_weight", "L1_gnn_bias", "L3_gnn_W", "L3_gnn_b", "L2_ffn_Wr", "L2_ffn_br", "L2_ffn_W2",
              "L2_ffn_b2", "L1_ffn_gfc2_b", "L1_ffn_tv_b1", "L1_ffn_tv_b2", "L1_ffn_tv_ln_g", "L1_ffn_tv_ln_b",
              "L1_ffn_ln_g", "L1_ffn_ln_b", "L1_ffn_b2"):
        o[n] = a[n]
    o["L2_ffn_w1_p"] = a["L2_ffn_W1"].reshape(8, C, 128, 512).transpose(0, 2, 1, 3)
    o["L2_ffn_b1_p"] = a["L2_ffn_b1"].reshape(8, 4, 128).transpose(0, 2, 1)
    o["L2_gnn_WT"] = a["L2_gnn_W"].transpose(0, 2, 1)
    o["L2_gnn_bgb"] = _np.stack([a["L2_gnn_" + n].reshape(3, C, 128).transpose(2, 0, 1)
                                 for n in ("b", "gamma", "beta")], 1)
    o["L1_ffn_gfc1_wT"], o["L1_ffn_gfc2_wT"] = a["L1_ffn_gfc1_w"].T, a["L1_ffn_gfc2_w"].T
    o["L1_ffn_gfc1_b_c"], o["L1_ffn_b1_c"] = columns(a["L1_ffn_gfc1_b"]), columns(a["L1_ffn_b1"])
    o["L1_ffn_W1T"], o["L1_ffn_W2T"] = a["L1_ffn_W1"].T, a["L1_ffn_W2"].T
    o["L1_ffn_tv_W1_p"] = a["L1_ffn_tv_W1"].reshape(8, 256, C, 128).transpose(3, 0, 2, 1).reshape(128, 8, C * 256)
    o["L1_ffn_tv_W2_p"] = a["L1_ffn_tv_W2"].reshape(8, D, 2, 128).transpose(3, 0, 2, 1).reshape(128, 8, 2 * D)
    return {"in_" + n: _np.ascontiguousarray(v) for n, v in o.items()}


def kernel(**inputs):
    import concourse.bacc as _bacc
    from concourse import mybir as _mybir
    from concourse.bass_utils import run_bass_kernel_spmd as _run

    nc = _bacc.Bacc("TRN2", target_bir_lowering=False, num_devices=1)
    arrays = layouts(inputs)
    a = {n[3:]: nc.dram_tensor(n, v.shape, _mybir.dt.from_np(v.dtype), kind="ExternalInput").ap()
         for n, v in arrays.items()}
    out = nc.dram_tensor("out_x", (N, D), _mybir.dt.float32, kind="ExternalOutput").ap()
    program(nc, a, out)
    r = _run(nc, [arrays], core_ids=[0])
    return r.results[0]["out_x"]
```

```python
import concourse.bass as bass
from concourse import mybir
from contextlib import ExitStack, contextmanager
import numpy as np

N = 1250
D = 512
E = 40000
P = 125
T = N // P
C = D // 128
ET = E // P
ETP = ET + 2
WIN = 32
WPT = 4
NW = T * WPT
CH = [(0, 500), (500, 500), (1000, 250)]

fp32 = mybir.dt.float32
f32r = mybir.dt.float32r
fp16 = mybir.dt.float16
bf16 = mybir.dt.bfloat16
i32 = mybir.dt.int32
u32 = mybir.dt.uint32
ALU = mybir.AluOpType
ACT = mybir.ActivationFunctionType
AX = mybir.AxisListType


class Steps:

    def __init__(self, eng, sem, base=0):
        self.eng, self.sem, self.base, self.n = eng, sem, base, 0

    def did(self, ins):
        ins.then_inc(self.sem, 1)
        self.n += 1
        return ins

    def wait(self):
        self.eng.wait_ge(self.sem, self.base + self.n)


def load_rows(eng, dst, src, sem):
    eng.dma_start(dst[0:120], src[0:120]).then_inc(sem, 16)
    eng.dma_start(dst[120:P], src[120:P]).then_inc(sem, 16)
def build_graph(nc, k, CT, WT, src_pt, dst_pt, w_pt, dst_rows, scr_minmax, scr_tab, beside):
    SLOTS = 8
    with ExitStack() as ctx:
        def sb(name, shape, dt=fp32):
            return ctx.enter_context(nc.sbuf_tensor(name, shape, dt))

        def sem(name):
            return ctx.enter_context(k.semaphore(nc, name))

        ei = sb("edge_int", [P, 2, ET], i32)
        dF = sb("dst_f", [P, ETP])
        sF = sb("src_f", [P, ETP])
        wF = sb("w_f", [P, 3, ET])
        wp = sb("w_parts", [P, ETP, 4], bf16)
        dr = sb("dst_rows", [80, 4, P], i32)
        mm = sb("tile_minmax", [80, 2, 4])
        mb = sb("minmax_b", [NW, 2, ET])
        ov = sb("overlap", [NW, 3, ET])
        tl = sb("win_limits", [NW, 8])
        ti = sb("win_ints", [NW, 4], i32)
        tf = sb("win_tab", [NW, 4], i32)
        tab = sb("win_row", [1, NW * 4], i32)
        ioi = sb("iota_i", [P, N], i32)
        io16 = sb("iota16", [P, N + WIN], fp16)
        iot = sb("iota_t", [NW, ET])
        sel = sb("sel_parts", [128, 64])
        ohs = sb("onehot_src", [P, SLOTS, N], bf16)
        ohd = sb("onehot_dst", [P, SLOTS, 4 * WIN], bf16)
        stage = sb("stage", [128, 2, N])
        ps = k.ps

        edges_in, consts_in, minmax_in, tab_in = (sem(n) for n in ("edges_in", "consts_in", "minmax_in", "tab_in"))
        steps, minmax_ready, iota_done = sem("table_steps"), sem("minmax_ready"), sem("iota_done")
        lens_ready, before_ready, table_ready = sem("lens_ready"), sem("before_ready"), sem("table_ready")

        with nc.Block() as block:
            @block.sync
            def _(sp):
                sp.dma_start(dr[:, :, :], dst_rows).then_inc(edges_in, 16)
                sp.dma_start(ei[:, 0, :], src_pt).then_inc(edges_in, 16)
                sp.dma_start(ei[:, 1, :], dst_pt).then_inc(edges_in, 16)
                sp.dma_start(wF[:, 0, :], w_pt).then_inc(edges_in, 16)
                sp.dma_start(sel[:, :], k.c_sel).then_inc(consts_in, 16)
                sp.dma_start(tl[:, 0:2], k.c_win).then_inc(consts_in, 16)
                sp.wait_ge(minmax_ready, 2)
                sp.dma_start(scr_minmax.rearrange("m (p q) -> p m q", q=4), mm[:, :, :]).then_inc(minmax_in, 16)
                sp.wait_ge(minmax_in, 16)
                sp.dma_start(mb[:, :, :], scr_minmax.partition_broadcast(NW)).then_inc(minmax_in, 16)
                sp.wait_ge(table_ready, 4)
                sp.dma_start(scr_tab, tf[:, :]).then_inc(tab_in, 16)
                sp.wait_ge(tab_in, 16)
                sp.dma_start(tab[:, :], scr_tab.rearrange("(o w) c -> o (w c)", o=1)).then_inc(tab_in, 16)
                sp.wait_ge(tab_in, 32)

            @block.gpsimd
            def _(pool):
                pool.iota(ioi[:, :], [[1, N]], base=0, channel_multiplier=0).then_inc(iota_done, 1)
                pool.iota(iot[:, :], [[1, ET]], base=0, channel_multiplier=0,
                          allow_small_or_imprecise_dtypes=True).then_inc(iota_done, 1)

            @block.tensor
            def _(pe):
                pe.wait_ge(lens_ready, 1)
                pe.matmul(ps[0:NW, 0, 0:1], k.tri[0:NW, 0:NW], tl[:, 6:7], start=True, stop=True)\
                    .then_inc(before_ready, 1)

            @block.vector
            def _(v):
                v.wait_ge(edges_in, 64)
                v.tensor_reduce(mm[:, 0, :], dr[:, :, :], AX.X, ALU.min).then_inc(minmax_ready, 1)
                v.tensor_reduce(mm[:, 1, :], dr[:, :, :], AX.X, ALU.max).then_inc(minmax_ready, 1)
                s = Steps(v, steps)
                s.did(v.memset(dF[:, ET:ETP], -1.0))
                s.did(v.memset(sF[:, ET:ETP], 0.0))
                s.did(v.memset(tf[:, 3:4], 0))
                s.did(v.memset(wp[:, :, :], 0.0))
                s.wait()
                s.did(v.memset(wp[:, 0:ET, 0:1], 1.0))
                s.did(v.tensor_copy(sF[:, 0:ET], ei[:, 0, :]))
                s.did(v.tensor_copy(dF[:, 0:ET], ei[:, 1, :]))
                s.did(v.tensor_copy(wp[:, 0:ET, 1], wF[:, 0, :]))
                s.wait()
                s.did(v.tensor_tensor(wF[:, 1, :], wF[:, 0, :], wp[:, 0:ET, 1], ALU.subtract))
                s.wait()
                s.did(v.tensor_copy(wp[:, 0:ET, 2], wF[:, 1, :]))
                s.wait()
                s.did(v.tensor_tensor(wF[:, 2, :], wF[:, 1, :], wp[:, 0:ET, 2], ALU.subtract))
                s.wait()
                s.did(v.tensor_copy(wp[:, 0:ET, 3], wF[:, 2, :]))
                v.wait_ge(iota_done, 2)
                s.did(v.memset(io16[:, N:], 2000.0))
                s.did(v.tensor_copy(io16[:, 0:N], ioi[:, :]))
                v.wait_ge(minmax_in, 32)
                v.wait_ge(consts_in, 32)
                s.did(v.tensor_scalar(ov[:, 0, :], mb[:, 0, :], tl[:, 1:2], None, ALU.is_le))
                s.wait()
                s.did(v.scalar_tensor_tensor(ov[:, 1, :], mb[:, 1, :], tl[:, 0:1], ov[:, 0, :],
                                             ALU.is_ge, ALU.mult))
                s.wait()
                s.did(v.scalar_tensor_tensor(ov[:, 2, :], ov[:, 1, :], -1000.0, iot[:, :], ALU.mult, ALU.add))
                s.did(v.scalar_tensor_tensor(ov[:, 0, :], iot[:, :], 1.0, ov[:, 1, :], ALU.add, ALU.mult))
                s.wait()
                s.did(v.tensor_reduce(tl[:, 2:3], ov[:, 2, :], AX.X, ALU.min))
                s.did(v.tensor_reduce(tl[:, 3:4], ov[:, 0, :], AX.X, ALU.max))
                s.wait()
                s.did(v.tensor_scalar(tl[:, 4:5], tl[:, 2:3], 1000.0, float(ET - 1), ALU.add, ALU.min))
                s.wait()
                s.did(v.tensor_tensor(tl[:, 5:6], tl[:, 3:4], tl[:, 4:5], ALU.subtract))
                s.wait()
                s.did(v.tensor_scalar(ti[:, 0:1], tl[:, 5:6], 1.0, None, ALU.max))
                s.wait()
                s.did(v.tensor_scalar(ti[:, 1:2], ti[:, 0:1], 1, None, ALU.arith_shift_right))
                s.wait()
                v.tensor_scalar(tf[:, 1:2], ti[:, 1:2], 1.0, None, ALU.max).then_inc(table_ready, 1)
                v.tensor_copy(tf[:, 0:1], tl[:, 4:5]).then_inc(table_ready, 1)
                v.wait_ge(table_ready, 2)
                v.tensor_scalar(tl[:, 6:7], tf[:, 1:2], 2.0, 1.0, ALU.mult, ALU.add).then_inc(lens_ready, 1)
                v.wait_ge(before_ready, 1)
                v.tensor_copy(tf[:, 2:3], ps[0:NW, 0, 0:1]).then_inc(table_ready, 1)
                v.wait_ge(table_ready, 3)
                s.did(v.tensor_scalar(ti[:, 2:3], tf[:, 2:3], 17, None, ALU.logical_shift_left))
                s.did(v.tensor_scalar(ti[:, 3:4], tf[:, 0:1], 8, None, ALU.logical_shift_left))
                s.wait()
                s.did(v.tensor_tensor(ti[:, 2:3], ti[:, 2:3], ti[:, 3:4], ALU.bitwise_or))
                s.wait()
                v.tensor_tensor(tf[:, 3:4], ti[:, 2:3], tf[:, 1:2], ALU.bitwise_or).then_inc(table_ready, 1)

        onehots_ready, onehots_used = sem("onehots_ready"), sem("onehots_used")
        window_summed, window_staged = sem("window_summed"), sem("window_staged")
        parts_added, parts_out = sem("parts_added"), sem("parts_out")
        SPLIT = ((0, 5), (5, 5))

        def window(eng, w):
            entry = eng.snap(eng.value_load(tab[0:1, bass.ds(w * 4 + 3, 1)], min_val=0, max_val=2 ** 31 - 1))
            known = "a window's entry holds numbers in these ranges"
            return (nc.s_assert_within(eng.snap((entry >> 8) & 511), 0, ET - 1,
                                       skip_runtime_bounds_check_because=known),
                    nc.s_assert_within(eng.snap(entry & 255), 1, ET // 2, skip_runtime_bounds_check_because=known),
                    nc.s_assert_within(eng.snap(entry >> 17), 0, NW * (ET + 1),
                                       skip_runtime_bounds_check_because=known))

        with nc.Block() as block:
            @block.sync
            def _(sp):
                beside(sp)

            @block.vector
            def _(v):
                def onehots(tile, nth, base):
                    slot = bass.ds(nth % SLOTS, 1)
                    tile = nc.s_assert_within(tile, 0, ETP - 1, skip_runtime_bounds_check_because="a pair starts at tile ET at the latest")
                    v.wait_ge(onehots_used, nth + 1)
                    v.tensor_scalar(ohs[:, slot, :].rearrange("p o n -> p (o n)"), io16[:, 0:N], sF[:, bass.ds(tile, 1)], None, ALU.is_equal)
                    v.scalar_tensor_tensor(
                        ohd[:, slot, :].rearrange("p o (a b) -> p (o a) b", a=4),
                        io16[:, bass.ds(base, WIN)].unsqueeze(1).broadcast_to([P, 4, WIN]),
                        dF[:, bass.ds(tile, 1)],
                        wp[:, bass.ds(tile, 1), :].rearrange("p o f -> p (o f)").unsqueeze(2).broadcast_to([P, 4, WIN]),
                        ALU.is_equal, ALU.mult).then_inc(onehots_ready, 1)

                with v.Fori(0, T) as i:
                    for j in range(WPT):
                        first, pairs, before = window(v, i * WPT + j)
                        base = i * P + j * WIN
                        onehots(first, before, base)
                        with v.Fori(0, pairs) as q:
                            for h in range(2):
                                onehots(first + 2 * q + 1 + h, before + 2 * q + 1 + h, base)

            @block.tensor
            def _(pe):
                pe.sem_inc(onehots_used, SLOTS)

                def add_tile(half, nth, start):
                    slot = bass.ds(nth % SLOTS, 1)
                    pe.wait_ge(onehots_ready, nth + 1)
                    for c, (c0, cn) in enumerate(CH):
                        mm_ = pe.matmul(ps[:, 3 * half + c, 0:cn], ohd[:, slot, :].rearrange("p o n -> p (o n)"),
                                        ohs[:, slot, c0:c0 + cn].rearrange("p o n -> p (o n)"), start=start, stop=True, skip_group_check=True)
                    mm_.then_inc(onehots_used, 1)

                def add_parts(i, j):
                    w = i * WPT + j
                    pe.wait_ge(window_staged, w + 3)
                    pe.wait_ge(parts_out, w * 4 + 4)
                    for b, (s0, sn) in enumerate(SPLIT):
                        for s_ in range(sn):
                            t = s0 + s_
                            mm_ = pe.matmul(ps[0:P, 6 + b, 64 * s_:64 * s_ + 64],
                                            stage[:, j % 2, P * t:P * t + P], sel[:, :], start=True, stop=True,
                                            skip_group_check=True)
                    mm_.then_inc(parts_added, 1)

                with pe.Fori(0, T) as i:
                    for j in range(WPT):
                        w = i * WPT + j
                        first, pairs, before = window(pe, w)
                        pe.wait_ge(window_staged, w + 1)
                        add_tile(j % 2, before, True)
                        with pe.Fori(0, pairs) as q:
                            for h in range(2):
                                add_tile(j % 2, before + 2 * q + 1 + h, False)
                        pe.drain().then_inc(window_summed, 1)
                        if j:
                            add_parts(i, j - 1)
                    add_parts(i, WPT - 1)

            @block.scalar
            def _(act):
                act.sem_inc(window_staged, 2)
                act.sem_inc(parts_out, 4)

                def stage_window(i, j):
                    act.wait_ge(window_summed, i * WPT + j + 1)
                    h = j % 2
                    act.activation(stage[:, h, 0:1000].rearrange("p (c n) -> p c n", c=2),
                                   ps[:, 3 * h:3 * h + 2, 0:500], ACT.Copy)
                    act.activation(stage[:, h, 1000:N], ps[:, 3 * h + 2, 0:250], ACT.Copy).then_inc(window_staged, 1)

                def parts_to_columns(i, j):
                    act.wait_ge(parts_added, i * WPT + j + 1)
                    n = min(WIN, P - j * WIN)
                    for b, (s0, sn) in enumerate(SPLIT):
                        for half, mat in enumerate((CT, WT)):
                            act.activation(mat[:, s0:s0 + sn, bass.ds(i * P + j * WIN, n)],
                                           ps[0:P, 6 + b, 0:64 * sn].rearrange("p (s n) -> p s n", n=64)
                                           [:, :, WIN * half:WIN * half + n], ACT.Copy).then_inc(parts_out, 1)

                with act.Fori(0, T) as i:
                    for j in range(WPT):
                        stage_window(i, j)
                        if j:
                            parts_to_columns(i, j - 1)
                    parts_to_columns(i, WPT - 1)
class Kit:

    def __init__(self):
        self.names = 0
        self.used_semaphores = []
        self.lasting = None

    def name(self, base):
        self.names += 1
        return f"{base}_{self.names}"


    def gpsimd_dma_semaphore(self, nc, name):
        return self.lasting.enter_context(nc.semaphore(self.name(name)))

    @contextmanager
    def semaphore(self, nc, name):
        with nc.semaphore(name) as s:
            yield s
        self.used_semaphores.append(s)

    def clear_semaphores(self, nc):
        todo, self.used_semaphores = self.used_semaphores, []
        with nc.Block() as block:
            @block.gpsimd
            def _(pool):
                for s in todo:
                    pool.sem_clear(s)
def norm_rows(nc, k, x, xn, xT=None, affine=None, eps=1e-5):
    with ExitStack() as ctx:
        def sb(name, shape, dt=fp32):
            return ctx.enter_context(nc.sbuf_tensor(k.name(name), shape, dt))

        def sem(name):
            return ctx.enter_context(k.semaphore(nc, k.name(name)))

        st = sb("bn_parts", [P, T, 6])
        mv = sb("mean_var", [P, T, 2])
        sd = sb("std", [P, T])
        rs = sb("rstd", [P, T])
        stats, var_ready, std_ready, inv_ready = sem("stats"), sem("var_ready"), sem("std_ready"), sem("inv_ready")
        rows_ready, transposed, copied = sem("rows_ready"), sem("transposed"), sem("copied")
        with nc.Block() as block:
            @block.vector
            def _(v):
                with v.Fori(0, T) as i:
                    v.bn_stats(st[:, bass.ds(i, 1), :].rearrange("p o n -> p (o n)"),
                               x[:, bass.ds(i, 1), :].rearrange("p o n -> p (o n)")).then_inc(stats, 1)
                v.wait_ge(stats, T)
                for i in range(T):
                    v.bn_aggr(mv[:, i, :], st[:, i, :]).then_inc(stats, 1)
                v.wait_ge(stats, 2 * T)
                v.tensor_scalar(sd[:, :], mv[:, :, 1], eps, None, ALU.add).then_inc(var_ready, 1)
                v.wait_ge(std_ready, 1)
                v.reciprocal(rs[:, :], sd[:, :]).then_inc(inv_ready, 1)
                v.wait_ge(inv_ready, 1)
                with v.Fori(0, T) as i:
                    v.tensor_scalar(xn[:, bass.ds(i, 1), :].rearrange("p o n -> p (o n)"),
                                    x[:, bass.ds(i, 1), :].rearrange("p o n -> p (o n)"),
                                    mv[:, bass.ds(i, 1), 0:1].rearrange("p o n -> p (o n)"), rs[:, bass.ds(i, 1)],
                                    ALU.subtract, ALU.mult).then_inc(rows_ready, 1)

            @block.scalar
            def _(act):
                act.wait_ge(var_ready, 1)
                act.activation(sd[:, :], sd[:, :], ACT.Sqrt).then_inc(std_ready, 1)
                if xT is not None:
                    copy_transposed(act, k, xT, transposed, copied, affine)

            if xT is not None:
                @block.tensor
                def _(pe):
                    transpose_rows(pe, k, xn, transposed, copied, rows_ready)


def transpose_rows(pe, k, xn, transposed, copied, rows_ready=None):
    g = 0
    for c0, cn in CH:
        if rows_ready is not None:
            pe.wait_ge(rows_ready, (c0 + cn) // P)
        for c in range(C):
            if g >= 8:
                pe.wait_ge(copied, g - 7)
            for t in range(c0 // P, (c0 + cn) // P):
                mm = pe.transpose(k.ps[:, g % 8, P * t - c0:P * t - c0 + P], xn[:, t, 128 * c:128 * c + 128],
                                  k.ident[0:P, 0:P])
            mm.then_inc(transposed, 1)
            g += 1


def copy_transposed(act, k, xT, transposed, copied, affine=None):
    g = 0
    for c0, cn in CH:
        for c in range(C):
            act.wait_ge(transposed, g + 1)
            if affine is None:
                act.activation(xT[:, c, c0:c0 + cn], k.ps[:, g % 8, 0:cn], ACT.Copy).then_inc(copied, 1)
            else:
                act.activation(xT[:, c, c0:c0 + cn], k.ps[:, g % 8, 0:cn], ACT.Identity,
                               bias=affine[1][:, c:c + 1], scale=affine[0][:, c:c + 1]).then_inc(copied, 1)
            g += 1


def transpose_only(nc, k, xn, xT):
    with k.semaphore(nc, k.name("transposed")) as transposed, k.semaphore(nc, k.name("copied")) as copied:
        with nc.Block() as block:
            @block.tensor
            def _(pe):
                transpose_rows(pe, k, xn, transposed, copied)

            @block.scalar
            def _(act):
                copy_transposed(act, k, xT, transposed, copied)


def load(nc, k, pairs):
    with k.semaphore(nc, k.name("loaded")) as loaded:
        with nc.Block() as block:
            @block.sync
            def _(sp):
                for dst, src in pairs:
                    sp.dma_start(dst, src).then_inc(loaded, 16)
                sp.wait_ge(loaded, 16 * len(pairs))


def rows_product(nc, k, terms, bias, finish):
    (engine, take), = finish.items()
    with k.semaphore(nc, k.name("summed")) as summed, k.semaphore(nc, k.name("taken")) as taken:
        with nc.Block() as block:
            @block.tensor
            def _(pe):
                for i in range(T):
                    if i >= 8:
                        pe.wait_ge(taken, i - 7)
                    todo = [(lhsT[:, c, P * i:P * i + P], rhs[:, c, :]) for lhsT, rhs, n in terms for c in range(n)]
                    if bias is not None:
                        todo.append((k.ones[0:1, 0:P], bias))
                    for n, (l, r) in enumerate(todo):
                        mm = pe.matmul(k.ps[0:P, i % 8, :], l, r, start=(n == 0), stop=(n == len(todo) - 1))
                    mm.then_inc(summed, 1)

            def takes(eng):
                for i in range(T):
                    eng.wait_ge(summed, i + 1)
                    take(eng, i, k.ps[0:P, i % 8, :]).then_inc(taken, 1)

            if engine == "scalar":
                block.scalar(takes)
            else:
                block.vector(takes)


def columns_product(nc, k, lhsT, rhs, chunks, mchunks, take, reuse=None):
    with k.semaphore(nc, k.name("summed")) as summed, k.semaphore(nc, k.name("taken")) as taken:
        with nc.Block() as block:
            @block.tensor
            def _(pe):
                g = 0
                for m in range(mchunks):
                    for c0, cn in CH:
                        if g >= 8:
                            pe.wait_ge(taken, g - 7)
                        for c in range(chunks):
                            mm = pe.matmul(k.ps[:, g % 8, 0:cn], lhsT[:, c, 128 * m:128 * m + 128],
                                           rhs[:, c, c0:c0 + cn], start=(c == 0), stop=(c == chunks - 1))
                        mm.then_inc(summed, 1)
                        g += 1

            @block.scalar
            def _(act):
                g = 0
                for m in range(mchunks):
                    for n, (c0, cn) in enumerate(CH):
                        if reuse is not None and g >= reuse:
                            act.wait_ge(taken, g - reuse + 1)
                        act.wait_ge(summed, g + 1)
                        take(act, m, (c0, cn), n, k.ps[:, g % 8, 0:cn]).then_inc(taken, 1)
                        g += 1


def copy_rows(out, func=None):
    return {"scalar": lambda act, i, psum: act.activation(out[:, i, :], psum, func or ACT.Copy)}


def add_rows(out, base=None):
    return {"vector": lambda v, i, psum: v.tensor_tensor(out[:, i, :], (out if base is None else base)[:, i, :],
                                                         psum, ALU.add)}


def add_into(nc, k, x, y):
    with k.semaphore(nc, k.name("added")) as added:
        with nc.Block() as block:
            @block.vector
            def _(v):
                v.tensor_tensor(x[:, :, :], x[:, :, :], y[:, :, :], ALU.add).then_inc(added, 1)


def split(nc, k, pairs):
    with k.semaphore(nc, k.name("hi")) as hi_done:
        with nc.Block() as block:
            @block.scalar
            def _(act):
                for x, hi, lo in pairs:
                    for c in range(x.shape[1]):
                        act.activation(hi[:, c, :], x[:, c, :], ACT.Copy).then_inc(hi_done, 1)

            @block.vector
            def _(v):
                n = 0
                for x, hi, lo in pairs:
                    for c in range(x.shape[1]):
                        n += 1
                        v.wait_ge(hi_done, n)
                        v.tensor_tensor(lo[:, c, :], x[:, c, :], hi[:, c, :].bitcast(fp32), ALU.subtract)


def three_terms(l, r, chunks):
    return [(l[0], r[0], chunks), (l[0], r[1], chunks), (l[1], r[0], chunks)]


def values(nc, k, x1, w_v, b_v, V):
    with ExitStack() as ctx:
        def sb(name, shape, dt=fp32):
            return ctx.enter_context(nc.sbuf_tensor(k.name(name), shape, dt))
        wraw = sb("wv_raw", [128, C, D])
        wp = sb("wv_hi", [128, C, D], f32r), sb("wv_lo", [128, C, D], f32r)
        terms, loads, parts = three_terms(x1, wp, C), [(wraw[:, :, :], kchunks(w_v))], [(wraw, *wp)]
        if b_v is not None:
            braw = sb("bv_raw", [1, 1, D])
            bp = sb("bv_hi", [1, 1, D], f32r), sb("bv_lo", [1, 1, D], f32r)
            one = sb("one_v", [1, 1, N], f32r)
            terms += [(one, bp[0], 1), (one, bp[1], 1)]
            loads.append((braw[:, 0, :], row(b_v)))
            parts.append((braw, *bp))
        load(nc, k, loads)
        split(nc, k, parts)
        if b_v is not None:
            with nc.Block() as block:
                @block.vector
                def _(v):
                    v.memset(one[:, :, :].bitcast(fp32), 1.0)
        rows_product(nc, k, terms, None, copy_rows(V))


def attention(nc, k, x1, w_qk, b_qk, w_v, b_v, ctxT, room):
    H, DH = 8, 64
    HALF, PIECE = 5, 250
    SCALE = DH ** -0.5
    with ExitStack() as ctx:
        def sb(name, shape, dt=fp32):
            return ctx.enter_context(nc.sbuf_tensor(k.name(name), shape, dt))

        def sem(name):
            return ctx.enter_context(k.semaphore(nc, k.name(name)))

        def pair(name, shape):
            return sb(name + "_hi", shape, f32r), sb(name + "_lo", shape, f32r)

        Vall = room(P, (T, D))
        values(nc, k, x1, w_v, b_v, Vall)
        wraw = room(128, (C, 128))
        wph, wpl = pair("w", [128, C, 128])
        braw = sb("b_raw", [1, 128])
        bh, bl = pair("b", [1, 128])
        one = sb("one_r", [1, 500], f32r)
        QT, KT = pair("QT", [DH + 1, 2, N]), pair("KT", [DH + 1, 2, N])
        V = sb("V", [P, T, 128])
        PT = sb("probs", [P, 2, N])
        cu = room(128, (N,))
        inv = room(DH, (2, PIECE))
        mx, mr, negm = sb("mx", [P, T, 3]), sb("mr", [P, T]), sb("negm", [P, T])
        w_in, w_hi, w_split, ones_set = sem("w_in"), sem("w_hi"), sem("w_split"), sem("ones_set")
        proj_done, v_in, s_done, row_done = sem("proj_done"), sem("v_in"), sem("s_done"), sem("row_done")
        st_done, pv_done, qk_hi, row_hi = (sem(n) for n in ("st_done", "pv_done", "qk_hi", "row_hi"))
        s_out, p_out, qk_lo, ctx_out = (sem(n) for n in ("s_out", "p_out", "qk_lo", "ctx_out"))
        row_lo, negm_ready, inv_ready, norm_out = (sem(n) for n in ("row_lo", "negm_ready", "inv_ready",
                                                                    "norm_out"))
        max_steps = sem("max_steps")
        ps = k.ps
        ACC, ST, SQ = 0, 3, 6
        ROW = [ps[DH:DH + 1, SQ, 0:500], ps[DH:DH + 1, SQ + 1, 0:500], ps[0:1, SQ, 0:250]]
        bias = b_qk is not None
        LOADS = 32 if bias else 16

        def three(pe, out, l, r, start, stop):
            pe.matmul(out, l[0], r[0], start=start, stop=False)
            pe.matmul(out, l[0], r[1], start=False, stop=False)
            return pe.matmul(out, l[1], r[0], start=False, stop=stop)

        def schedule(eng, tiles, between):
            first, second = range(HALF), range(HALF, T)
            tiles(0, 0, first, True, True)
            with eng.Fori(0, H // 2 - 1) as i:
                for j in range(2):
                    tiles(i * 2 + j, j, second, True, True)
                    between(i * 2 + j, j, bass.ds(i, 1), True, True)
                    tiles(i * 2 + (j + 1), 1 - j, first, True, True)
            tiles(H - 2, 0, second, True, False)
            between(H - 2, 0, slice(H // 2 - 1, H // 2), True, False)
            tiles(H - 1, 1, first, False, False)
            tiles(H - 1, 1, second, False, False)
            between(H - 1, 1, slice(H // 2 - 1, H // 2), False, False)

        with nc.Block() as block:
            @block.sync
            def _(sp):
                def load_weights(h, wait):
                    sp.wait_ge(w_split, wait)
                    sp.dma_start(wraw[:, :, :], w_qk[bass.ds(h, 1)].rearrange("o p c n -> p (o c) n"))\
                        .then_inc(w_in, 16)
                    if bias:
                        sp.dma_start(braw[:, :], b_qk[bass.ds(h, 1), :]).then_inc(w_in, 16)
                load_weights(0, 1)
                with sp.Fori(1, H) as h:
                    load_weights(h, h + 1)

            @block.tensor
            def _(pe):
                pe.sem_inc(pv_done, 1)
                pe.wait_ge(ones_set, 4)

                def project(h):
                    pe.wait_ge(w_split, h + 2)
                    for n, (c0, cn) in enumerate(CH):
                        o = ps[:, ST + n, 0:cn]
                        for c in range(C):
                            mm = three(pe, o, (wph[:, c, :], wpl[:, c, :]), [x[:, c, c0:c0 + cn] for x in x1],
                                       c == 0, c == C - 1 and not bias)
                        if bias:
                            pe.matmul(o, bh[:, :], one[0:1, 0:cn], start=False, stop=False)
                            mm = pe.matmul(o, bl[:, :], one[0:1, 0:cn], start=False, stop=True)
                        mm.then_inc(proj_done, 1)

                def score(h, j, cc):
                    t, (c0, cn) = cc // 3, CH[cc % 3]
                    if cc >= 2:
                        pe.wait_ge(s_out, h * 30 + (cc - 1))
                    pe.matmul(ps[0:P, SQ + cc % 2, 0:cn], QT[0][0:DH, j, P * t:P * t + P],
                              KT[0][0:DH, j, c0:c0 + cn], start=True, stop=True).then_inc(s_done, 1)

                def score_t(h, j, t, n):
                    c0, cn = CH[n]
                    if t >= 1:
                        pe.wait_ge(p_out, h * 30 + (3 * t + n - 2))
                    three(pe, ps[0:P, ST + n, 0:cn], [x[:, j, P * t:P * t + P] for x in KT],
                          [x[:, j, c0:c0 + cn] for x in QT], True, True).then_inc(st_done, 1)

                def times_v(h, t, n):
                    c0, cn = CH[n]
                    if n == 0:
                        pe.wait_ge(p_out, h * 30 + (3 * t + 3))
                    mm = pe.matmul(ps[:, ACC + n, 0:cn], V[:, t, :], PT[:, t % 2, c0:c0 + cn],
                                   start=(t == 0), stop=(t == T - 1))
                    if n == 2:
                        mm.then_inc(pv_done, 1)

                def minus_max(h):
                    pe.wait_ge(negm_ready, h + 1)
                    for n, (c0, cn) in enumerate(CH):
                        for t in range(c0 // P, (c0 + cn) // P):
                            mm = pe.matmul(ROW[n][:, P * t - c0:P * t - c0 + P], negm[:, t:t + 1],
                                           k.ident[0:P, 0:P], start=True, stop=True)
                        mm.then_inc(row_done, 1)

                def tiles(h, j, those, has_next, has_second):
                    for t in those:
                        if t == 0:
                            ready = h * 6 + 12 if has_next else H * 6
                            pe.wait_ge(qk_hi, ready)
                            pe.wait_ge(qk_lo, ready)
                            pe.wait_ge(row_hi, h * 3 + 3)
                            pe.wait_ge(row_lo, h * 3 + 3)
                        for n in range(3):
                            score_t(h, j, t, n)
                            if has_next and n < 2:
                                score(h + 1, 1 - j, 3 * t + n)
                        if t == 1:
                            pe.wait_ge(ctx_out, h * 3 + 1)
                            pe.wait_ge(v_in, h + 1)
                        for n in range(3):
                            if t:
                                times_v(h, t - 1, n)
                            if has_next and n == 0:
                                score(h + 1, 1 - j, 3 * t + 2)

                def between(h, j, chunk, has_next, has_second):
                    for n in range(3):
                        times_v(h, T - 1, n)
                    if has_next:
                        minus_max(h + 1)
                    if has_second:
                        project(h + 2)

                project(0)
                pe.wait_ge(qk_hi, 6)
                pe.wait_ge(qk_lo, 6)
                project(1)
                for cc in range(3 * T):
                    score(0, 0, cc)
                minus_max(0)
                schedule(pe, tiles, between)

            @block.scalar
            def _(act):
                act.sem_inc(ctx_out, 1)

                def split_hi(h, through):
                    if through is not None:
                        act.wait_ge(proj_done, through)
                    act.wait_ge(w_in, h * LOADS + LOADS)
                    act.activation(wph[:, :, :], wraw[:, :, :], ACT.Copy).then_inc(w_hi, 1)
                    if bias:
                        act.activation(bh[:, :], braw[:, :], ACT.Copy).then_inc(w_hi, 1)

                def take_projections(h, j):
                    for n, (c0, cn) in enumerate(CH):
                        act.wait_ge(proj_done, h * 3 + (n + 1))
                        act.activation(QT[0][0:DH, j, c0:c0 + cn], ps[0:DH, ST + n, 0:cn], ACT.Copy)\
                            .then_inc(qk_hi, 1)
                        act.activation(KT[0][0:DH, j, c0:c0 + cn], ps[DH:128, ST + n, 0:cn], ACT.Copy)\
                            .then_inc(qk_hi, 1)

                def take_row(h, j):
                    for n, (c0, cn) in enumerate(CH):
                        act.wait_ge(row_done, h * 3 + (n + 1))
                        act.activation(QT[0][DH:DH + 1, j, c0:c0 + cn], ROW[n], ACT.Copy).then_inc(row_hi, 1)

                def tiles(h, j, those, has_next, has_second):
                    for t in those:
                        act.wait_ge(pv_done, h * T + (max(t - 1, 0) + 1))
                        for n, (c0, cn) in enumerate(CH):
                            act.wait_ge(st_done, h * 30 + (3 * t + n + 1))
                            act.activation(PT[:, t % 2, c0:c0 + cn], ps[0:P, ST + n, 0:cn], ACT.Exp,
                                           scale=SCALE).then_inc(p_out, 1)
                        if t == HALF and has_second:
                            split_hi(h + 2, h * 3 + 6)

                def between(h, j, chunk, has_next, has_second):
                    act.wait_ge(norm_out, h * HALF + 1)
                    act.wait_ge(pv_done, h * T + (T + 1))
                    for n, (c0, cn) in enumerate(CH):
                        act.activation(cu[:, c0:c0 + cn], ps[:, ACC + n, 0:cn], ACT.Copy).then_inc(ctx_out, 1)
                    if has_next:
                        take_row(h + 1, 1 - j)
                    if has_second:
                        take_projections(h + 2, j)

                for h in range(2):
                    split_hi(h, 3 if h else None)
                    take_projections(h, h)
                take_row(0, 0)
                schedule(act, tiles, between)

            @block.vector
            def _(v):
                v.sem_inc(w_split, 1)
                v.sem_inc(norm_out, 1)
                v.memset(KT[0][DH:DH + 1, :, :].bitcast(fp32), 1.0).then_inc(ones_set, 1)
                v.memset(KT[1][DH:DH + 1, :, :].bitcast(fp32), 0.0).then_inc(ones_set, 1)
                v.memset(V[:, :, DH:128], 1.0).then_inc(ones_set, 1)
                v.memset(one[:, :].bitcast(fp32), 1.0).then_inc(ones_set, 1)

                def take_projections(h, j):
                    for n, (c0, cn) in enumerate(CH):
                        v.wait_ge(qk_hi, h * 6 + (2 * n + 2))
                        v.tensor_tensor(QT[1][0:DH, j, c0:c0 + cn], ps[0:DH, ST + n, 0:cn],
                                        QT[0][0:DH, j, c0:c0 + cn].bitcast(fp32), ALU.subtract).then_inc(qk_lo, 1)
                        v.tensor_tensor(KT[1][0:DH, j, c0:c0 + cn], ps[DH:128, ST + n, 0:cn],
                                        KT[0][0:DH, j, c0:c0 + cn].bitcast(fp32), ALU.subtract).then_inc(qk_lo, 1)

                def split_lo(h):
                    parts = 2 if bias else 1
                    v.wait_ge(w_hi, h * parts + parts)
                    if bias:
                        v.tensor_tensor(bl[:, :], braw[:, :], bh[:, :].bitcast(fp32), ALU.subtract)
                    v.tensor_tensor(wpl[:, :, :], wraw[:, :, :], wph[:, :, :].bitcast(fp32), ALU.subtract)\
                        .then_inc(w_split, 1)

                def take_v(h):
                    v.tensor_copy(V[:, :, 0:DH], Vall[:, :, bass.ds(h * DH, DH)]).then_inc(v_in, 1)

                def maxima(h, t):
                    for n, (c0, cn) in enumerate(CH):
                        cc = 3 * t + n
                        v.wait_ge(s_done, h * 30 + (cc + 1))
                        v.tensor_reduce(mx[:, t, n:n + 1], ps[0:P, SQ + cc % 2, 0:cn], AX.X, ALU.max)\
                            .then_inc(s_out, 1)

                def negate(h):
                    v.wait_ge(s_out, h * 30 + 30)
                    v.tensor_reduce(mr[:, :], mx[:, :, :], AX.X, ALU.max).then_inc(max_steps, 1)
                    v.wait_ge(max_steps, h + 1)
                    v.tensor_scalar(negm[:, :], mr[:, :], -1.0, None, ALU.mult).then_inc(negm_ready, 1)

                def take_row(h, j):
                    for n, (c0, cn) in enumerate(CH):
                        v.wait_ge(row_hi, h * 3 + (n + 1))
                        v.tensor_tensor(QT[1][DH:DH + 1, j, c0:c0 + cn], ROW[n],
                                        QT[0][DH:DH + 1, j, c0:c0 + cn].bitcast(fp32), ALU.subtract)\
                            .then_inc(row_lo, 1)

                def finish(h, j, chunk, m):
                    if m == 0:
                        v.wait_ge(ctx_out, h * 3 + 4)
                    c0 = PIECE * m
                    v.reciprocal(inv[:, m % 2, :], cu[DH:128, c0:c0 + PIECE]).then_inc(inv_ready, 1)
                    v.wait_ge(inv_ready, h * HALF + (m + 1))
                    v.tensor_tensor(ctxT[DH * j:DH * j + DH, chunk, c0:c0 + PIECE].rearrange("p o n -> p (o n)"),
                                    cu[0:DH, c0:c0 + PIECE], inv[:, m % 2, :], ALU.mult).then_inc(norm_out, 1)

                last = []

                def tiles(h, j, those, has_next, has_second):
                    for t in those:
                        if has_next:
                            maxima(h + 1, t)
                        if last and t < HALF:
                            finish(*last[0], t)
                        if t == HALF and has_second:
                            split_lo(h + 2)

                def between(h, j, chunk, has_next, has_second):
                    if has_next:
                        negate(h + 1)
                        v.wait_ge(pv_done, h * T + (T + 1))
                        take_v(h + 1)
                        take_row(h + 1, 1 - j)
                    if has_second:
                        take_projections(h + 2, j)
                    last[:] = [(h, j, chunk)]

                take_v(0)
                for h in range(2):
                    split_lo(h)
                    take_projections(h, h)
                for t in range(T):
                    maxima(0, t)
                negate(0)
                take_row(0, 0)
                schedule(v, tiles, between)
                for m in range(HALF):
                    finish(*last[0], m)
def route(nc, k, yT, wr, br, E_, topk, cap, keep_last, r):
    with ExitStack() as ctx:
        def sb(name, shape, dt=fp32):
            return ctx.enter_context(nc.sbuf_tensor(k.name(name), shape, dt))

        def sem(name):
            return ctx.enter_context(k.semaphore(nc, k.name(name)))

        L = sb("logits", [P, T, E_])
        W = sb("work", [P, T, E_])
        PR = sb("probs", [P, T, E_])
        OH = sb("onehot", [P, 2, T, E_])
        M16 = sb("mask16", [P, T, E_], bf16)
        POS = sb("pos", [P, T, E_])
        G = sb("gates_by_expert", [P, T, E_])
        m1 = sb("m1", [P, T])
        top = sb("top", [P, T, 8])
        idx = sb("idx", [P, T, 8], u32)
        ix = sb("ix", [P, 2, T])
        pk = sb("pk", [P, 2, T])
        keep = sb("keep", [P, 2, T])
        tmp = sb("tmp", [P, 4, T])
        spare = sb("spare", [P, 2, T])
        ioE = sb("iota_e", [P, E_])
        cnt = sb("cnt", [P, E_])
        cnti = sb("cnt_i", [P, 2, E_], i32)
        blk = sb("blk", [P, 3, E_])
        ps = k.ps
        iotas, logit_done, logit_out = sem("iotas"), sem("logit_done"), sem("logit_out")
        steps, shifted, exps, masks = sem("route_steps"), sem("shifted"), sem("exps"), sem("masks")
        pos_done, gates_ready, gT_done, gT_out = sem("pos_done"), sem("gates_ready"), sem("gT_done"), sem("gT_out")
        PB = T // 2

        def two(bank):
            return [(ps[0:P, bank + b, 0:PB * E_].rearrange("p (t e) -> p t e", e=E_), slice(PB * b, PB * b + PB))
                    for b in range(2)]

        def over_e(ap):
            return ap.unsqueeze(2).broadcast_to([P, T, E_])

        with nc.Block() as block:
            @block.gpsimd
            def _(pool):
                pool.iota(ioE[:, :], [[1, E_]], base=0, channel_multiplier=0,
                          allow_small_or_imprecise_dtypes=True).then_inc(iotas, 1)
                for c in range(topk):
                    pool.iota(spare[:, c, :], [[topk * P, T]], base=c + r.spare0, channel_multiplier=topk,
                              allow_small_or_imprecise_dtypes=True).then_inc(iotas, 1)

            @block.tensor
            def _(pe):
                for t in range(T):
                    o = ps[0:P, t // PB, E_ * (t % PB):E_ * (t % PB) + E_]
                    for c in range(C):
                        mm = pe.matmul(o, yT[:, c, P * t:P * t + P], wr[:, c, :], start=(c == 0),
                                       stop=(c == C - 1 and br is None))
                    if br is not None:
                        mm = pe.matmul(o, k.ones[0:1, 0:P], br, start=False, stop=True)
                mm.then_inc(logit_done, 1)
                pe.wait_ge(masks, 1)
                for t in range(T):
                    o = ps[0:P, 2 + t // PB, E_ * (t % PB):E_ * (t % PB) + E_]
                    for u in range(t):
                        pe.matmul(o, k.ones16[0:P, 0:P], M16[:, u, :], start=(u == 0), stop=False)
                    mm = pe.matmul(o, k.tri16[0:P, 0:P], M16[:, t, :], start=(t == 0), stop=True)
                if cap is None:
                    for u in range(T):
                        mm = pe.matmul(ps[0:P, 4, 0:E_], k.ones16[0:P, 0:P], M16[:, u, :], start=(u == 0),
                                       stop=(u == T - 1))
                mm.then_inc(pos_done, 1)
                pe.wait_ge(gates_ready, 1)
                for n, (c0, cn) in enumerate(CH):
                    for t in range(c0 // P, (c0 + cn) // P):
                        mm = pe.transpose(ps[0:E_, 5 + n, P * t - c0:P * t - c0 + P], G[:, t, :], k.ident[0:P, 0:P])
                mm.then_inc(gT_done, 1)

            @block.scalar
            def _(act):
                act.wait_ge(shifted, 1)
                act.activation(W[:, :, :], L[:, :, :], ACT.Exp).then_inc(exps, 1)
                act.wait_ge(gT_done, 1)
                for n, (c0, cn) in enumerate(CH):
                    act.activation(r.gateT[:, c0:c0 + cn], ps[0:E_, 5 + n, 0:cn], ACT.Copy).then_inc(gT_out, 1)

            @block.vector
            def _(v):
                s = Steps(v, steps)
                v.wait_ge(iotas, 1 + topk)
                v.wait_ge(logit_done, 1)
                for part, tt in two(0):
                    s.did(v.tensor_copy(POS[:, tt, :], part))
                s.wait()
                s.did(v.tensor_reduce(m1[:, :], POS[:, :, :], AX.X, ALU.max))
                s.wait()
                v.tensor_tensor(L[:, :, :], POS[:, :, :], over_e(m1[:, :]), ALU.subtract).then_inc(shifted, 1)
                v.wait_ge(exps, 1)
                s.did(v.tensor_reduce(m1[:, :], W[:, :, :], AX.X, ALU.add))
                s.wait()
                s.did(v.reciprocal(tmp[:, 0, :], m1[:, :]))
                s.wait()
                s.did(v.tensor_tensor(PR[:, :, :], W[:, :, :], over_e(tmp[:, 0, :]), ALU.mult))
                s.wait()
                for t in range(T):
                    s.did(v.max(top[:, t, :], PR[:, t, :]))
                s.wait()
                for t in range(T):
                    s.did(v.max_index(idx[:, t, :], top[:, t, :], PR[:, t, :]))
                s.wait()
                for c in range(topk):
                    s.did(v.tensor_copy(ix[:, c, :], idx[:, :, c]))
                s.wait()
                for c in range(topk):
                    s.did(v.tensor_tensor(OH[:, c, :, :], ioE[:, :].unsqueeze(1).broadcast_to([P, T, E_]),
                                          over_e(ix[:, c, :]), ALU.is_equal))
                s.wait()
                if topk == 2:
                    v.tensor_tensor(M16[:, :, :], OH[:, 0, :, :], OH[:, 1, :, :], ALU.add).then_inc(masks, 1)
                else:
                    v.tensor_copy(M16[:, :, :], OH[:, 0, :, :]).then_inc(masks, 1)
                v.wait_ge(pos_done, 1)
                for part, tt in two(2):
                    s.did(v.tensor_copy(POS[:, tt, :], part))
                s.wait()
                if cap is None:
                    s.did(v.tensor_copy(cnt[:, :], ps[0:P, 4, 0:E_]))
                    s.wait()
                    s.did(v.memset(blk[:, 0, :], 1.0))
                    s.wait()
                    for b in range(1, N // (2 * P)):
                        s.did(v.scalar_tensor_tensor(blk[:, 0, :], cnt[:, :], float(2 * P * b), blk[:, 0, :],
                                                     ALU.is_gt, ALU.add))
                        s.wait()
                    s.did(v.memset(blk[:, 1, :], 0.0))
                    s.did(v.memset(blk[:, 2, 0:1], 0.0))
                    s.wait()
                    for e in range(1, E_):
                        s.did(v.tensor_tensor(blk[:, 2, e:e + 1], blk[:, 2, e - 1:e], blk[:, 0, e - 1:e], ALU.add))
                        s.wait()
                    s.did(v.tensor_copy(r.tab[:, 0, :], blk[0:1, 0, :]))
                    s.did(v.tensor_copy(r.tab[:, 1, :], blk[0:1, 2, :]))
                    s.did(v.tensor_scalar(blk[:, 1, :], blk[:, 2, :], float(2 * P), None, ALU.mult))
                    s.wait()
                    s.did(v.tensor_tensor(POS[:, :, :], POS[:, :, :],
                                          blk[:, 1, :].unsqueeze(1).broadcast_to([P, T, E_]), ALU.add))
                    s.wait()
                for c in range(topk):
                    s.did(v.tensor_tensor(W[:, :, :], OH[:, c, :, :], POS[:, :, :], ALU.mult))
                    s.wait()
                    s.did(v.tensor_reduce(pk[:, c, :], W[:, :, :], AX.X, ALU.add))
                    s.wait()
                if cap is None:
                    s.did(v.tensor_copy(r.put[:, 0, :], pk[:, 0, :]))
                    s.did(v.tensor_copy(r.get[:, 0, :], pk[:, 0, :]))
                    s.did(v.tensor_copy(r.gate[:, 0, :], top[:, :, 0]))
                    s.wait()
                else:
                    for c in range(2):
                        s.did(v.tensor_scalar(keep[:, c, :], pk[:, c, :], float(cap), None, ALU.is_lt))
                        s.did(v.tensor_scalar(tmp[:, c, :], pk[:, c, :], float(cap - 1), None, ALU.min))
                    s.wait()
                    for c in range(2):
                        s.did(v.scalar_tensor_tensor(tmp[:, 2 + c, :], ix[:, c, :], float(cap), tmp[:, c, :],
                                                     ALU.mult, ALU.add))
                    s.wait()
                    for c in range(2):
                        s.did(v.tensor_copy(r.get[:, c, :], tmp[:, 2 + c, :]))
                        s.did(v.tensor_tensor(tmp[:, c, :], tmp[:, 2 + c, :], spare[:, c, :], ALU.subtract))
                    s.wait()
                    for c in range(2):
                        s.did(v.tensor_tensor(tmp[:, c, :], tmp[:, c, :], keep[:, c, :], ALU.mult))
                    s.wait()
                    for c in range(2):
                        s.did(v.tensor_tensor(r.put[:, c, :], tmp[:, c, :], spare[:, c, :], ALU.add))
                    s.wait()
                    if keep_last:
                        s.did(v.tensor_tensor(tmp[:, 0, :], ix[:, 1, :], ix[:, 0, :], ALU.is_gt))
                        s.did(v.tensor_tensor(tmp[:, 1, :], ix[:, 0, :], ix[:, 1, :], ALU.is_gt))
                        s.wait()
                        for c in range(2):
                            s.did(v.tensor_tensor(tmp[:, c, :], tmp[:, c, :], keep[:, 1 - c, :], ALU.mult))
                        s.wait()
                        for c in range(2):
                            s.did(v.tensor_scalar(tmp[:, c, :], tmp[:, c, :], -1.0, 1.0, ALU.mult, ALU.add))
                        s.wait()
                    else:
                        s.did(v.tensor_tensor(m1[:, :], top[:, :, 0], top[:, :, 1], ALU.add))
                        s.wait()
                        s.did(v.reciprocal(tmp[:, 2, :], m1[:, :]))
                        s.wait()
                        for c in range(2):
                            s.did(v.tensor_tensor(tmp[:, c, :], tmp[:, 2, :], top[:, :, c], ALU.mult))
                        s.wait()
                    for c in range(2):
                        s.did(v.tensor_tensor(r.gate[:, c, :], tmp[:, c, :], keep[:, c, :], ALU.mult))
                    s.wait()
                if topk == 2:
                    s.did(v.tensor_tensor(W[:, :, :], OH[:, 0, :, :], over_e(r.gate[:, 0, :]), ALU.mult))
                    s.did(v.tensor_tensor(PR[:, :, :], OH[:, 1, :, :], over_e(r.gate[:, 1, :]), ALU.mult))
                    s.wait()
                    v.tensor_tensor(G[:, :, :], W[:, :, :], PR[:, :, :], ALU.add).then_inc(gates_ready, 1)
                else:
                    v.tensor_tensor(G[:, :, :], OH[:, 0, :, :], over_e(r.gate[:, 0, :]), ALU.mult)\
                        .then_inc(gates_ready, 1)


def experts(nc, k, r, rows_in, E_, F, R, tiles, func, w1, b1, w2, affine, buf, ybuf, dynamic):
    FC = F // 128
    EPG = 2 if tiles == 1 else 1
    with ExitStack() as ctx:
        def sb(name, shape, dt=fp32):
            return ctx.enter_context(nc.sbuf_tensor(k.name(name), shape, dt))

        def sem(name):
            return ctx.enter_context(k.semaphore(nc, k.name(name)))

        w1s = sb("w1s", [128, 2 * EPG, C, F])
        w2s = sb("w2s", [128, 2 * EPG, FC, D])
        b1s = sb("b1s", [128, 2 * EPG, FC])
        xb = sb("xb", [R, 2, D])
        xbT = sb("xbT", [128, 2, C, R])
        hT = sb("hT", [128, 2, FC, R])
        yb = sb("yb", [R, 2, D])
        put_done = k.gpsimd_dma_semaphore(nc, "put_done")
        stored = [k.gpsimd_dma_semaphore(nc, "stored") for _ in range(2)]
        w_in, w_used = [sem("w_in0"), sem("w_in1")], [sem("w_used0"), sem("w_used1")]
        rows_loaded, turned = [sem("rows0"), sem("rows1")], [sem("turned0"), sem("turned1")]
        xT_out, h_done, h_out = [[sem(n + "0"), sem(n + "1")] for n in ("xT_out", "h_done", "h_out")]
        yb_free = [sem("yb_free0"), sem("yb_free1")]
        y_done, y_out = [[sem(n + "0"), sem(n + "1")] for n in ("y_done", "y_out")]
        ps = k.ps

        with nc.Block() as block:
            @block.gpsimd
            def _(pool):
                n = 0
                for c in range(r.topk):
                    for t in range(T):
                        pool.indirect_dma_start(buf, bass.IndirectOffsetOnAxis(ap=r.put[:, c, t:t + 1], axis=0),
                                                rows_in[:, t, :], None).then_inc(put_done, 16)
                        n += 16
                pool.wait_ge(put_done, n)

        def run(eng, body, before=None, after=None):
            with eng.Fori(0, E_ // (2 * EPG)) as i:
                for g in range(2):
                    if before is not None:
                        before(i, g)
                    e = i * 2 + g
                    if dynamic:
                        n = eng.snap(eng.value_load(r.tab[0:1, 0, bass.ds(e, 1)], min_val=1, max_val=N // (2 * P)))
                        first = eng.snap(eng.value_load(r.tab[0:1, 1, bass.ds(e, 1)], min_val=0,
                                                        max_val=r.max_blocks))
                        with eng.Fori(0, n) as q:
                            body(i, first + q, g)
                    else:
                        body(i, e, g)
                    if after is not None:
                        after(g)

        def rows_of(u, s):
            return bass.ds(nc.s_assert_within(u * (2 * R) + s * R, 0, r.rows - R,
                                              skip_runtime_bounds_check_because="the blocks fit the buffer"), R)

        def second(s):
            return s if EPG == 2 else 0

        with nc.Block() as block:
            @block.sync
            def _(sp):
                def weights(i, g):
                    sp.wait_ge(w_used[g], i + 1)
                    for x_ in range(EPG):
                        e = (i * 2 + g) * EPG + x_
                        sp.dma_start(w1s[:, g * EPG + x_, :, :], w1[bass.ds(e, 1)].rearrange("o p c f -> p (o c) f"))\
                            .then_inc(w_in[g], 16)
                        sp.dma_start(w2s[:, g * EPG + x_, :, :],
                                     w2[bass.ds(e, 1)].rearrange("o (c p) n -> p (o c) n", p=128))\
                            .then_inc(w_in[g], 16)
                        sp.dma_start(b1s[:, g * EPG + x_, :], b1[bass.ds(e, 1)].rearrange("o p f -> p (o f)"))\
                            .then_inc(w_in[g], 16)

                def rows(i, u, g):
                    for s in range(2):
                        sp.wait_ge(turned[s], u + 1)
                        sp.dma_start(xb[:, s, :], buf[rows_of(u, s), :]).then_inc(rows_loaded[s], 16)
                run(sp, rows, before=weights)

            @block.gpsimd
            def _(pool):
                pool.sem_inc(yb_free[0], 1)
                pool.sem_inc(yb_free[1], 1)

                def store(i, u, g):
                    for s in range(2):
                        pool.wait_ge(y_out[s], u + 2)
                        pool.dma_start(ybuf[rows_of(u, s), :], yb[:, s, :]).then_inc(stored[s], 16)
                    for s in range(2):
                        pool.wait_ge(stored[s], u * 16 + 16)
                        pool.sem_inc(yb_free[s], 1)
                run(pool, store)

            @block.tensor
            def _(pe):
                for g in range(2):
                    pe.sem_inc(w_used[g], 1)
                    pe.sem_inc(turned[g], 1)

                def products(i, u, g):
                    for s in range(2):
                        pe.wait_ge(rows_loaded[s], u * 16 + 16)
                        for c in range(C):
                            mm = pe.transpose(ps[:, 4 * s, R * c:R * c + R], xb[:, s, 128 * c:128 * c + 128],
                                              k.ident[0:R, 0:R])
                        mm.then_inc(turned[s], 1)
                    pe.wait_ge(w_in[g], (i + 1) * (48 * EPG))
                    for s in range(2):
                        w = g * EPG + second(s)
                        pe.wait_ge(xT_out[s], u * C + C)
                        for m in range(FC):
                            for c in range(C):
                                mm = pe.matmul(ps[:, 4 * s + 1, R * m:R * m + R],
                                               w1s[:, w, c, 128 * m:128 * m + 128],
                                               xbT[:, s, c, :], start=(c == 0), stop=(c == C - 1))
                        mm.then_inc(h_done[s], 1)
                    for s in range(2):
                        w = g * EPG + second(s)
                        pe.wait_ge(h_out[s], u * FC + FC)
                        pe.wait_ge(y_out[s], u + 1)
                        for m in range(FC):
                            mm = pe.matmul(ps[0:R, 4 * s + 2, :], hT[:, s, m, :], w2s[:, w, m, :],
                                           start=(m == 0), stop=(m == FC - 1))
                        mm.then_inc(y_done[s], 1)

                run(pe, products, after=lambda g: pe.drain().then_inc(w_used[g], 1))

            @block.scalar
            def _(act):
                def bend(i, u, g):
                    for s in range(2):
                        act.wait_ge(turned[s], u + 2)
                        for c in range(C):
                            o, in_ = xbT[:, s, c, :], ps[:, 4 * s, R * c:R * c + R]
                            if affine is None:
                                act.activation(o, in_, ACT.Copy).then_inc(xT_out[s], 1)
                            else:
                                act.activation(o, in_, ACT.Identity, bias=affine[1][:, c:c + 1],
                                               scale=affine[0][:, c:c + 1]).then_inc(xT_out[s], 1)
                    for s in range(2):
                        act.wait_ge(h_done[s], u + 1)
                        for m in range(FC):
                            act.activation(hT[:, s, m, :], ps[:, 4 * s + 1, R * m:R * m + R], func,
                                           bias=b1s[:, g * EPG + second(s), m:m + 1]).then_inc(h_out[s], 1)
                run(act, bend)

            @block.vector
            def _(v):
                v.sem_inc(y_out[0], 1)
                v.sem_inc(y_out[1], 1)

                def take(i, u, g):
                    for s in range(2):
                        v.wait_ge(y_done[s], u + 1)
                        v.wait_ge(yb_free[s], u + 1)
                        v.tensor_copy(yb[:, s, :], ps[0:R, 4 * s + 2, :]).then_inc(y_out[s], 1)
                run(v, take)


def combine(nc, k, r, x, res, b2, ybuf, E_):
    with ExitStack() as ctx:
        Y = ctx.enter_context(nc.sbuf_tensor(k.name("Y"), [P, 4, D], fp32))
        got = [k.gpsimd_dma_semaphore(nc, "got") for _ in range(4)]
        used, summed, taken = (ctx.enter_context(k.semaphore(nc, k.name(n))) for n in ("y_used", "summed", "taken"))
        K_ = r.topk
        with nc.Block() as block:
            @block.gpsimd
            def _(pool):
                for n in range(K_ * T):
                    t, c = n // K_, n % K_
                    if n >= 4:
                        pool.wait_ge(used, n - 3)
                    pool.indirect_dma_start(Y[:, n % 4, :], None, ybuf,
                                            bass.IndirectOffsetOnAxis(ap=r.get[:, c, t:t + 1], axis=0))\
                        .then_inc(got[n % 4], 16)

            @block.tensor
            def _(pe):
                for t in range(T):
                    if t >= 8:
                        pe.wait_ge(taken, 2 * (t - 7))
                    pe.matmul(k.ps[0:P, t % 8, :], r.gateT[:, P * t:P * t + P], b2, start=True, stop=True)\
                        .then_inc(summed, 1)

            @block.vector
            def _(v):
                for t in range(T):
                    v.wait_ge(summed, t + 1)
                    if res is not None:
                        v.tensor_tensor(x[:, t, :], x[:, t, :], res[:, t, :], ALU.add).then_inc(taken, 1)
                    else:
                        v.sem_inc(taken, 1)
                    v.wait_ge(taken, 2 * t + 1)
                    v.tensor_tensor(x[:, t, :], x[:, t, :], k.ps[0:P, t % 8, :], ALU.add).then_inc(taken, 1)
                    v.wait_ge(taken, 2 * t + 2)
                    for c in range(K_):
                        n = t * K_ + c
                        v.wait_ge(got[n % 4], 16 * (n // 4 + 1))
                        v.scalar_tensor_tensor(x[:, t, :], Y[:, n % 4, :], r.gate[:, c, t:t + 1], x[:, t, :],
                                               ALU.mult, ALU.add).then_inc(used, 1)
                        v.wait_ge(used, n + 1)
class Routing:

    def __init__(self, nc, k, ctx, E_, topk, cap):
        self.topk = topk
        blocks = None if cap else E_ + N // (2 * P) - 1
        self.max_blocks = blocks
        self.rows = E_ * cap if cap else blocks * 2 * P
        self.spare0 = self.rows
        self.put = ctx.enter_context(nc.sbuf_tensor(k.name("put"), [P, 2, T], u32))
        self.get = ctx.enter_context(nc.sbuf_tensor(k.name("get"), [P, 2, T], u32))
        self.gate = ctx.enter_context(nc.sbuf_tensor(k.name("gate"), [P, 2, T], fp32))
        self.gateT = ctx.enter_context(nc.sbuf_tensor(k.name("gateT"), [E_, N], fp32))
        self.tab = ctx.enter_context(nc.sbuf_tensor(k.name("tab"), [1, 2, E_], i32))


class Room:

    def __init__(self, tile):
        self.flat, self.used = tile[:, :, :].rearrange("p a b -> p (a b)"), 0

    def __call__(self, partitions, shape):
        size = int(np.prod(shape))
        piece = self.flat[0:partitions, self.used:self.used + size]
        self.used += size
        assert self.used <= self.flat.shape[1]
        return piece if len(shape) == 1 else piece.rearrange("p (a b) -> p a b", a=shape[0])


def rowtiles(ap):
    return ap.rearrange("(t p) n -> p t n", p=P)


def kchunks(ap):
    return ap.rearrange("(c p) n -> p c n", p=128)


def row(ap):
    return ap.rearrange("(o n) -> o n", o=1)


def l0_gnn(nc, k, a, x, G):
    with ExitStack() as ctx:
        def sb(name, shape):
            return ctx.enter_context(nc.sbuf_tensor(k.name(name), shape, fp32))
        h, hT, mT = sb("h", [P, T, D]), sb("hT", [128, C, N]), sb("meanT", [128, C, N])
        wl, wr, bl = sb("wl", [128, C, D]), sb("wr", [128, C, D]), sb("bl", [1, D])
        norm_rows(nc, k, x, h, hT)
        for l in range(2):
            load(nc, k, [(wl[:, :, :], kchunks(a[f"L0_gnn_Wl{l}T"])), (wr[:, :, :], kchunks(a[f"L0_gnn_Wr{l}T"])),
                         (bl[:, :], row(a[f"L0_gnn_bl{l}"]))])
            columns_product(nc, k, h, G, T, C, lambda act, m, ch, n, psum:
                            act.activation(mT[:, m, ch[0]:ch[0] + ch[1]], psum, ACT.Copy))
            rows_product(nc, k, [(mT, wl, C), (hT, wr, C)], bl[:, :], copy_rows(h, ACT.Relu))
            if l == 0:
                transpose_only(nc, k, h, hT)
        add_into(nc, k, x, h)


def transformer(nc, k, a, x, pre, E_, F, cap, func, keep_last, buf, ybuf, Gf):
    with ExitStack() as ctx:
        def sb(c_, name, shape):
            return c_.enter_context(nc.sbuf_tensor(k.name(name), shape, fp32))
        res = sb(ctx, "res", [P, T, D])
        g1, b1, g2, b2 = (sb(ctx, n, [128, C]) for n in ("g1", "b1", "g2", "b2"))
        load(nc, k, [(g1[:, :], a[pre + "ln1_g_c"]), (b1[:, :], a[pre + "ln1_b_c"]),
                     (g2[:, :], a[pre + "ln2_g_c"]), (b2[:, :], a[pre + "ln2_b_c"])])
        norm_rows(nc, k, x, res)
        bias = pre + "bo" in a
        with ExitStack() as c2:
            room = Room(Gf)
            ctxT = room(128, (C, N))
            pair = [c2.enter_context(nc.sbuf_tensor(k.name(n), [128, C, N], f32r)) for n in ("x_hi", "x_lo")]
            with ExitStack() as c3:
                xn = sb(c3, "xn", [P, T, D])
                norm_rows(nc, k, res, xn, ctxT, (g1, b1))
            split(nc, k, [(ctxT, *pair)])
            attention(nc, k, pair, a[pre + "wqk"], a[pre + "bqk"] if bias else None, a[pre + "wv"],
                      a[pre + "bv"] if bias else None, ctxT, room)
            wo, bo = sb(c2, "wo", [128, C, D]), sb(c2, "bo", [1, D])
            load(nc, k, [(wo[:, :, :], kchunks(a[pre + "wo"]))] + ([(bo[:, :], row(a[pre + "bo"]))] if bias else []))
            rows_product(nc, k, [(ctxT, wo, C)], bo[:, :] if bias else None, add_rows(res))
        yn, xnT = sb(ctx, "yn", [P, T, D]), sb(ctx, "xnT", [128, C, N])
        norm_rows(nc, k, res, yn, xnT, (g2, b2))
        r = Routing(nc, k, ctx, E_, 2, cap)
        with ExitStack() as c2:
            wr, br = sb(c2, "wr", [128, C, E_]), sb(c2, "br", [1, E_])
            load(nc, k, [(wr[:, :, :], kchunks(a[pre + ("router_w" if bias else "wr")]))]
                 + ([(br[:, :], row(a[pre + "router_b"]))] if bias else []))
            route(nc, k, xnT, wr, br[:, :] if bias else None, E_, 2, cap, keep_last, r)
        b2r = sb(ctx, "b2r", [E_, D])
        load(nc, k, [(b2r[:, :], a[pre + "b2"])])
        R = 78 if cap == 78 else P
        experts(nc, k, r, yn, E_, F, R, 1 if R == cap else 2, func, a[pre + "w1_p"], a[pre + "b1_p"], a[pre + "w2"],
                (g2, b2), buf, ybuf, False)
        combine(nc, k, r, x, res, b2r[:, :], ybuf, E_)


def l1_gnn(nc, k, a, x, G):
    with ExitStack() as ctx:
        def sb(name, shape):
            return ctx.enter_context(nc.sbuf_tensor(k.name(name), shape, fp32))
        xn, xT, w, b = sb("xn", [P, T, D]), sb("xT", [128, C, N]), sb("w", [128, C, D]), sb("b", [1, D])
        load(nc, k, [(w[:, :, :], kchunks(a["L1_gnn_weight"])), (b[:, :], row(a["L1_gnn_bias"]))])
        norm_rows(nc, k, x, xn, xT)
        rows_product(nc, k, [(xT, w, C)], None, copy_rows(xn))
        rows_product(nc, k, [(G, xn, T)], b[:, :], add_rows(x))


def l3_gnn(nc, k, a, x, G):
    with ExitStack() as ctx:
        def sb(name, shape):
            return ctx.enter_context(nc.sbuf_tensor(k.name(name), shape, fp32))
        xn, xT, w, b = sb("xn", [P, T, D]), sb("xT", [128, C, N]), sb("w", [128, C, D]), sb("b", [1, D])
        load(nc, k, [(w[:, :, :], kchunks(a["L3_gnn_W"])), (b[:, :], row(a["L3_gnn_b"]))])
        norm_rows(nc, k, x, xn, xT)
        rows_product(nc, k, [(xT, w, C)], b[:, :], copy_rows(xn))
        rows_product(nc, k, [(G, xn, T)], None,
                     {"vector": lambda v, i, psum: v.scalar_tensor_tensor(x[:, i, :], psum, 0.0, x[:, i, :],
                                                                          ALU.max, ALU.add)})


def l2_gnn(nc, k, a, x, G):
    with ExitStack() as ctx:
        def sb(name, shape):
            return ctx.enter_context(nc.sbuf_tensor(k.name(name), shape, fp32))

        def sem(name):
            return ctx.enter_context(k.semaphore(nc, k.name(name)))
        h, xT, aT = sb("h", [P, T, D]), sb("xT", [128, C, N]), sb("aggT", [128, C, N])
        w = sb("w", [128, C, D])
        cols = sb("bgb", [128, 3, 3, C])
        st, mv = sb("bn_parts", [128, C, 3, 6]), sb("mean_var", [128, C, 2])
        sc, sh = sb("scale", [128, C]), sb("shift", [128, C])
        norm_rows(nc, k, x, h, xT)
        for l in range(3):
            steps, var_ready, std_ready, scale_ready = sem("steps"), sem("var"), sem("std"), sem("scale_ready")
            load(nc, k, [(w[:, :, :], kchunks(a["L2_gnn_WT"][l]))] + ([(cols[:, :, :, :], a["L2_gnn_bgb"])] if l == 0 else []))
            rows_product(nc, k, [(xT, w, C)], None, copy_rows(h))
            columns_product(nc, k, h, G, T, C, lambda act, m, ch, n, psum:
                            act.activation(aT[:, m, ch[0]:ch[0] + ch[1]], psum, ACT.Identity,
                                           bias=cols[:, 0, l, m:m + 1]))
            with nc.Block() as block:
                @block.vector
                def _(v):
                    s = Steps(v, steps)
                    for m in range(C):
                        for n, (c0, cn) in enumerate(CH):
                            s.did(v.bn_stats(st[:, m, n, :], aT[:, m, c0:c0 + cn]))
                    s.wait()
                    for m in range(C):
                        s.did(v.bn_aggr(mv[:, m, :], st[:, m, :, :].rearrange("p a b -> p (a b)")))
                    s.wait()
                    v.tensor_scalar(sc[:, :], mv[:, :, 1], 1e-5, None, ALU.add).then_inc(var_ready, 1)
                    v.wait_ge(std_ready, 1)
                    s.did(v.reciprocal(sh[:, :], sc[:, :]))
                    s.wait()
                    s.did(v.tensor_tensor(sc[:, :], sh[:, :], cols[:, 1, l, :], ALU.mult))
                    s.wait()
                    s.did(v.tensor_tensor(sh[:, :], mv[:, :, 0], sc[:, :], ALU.mult))
                    s.wait()
                    v.tensor_tensor(sh[:, :], cols[:, 2, l, :], sh[:, :], ALU.subtract).then_inc(scale_ready, 1)

                @block.scalar
                def _(act):
                    act.wait_ge(var_ready, 1)
                    act.activation(sc[:, :], sc[:, :], ACT.Sqrt).then_inc(std_ready, 1)
                    act.wait_ge(scale_ready, 1)
                    for m in range(C):
                        act.activation(xT[:, m, :], aT[:, m, :], ACT.Relu, bias=sh[:, m:m + 1],
                                       scale=sc[:, m:m + 1])
        turned, taken = sem("turned"), sem("taken")
        with nc.Block() as block:
            @block.tensor
            def _(pe):
                for i in range(T):
                    if i >= 8:
                        pe.wait_ge(taken, i - 7)
                    for c in range(C):
                        mm = pe.transpose(k.ps[0:P, i % 8, 128 * c:128 * c + 128], xT[:, c, P * i:P * i + P],
                                          k.ident[:, :])
                    mm.then_inc(turned, 1)

            @block.vector
            def _(v):
                for i in range(T):
                    v.wait_ge(turned, i + 1)
                    v.tensor_tensor(x[:, i, :], x[:, i, :], k.ps[0:P, i % 8, :], ALU.add).then_inc(taken, 1)


def l2_ffn(nc, k, a, x, buf, ybuf):
    E_, F = 8, 512
    with ExitStack() as ctx:
        def sb(c_, name, shape):
            return c_.enter_context(nc.sbuf_tensor(k.name(name), shape, fp32))
        xn, xT = sb(ctx, "xn", [P, T, D]), sb(ctx, "xT", [128, C, N])
        norm_rows(nc, k, x, xn, xT)
        r = Routing(nc, k, ctx, E_, 1, None)
        with ExitStack() as c2:
            wr, br = sb(c2, "wr", [128, C, E_]), sb(c2, "br", [1, E_])
            load(nc, k, [(wr[:, :, :], kchunks(a["L2_ffn_Wr"])), (br[:, :], row(a["L2_ffn_br"]))])
            route(nc, k, xT, wr, br[:, :], E_, 1, None, False, r)
        b2r = sb(ctx, "b2r", [E_, D])
        load(nc, k, [(b2r[:, :], a["L2_ffn_b2"])])
        experts(nc, k, r, xn, E_, F, P, 2, ACT.Relu, a["L2_ffn_w1_p"], a["L2_ffn_b1_p"], a["L2_ffn_W2"], None, buf, ybuf, True)
        combine(nc, k, r, x, None, b2r[:, :], ybuf, E_)


def l1_ffn(nc, k, a, x, Gf):
    E_, F, FC = 8, 256, 2
    with ExitStack() as ctx:
        def sb(c_, name, shape):
            return c_.enter_context(nc.sbuf_tensor(k.name(name), shape, fp32))

        def sem(name):
            return ctx.enter_context(k.semaphore(nc, k.name(name)))
        xn, xT, hT = sb(ctx, "xn", [P, T, D]), sb(ctx, "xT", [128, C, N]), sb(ctx, "hT", [128, FC, N])
        W1m, W2m = sb(ctx, "W1m", [128, C, F]), sb(ctx, "W2m", [128, FC, D])
        b1m, b2b, lngb, lnbb = (sb(ctx, "b1m", [128, FC]), sb(ctx, "b2b", [P, D]), sb(ctx, "lngb", [P, D]),
                                sb(ctx, "lnbb", [P, D]))
        norm_rows(nc, k, x, xn, xT)
        with ExitStack() as c2:
            gw, gb = sb(c2, "gfc1", [128, C, D]), sb(c2, "gfc1_b", [128, C])
            g2w, g2b, g2c = sb(c2, "gfc2", [128, C, E_]), sb(c2, "gfc2_b", [128, E_]), sb(c2, "gfc2_bc", [E_, 1])
            tv1 = Gf[:, :, :].rearrange("p t n -> p (t n)")[:, 0:E_ * C * F].rearrange("p (e n) -> p e n", e=E_)
            tv2 = sb(c2, "tv2", [128, E_, FC * D])
            tb1, tb2 = sb(c2, "tb1", [E_, F]), sb(c2, "tb2", [E_, D])
            tg, tb, lg8, lb8 = (sb(c2, n, [E_, D]) for n in ("tg", "tb", "lg8", "lb8"))
            b1c, rows3 = sb(c2, "b1c", [128, FC]), sb(c2, "rows3", [1, 3, D])
            gh, ghs, ghb = sb(c2, "gh", [128, 4, 500]), sb(c2, "gh_sum", [128, C, 3]), sb(c2, "ghb", [128, C, 128])
            ghm, gB, gC = sb(c2, "gh_mean", [128, C]), sb(c2, "g_all", [128, E_]), sb(c2, "g_col", [E_, 1])
            load(nc, k, [(gw[:, :, :], kchunks(a["L1_ffn_gfc1_wT"])), (gb[:, :], a["L1_ffn_gfc1_b_c"]),
                         (g2w[:, :, :], kchunks(a["L1_ffn_gfc2_wT"])),
                         (g2b[:, :], a["L1_ffn_gfc2_b"].partition_broadcast(128)),
                         (g2c[:, :], a["L1_ffn_gfc2_b"].rearrange("(p o) -> p o", o=1)),
                         (tv1[:, :, :], a["L1_ffn_tv_W1_p"]), (tv2[:, :, :], a["L1_ffn_tv_W2_p"]),
                         (W1m[:, :, :], kchunks(a["L1_ffn_W1T"])), (W2m[:, :, :], kchunks(a["L1_ffn_W2T"])),
                         (tb1[:, :], a["L1_ffn_tv_b1"]), (tb2[:, :], a["L1_ffn_tv_b2"]),
                         (tg[:, :], a["L1_ffn_tv_ln_g"]), (tb[:, :], a["L1_ffn_tv_ln_b"]),
                         (lg8[:, :], a["L1_ffn_ln_g"].partition_broadcast(E_)),
                         (lb8[:, :], a["L1_ffn_ln_b"].partition_broadcast(E_)),
                         (b1c[:, :], a["L1_ffn_b1_c"]), (rows3[:, 0, :], row(a["L1_ffn_b2"])),
                         (rows3[:, 1, :], row(a["L1_ffn_ln_g"])), (rows3[:, 2, :], row(a["L1_ffn_ln_b"]))])
            columns_product(nc, k, gw, xT, C, C, lambda act, m, ch, n, psum:
                            act.activation(gh[:, (3 * m + n) % 4, 0:ch[1]], psum, ACT.Relu, bias=gb[:, m:m + 1],
                                           accum_out=ghs[:, m, n:n + 1]), reuse=4)
            steps, mean_ready, g_done, g_out = sem("steps"), sem("mean_ready"), sem("g_done"), sem("g_out")
            rows_ready, sums_done, accs = sem("rows_ready"), sem("sums_done"), sem("accs")
            with nc.Block() as block:
                @block.tensor
                def _(pe):
                    pe.wait_ge(mean_ready, C)
                    for c in range(C):
                        pe.matmul(k.ps[:, 0, 0:E_], ghb[:, c, :], g2w[:, c, :], start=(c == 0), stop=(c == C - 1))
                    for c in range(C):
                        mm = pe.matmul(k.ps[0:E_, 1, 0:1], g2w[:, c, :], ghm[:, c:c + 1], start=(c == 0),
                                       stop=(c == C - 1))
                    mm.then_inc(g_done, 1)
                    pe.wait_ge(rows_ready, 4)
                    for n, t_ in enumerate((tb2, tg, tb)):
                        pe.matmul(k.ps[0:P, 2 + n, :], k.ones[0:E_, 0:P], t_[:, :], start=True, stop=False)
                        pe.matmul(k.ps[0:P, 2 + n, :], k.ones[0:1, 0:P], rows3[:, n, :], start=False, stop=True)
                    for m in range(FC):
                        mm = pe.matmul(k.ps[:, 5, m:m + 1], tb1[:, 128 * m:128 * m + 128], gC[:, :], start=True,
                                       stop=True, skip_group_check=True)
                    mm.then_inc(sums_done, 1)

                @block.scalar
                def _(act):
                    act.wait_ge(sums_done, 1)
                    for n, o in enumerate((b2b, lngb, lnbb)):
                        act.activation(o[:, :], k.ps[0:P, 2 + n, :], ACT.Copy)

                @block.vector
                def _(v):
                    s = Steps(v, steps)
                    s.did(v.tensor_reduce(ghm[:, :], ghs[:, :, :], AX.X, ALU.add))
                    s.wait()
                    s.did(v.tensor_scalar(ghm[:, :], ghm[:, :], 1.0 / N, None, ALU.mult))
                    s.wait()
                    for c in range(C):
                        v.tensor_scalar(ghb[:, c, :], k.ones[:, :], ghm[:, c:c + 1], None, ALU.mult)\
                            .then_inc(mean_ready, 1)
                    s.did(v.tensor_tensor(tg[:, :], tg[:, :], lg8[:, :], ALU.subtract))
                    s.did(v.tensor_tensor(tb[:, :], tb[:, :], lb8[:, :], ALU.subtract))
                    s.wait()
                    v.tensor_scalar(tg[:, :], tg[:, :], 0.03, None, ALU.mult).then_inc(rows_ready, 1)
                    v.tensor_scalar(tb[:, :], tb[:, :], 0.03, None, ALU.mult).then_inc(rows_ready, 1)
                    v.wait_ge(g_done, 1)
                    s.did(v.tensor_tensor(gB[:, :], g2b[:, :], k.ps[:, 0, 0:E_], ALU.add))
                    v.tensor_tensor(gC[:, :], g2c[:, :], k.ps[0:E_, 1, 0:1], ALU.add).then_inc(rows_ready, 1)
                    v.wait_ge(rows_ready, 3)
                    s.wait()
                    v.tensor_scalar(tb2[:, :], tb2[:, :], gC[:, 0:1], None, ALU.mult).then_inc(rows_ready, 1)
                    W1f = W1m[:, :, :].rearrange("p c f -> p (c f)")
                    W2f = W2m[:, :, :].rearrange("p c f -> p (c f)")
                    for e in range(E_):
                        if e:
                            v.wait_ge(accs, 2 * e)
                        v.scalar_tensor_tensor(W1f, tv1[:, e, :], gB[:, e:e + 1], W1f, ALU.mult, ALU.add)\
                            .then_inc(accs, 1)
                        v.scalar_tensor_tensor(W2f, tv2[:, e, :], gB[:, e:e + 1], W2f, ALU.mult, ALU.add)\
                            .then_inc(accs, 1)
                    v.wait_ge(sums_done, 1)
                    v.tensor_tensor(b1m[:, :], b1c[:, :], k.ps[:, 5, 0:FC], ALU.add)
        columns_product(nc, k, W1m, xT, C, FC, lambda act, m, ch, n, psum:
                        act.activation(hT[:, m, ch[0]:ch[0] + ch[1]], psum, ACT.Relu, bias=b1m[:, m:m + 1]))
        rows_product(nc, k, [(hT, W2m, FC)], None, add_rows(xn))
        steps = sem("steps")
        with nc.Block() as block:
            @block.vector
            def _(v):
                v.tensor_tensor(xn[:, :, :], xn[:, :, :], b2b[:, :].unsqueeze(1).broadcast_to([P, T, D]), ALU.add)
        norm_rows(nc, k, xn, xn)
        with nc.Block() as block:
            @block.vector
            def _(v):
                s = Steps(v, steps)
                s.did(v.tensor_tensor(xn[:, :, :], xn[:, :, :], lngb[:, :].unsqueeze(1).broadcast_to([P, T, D]),
                                      ALU.mult))
                s.wait()
                s.did(v.tensor_tensor(xn[:, :, :], xn[:, :, :], lnbb[:, :].unsqueeze(1).broadcast_to([P, T, D]),
                                      ALU.add))
                s.wait()
                s.did(v.tensor_tensor(x[:, :, :], x[:, :, :], xn[:, :, :], ALU.add))


def finish_graph(nc, k, CT, WT, W, w_spill, ah_spill):
    with ExitStack() as ctx:
        def sb(name, shape):
            return ctx.enter_context(nc.sbuf_tensor(k.name(name), shape, fp32))

        def sem(name):
            return ctx.enter_context(k.semaphore(nc, k.name(name)))
        deg, rc, dr = sb("deg", [P, N]), sb("inv_deg", [P, N]), sb("dinv_row", [P, N])
        dc, junk = sb("dinv_col", [P, T]), sb("junk", [P, P])
        turned, taken, deg_done, steps = sem("turned"), sem("taken"), sem("deg_done"), sem("steps")
        deg1, root_done, spilled = sem("deg1"), sem("root_done"), sem("spilled")
        scaled, normed = sem("scaled"), sem("normed")
        with nc.Block() as block:
            @block.sync
            def _(sp):
                sp.wait_ge(taken, 3 * T)
                spill_rows(sp, rowtiles(w_spill), W, spilled)
                sp.wait_ge(spilled, 32)

            @block.tensor
            def _(pe):
                for n, (c0, cn) in enumerate(CH):
                    for t in range(T):
                        mm = pe.matmul(k.ps[0:P, 5 + n, 0:cn], k.ones[0:P, 0:P], CT[:, t, c0:c0 + cn],
                                       start=(t == 0), stop=(t == T - 1))
                    mm.then_inc(deg_done, 1)
                g = 0
                for d in range(T):
                    for c0, cn in CH:
                        if g >= 5:
                            pe.wait_ge(taken, g - 4)
                        for s_ in range(c0 // P, (c0 + cn) // P):
                            mm = pe.transpose(k.ps[0:P, g % 5, P * s_ - c0:P * s_ - c0 + P],
                                              WT[:, s_, P * d:P * d + P], k.ident[0:P, 0:P])
                        mm.then_inc(turned, 1)
                        g += 1

            @block.scalar
            def _(act):
                g = 0
                for d in range(T):
                    for c0, cn in CH:
                        act.wait_ge(turned, g + 1)
                        act.activation(W[:, d, c0:c0 + cn], k.ps[0:P, g % 5, 0:cn], ACT.Copy).then_inc(taken, 1)
                        g += 1
                act.wait_ge(deg1, 1)
                act.activation(rc[:, :], dr[:, :], ACT.Sqrt).then_inc(root_done, 1)

            @block.vector
            def _(v):
                s = Steps(v, steps)
                v.wait_ge(deg_done, 3)
                for n, (c0, cn) in enumerate(CH):
                    s.did(v.tensor_copy(deg[:, c0:c0 + cn], k.ps[0:P, 5 + n, 0:cn]))
                s.wait()
                v.tensor_scalar(dr[:, :], deg[:, :], 1.0, None, ALU.add).then_inc(deg1, 1)
                v.wait_ge(root_done, 1)
                s.did(v.reciprocal(dr[:, :], rc[:, :]))
                s.did(v.tensor_scalar(deg[:, :], deg[:, :], 1.0, None, ALU.max))
                s.wait()
                s.did(v.reciprocal(rc[:, :], deg[:, :]))
                for t in range(T):
                    s.did(v.tensor_tensor(junk[:, :], dr[:, P * t:P * t + P], k.ident[0:P, 0:P], ALU.mult))
                    s.wait()
                    s.did(v.tensor_reduce(dc[:, t:t + 1], junk[:, :], AX.X, ALU.add))
                    s.wait()
        diag = sb("diag", [P, T, P])
        with nc.Block() as block:
            @block.sync
            def _(sp):
                for half in range(2):
                    t0, t1 = half * (T // 2), (half + 1) * (T // 2)
                    sp.wait_ge(normed, t1)
                    spill_rows(sp, rowtiles(ah_spill)[:, t0:t1], WT[:, t0:t1], spilled)
                sp.wait_ge(spilled, 96)

            @block.vector
            def _(v):
                for t in range(T):
                    v.scalar_tensor_tensor(WT[:, t, :], CT[:, t, :], dc[:, t:t + 1], dr[:, :], ALU.mult, ALU.mult)\
                        .then_inc(scaled, 1)
                    v.scalar_tensor_tensor(diag[:, t, :], k.ident[0:P, 0:P], dc[:, t:t + 1],
                                           dr[:, P * t:P * t + P], ALU.mult, ALU.mult).then_inc(scaled, 1)
                v.wait_ge(scaled, 2 * T)
                for t in range(T):
                    v.tensor_tensor(WT[:, t, P * t:P * t + P], WT[:, t, P * t:P * t + P], diag[:, t, :], ALU.add)\
                        .then_inc(normed, 1)
                for t in range(T):
                    v.tensor_tensor(CT[:, t, :], CT[:, t, :], rc[:, :], ALU.mult)


def spill_rows(sp, dram, sbuf, sem):
    sp.dma_start(dram[0:120], sbuf[0:120]).then_inc(sem, 16)
    sp.dma_start(dram[120:P], sbuf[120:P]).then_inc(sem, 16)




def program(nc, a, out):
    k = Kit()
    with ExitStack() as ctx:
        k.lasting = ctx
        k.ps = ctx.enter_context(nc.psum_tensor("ps", [128, 8, 512], fp32))
        k.ident = ctx.enter_context(nc.sbuf_tensor("ident", [128, 128], fp32))
        k.ones = ctx.enter_context(nc.sbuf_tensor("ones", [128, 128], fp32))
        k.tri = ctx.enter_context(nc.sbuf_tensor("tri", [128, 128], fp32))
        k.ones_row = ctx.enter_context(nc.sbuf_tensor("ones_row", [1, 512], fp32))
        k.ones16 = ctx.enter_context(nc.sbuf_tensor("ones16", [128, 128], bf16))
        k.tri16 = ctx.enter_context(nc.sbuf_tensor("tri16", [128, 128], bf16))
        k.c_sel, k.c_win = a["c_sel"], a["c_win"]
        Gf = ctx.enter_context(nc.sbuf_tensor("G", [128, T, N], fp32))
        x = ctx.enter_context(nc.sbuf_tensor("x", [P, T, D], fp32))
        G = Gf[0:P]
        zeroed = ctx.enter_context(k.semaphore(nc, "zeroed"))
        stored = ctx.enter_context(k.semaphore(nc, "stored"))

        def scratch(name, shape, dt=fp32):
            return nc.dram_tensor(name, shape, dt).ap()
        w_spill, ah_spill = scratch("w_spill", (N, N)), scratch("ah_spill", (N, N))
        NB0, NB3 = 64 * 78, 8 * 250
        NB2 = 12 * 250
        buf0, buf3, buf2 = (scratch("buf0", (NB0 + 2 * N, D)), scratch("buf3", (NB3 + 2 * N, D)),
                            scratch("buf2", (NB2, D)))
        yb0, yb3 = scratch("yb0", (NB0, D)), scratch("yb3", (NB3, D))
        scr1, scr2 = scratch("scr_minmax", (2, ET)), scratch("scr_tab", (NW, 4), i32)

        load(nc, k, [(k.ident[:, :], a["c_ident"]), (k.tri[:, :], a["c_tri"]), (x[:, :, :], rowtiles(a["x"]))])
        with nc.Block() as block:
            @block.vector
            def _(v):
                v.memset(k.ones[:, :], 1.0)
                v.memset(k.ones_row[:, :], 1.0)
                v.memset(k.ones16[:, :], 1.0)
                v.tensor_copy(k.tri16[:, :], k.tri[:, :])
        with ExitStack() as c2:
            zeros = c2.enter_context(nc.sbuf_tensor("zeros", [128, 2 * D], fp32))
            with nc.Block() as block:
                @block.vector
                def _(v):
                    v.memset(zeros[:, :], 0.0)

            def zero_buffers(sp):
                n = 0
                for b, rows in ((buf0, NB0), (buf3, NB3), (buf2, NB2)):
                    for r0 in range(0, rows, 256):
                        m = min(256, rows - r0) // 2
                        sp.dma_start(b[r0:r0 + 2 * m, :].rearrange("(p q) n -> p q n", q=2),
                                     zeros[0:m, :].rearrange("p (q n) -> p q n", q=2)).then_inc(zeroed, 16)
                        n += 16
                sp.wait_ge(zeroed, n)
            WT = c2.enter_context(nc.sbuf_tensor("WT", [P, T, N], fp32))
            build_graph(nc, k, G, WT, a["src_pt"], a["dst_pt"], a["w_pt"], a["dst_rows"], scr1, scr2, zero_buffers)
            W = c2.enter_context(nc.sbuf_tensor("W", [P, T, N], fp32))
            finish_graph(nc, k, G, WT, W, w_spill, ah_spill)

        def load_matrix(dram):
            with k.semaphore(nc, k.name("matrix_in")) as loaded:
                with nc.Block() as block:
                    @block.sync
                    def _(sp):
                        spill_rows(sp, G, rowtiles(dram), loaded)
                        sp.wait_ge(loaded, 32)
        k.clear_semaphores(nc)
        l0_gnn(nc, k, a, x, G)
        k.clear_semaphores(nc)
        transformer(nc, k, a, x, "L0_ffn_", 64, 256, 78, ACT.Gelu_apprx_tanh, False, buf0, yb0, Gf)
        k.clear_semaphores(nc)
        load_matrix(w_spill)
        l1_gnn(nc, k, a, x, G)
        l1_ffn(nc, k, a, x, Gf)
        k.clear_semaphores(nc)
        load_matrix(ah_spill)
        l2_gnn(nc, k, a, x, G)
        k.clear_semaphores(nc)
        l2_ffn(nc, k, a, x, buf2, buf2)
        k.clear_semaphores(nc)
        l3_gnn(nc, k, a, x, G)
        k.clear_semaphores(nc)
        transformer(nc, k, a, x, "L3_ffn_", 8, 256, 250, ACT.Gelu, True, buf3, yb3, Gf)
        with nc.Block() as block:
            @block.sync
            def _(sp):
                spill_rows(sp, rowtiles(out), x, stored)
                sp.wait_ge(stored, 32)


def layouts(inputs):
    import numpy as _np

    a = {n: _np.asarray(v) for n, v in inputs.items()}

    def heads(w):
        return w.reshape(C, 128, 8, 64).transpose(2, 1, 0, 3)

    def columns(b):
        return b.reshape(-1, 128).T

    w = _np.arange(NW)
    base = P * (w // WPT) + WIN * (w % WPT)
    p = _np.arange(128)
    sel = _np.zeros((128, 2 * WIN), _np.float32)
    sel[p[:WIN], p[:WIN]] = 1
    for m in (1, 2, 3):
        sel[WIN * m + p[:WIN], WIN + p[:WIN]] = 1
    o = {"c_sel": sel, "c_win": _np.stack([base, base + WIN - 1], 1).astype(_np.float32),
         "c_tri": (p[:, None] < p[None, :]).astype(_np.float32), "c_ident": _np.eye(128, dtype=_np.float32),
         "x": a["x"], "src_pt": a["src"].reshape(ET, P).T, "dst_pt": a["dst"].reshape(ET, P).T,
         "w_pt": a["edge_weight"].reshape(ET, P).T, "dst_rows": a["dst"].reshape(80, 4, P)}
    for l in range(2):
        o[f"L0_gnn_Wl{l}T"], o[f"L0_gnn_Wr{l}T"] = a[f"L0_gnn_Wl{l}"].T, a[f"L0_gnn_Wr{l}"].T
        o[f"L0_gnn_bl{l}"] = a[f"L0_gnn_bl{l}"]
    for pre, names in (("L0_ffn_", ("wv", "wo", "wr", "w2", "b2")),
                       ("L3_ffn_", ("wv", "wo", "bo", "bv", "router_w", "router_b", "w2", "b2"))):
        for n in names:
            o[pre + n] = a[pre + n]
        o[pre + "wqk"] = _np.concatenate([heads(a[pre + "wq"]), heads(a[pre + "wk"])], 3)
        for n in ("ln1_g", "ln1_b", "ln2_g", "ln2_b"):
            o[pre + n + "_c"] = columns(a[pre + n])
        e, d, f = a[pre + "w1"].shape
        o[pre + "w1_p"] = a[pre + "w1"].reshape(e, C, 128, f).transpose(0, 2, 1, 3)
        o[pre + "b1_p"] = a[pre + "b1"].reshape(e, f // 128, 128).transpose(0, 2, 1)
    o["L3_ffn_bqk"] = _np.concatenate([a["L3_ffn_bq"].reshape(8, 64), a["L3_ffn_bk"].reshape(8, 64)], 1)
    for n in ("L1_gnn_weight", "L1_gnn_bias", "L3_gnn_W", "L3_gnn_b", "L2_ffn_Wr", "L2_ffn_br", "L2_ffn_W2",
              "L2_ffn_b2", "L1_ffn_gfc2_b", "L1_ffn_tv_b1", "L1_ffn_tv_b2", "L1_ffn_tv_ln_g", "L1_ffn_tv_ln_b",
              "L1_ffn_ln_g", "L1_ffn_ln_b", "L1_ffn_b2"):
        o[n] = a[n]
    o["L2_ffn_w1_p"] = a["L2_ffn_W1"].reshape(8, C, 128, 512).transpose(0, 2, 1, 3)
    o["L2_ffn_b1_p"] = a["L2_ffn_b1"].reshape(8, 4, 128).transpose(0, 2, 1)
    o["L2_gnn_WT"] = a["L2_gnn_W"].transpose(0, 2, 1)
    o["L2_gnn_bgb"] = _np.stack([a["L2_gnn_" + n].reshape(3, C, 128).transpose(2, 0, 1)
                                 for n in ("b", "gamma", "beta")], 1)
    o["L1_ffn_gfc1_wT"], o["L1_ffn_gfc2_wT"] = a["L1_ffn_gfc1_w"].T, a["L1_ffn_gfc2_w"].T
    o["L1_ffn_gfc1_b_c"], o["L1_ffn_b1_c"] = columns(a["L1_ffn_gfc1_b"]), columns(a["L1_ffn_b1"])
    o["L1_ffn_W1T"], o["L1_ffn_W2T"] = a["L1_ffn_W1"].T, a["L1_ffn_W2"].T
    o["L1_ffn_tv_W1_p"] = a["L1_ffn_tv_W1"].reshape(8, 256, C, 128).transpose(3, 0, 2, 1).reshape(128, 8, C * 256)
    o["L1_ffn_tv_W2_p"] = a["L1_ffn_tv_W2"].reshape(8, D, 2, 128).transpose(3, 0, 2, 1).reshape(128, 8, 2 * D)
    return {"in_" + n: _np.ascontiguousarray(v) for n, v in o.items()}


def kernel(**inputs):
    import concourse.bacc as _bacc
    from concourse import mybir as _mybir
    from concourse.bass_utils import run_bass_kernel_spmd as _run

    nc = _bacc.Bacc("TRN2", target_bir_lowering=False, num_devices=1)
    arrays = layouts(inputs)
    a = {n[3:]: nc.dram_tensor(n, v.shape, _mybir.dt.from_np(v.dtype), kind="ExternalInput").ap()
         for n, v in arrays.items()}
    out = nc.dram_tensor("out_x", (N, D), _mybir.dt.float32, kind="ExternalOutput").ap()
    program(nc, a, out)
    r = _run(nc, [arrays], core_ids=[0])
    return r.results[0]["out_x"]
```

```python
import concourse.bass as bass
from concourse import mybir
from contextlib import ExitStack, contextmanager
import numpy as np

N = 1250
D = 512
E = 40000
P = 125
T = N // P
C = D // 128
ET = E // P
RUN = 4
ETP = ET + RUN
WIN = 32
WPT = 4
NW = T * WPT
CH = [(0, 500), (500, 500), (1000, 250)]

fp32 = mybir.dt.float32
f32r = mybir.dt.float32r
fp16 = mybir.dt.float16
bf16 = mybir.dt.bfloat16
i32 = mybir.dt.int32
u32 = mybir.dt.uint32
ALU = mybir.AluOpType
ACT = mybir.ActivationFunctionType
AX = mybir.AxisListType


class Steps:

    def __init__(self, eng, sem, base=0):
        self.eng, self.sem, self.base, self.n = eng, sem, base, 0

    def did(self, ins):
        ins.then_inc(self.sem, 1)
        self.n += 1
        return ins

    def wait(self):
        self.eng.wait_ge(self.sem, self.base + self.n)


def build_graph(nc, k, CT, WT, src_pt, dst_pt, w_pt, dst_rows, scr_minmax, scr_tab, beside):
    SLOTS = 8
    with ExitStack() as ctx:
        def sb(name, shape, dt=fp32):
            return ctx.enter_context(nc.sbuf_tensor(name, shape, dt))

        def sem(name):
            return ctx.enter_context(k.semaphore(nc, name))

        ei = sb("edge_int", [P, 2, ET], i32)
        dF = sb("dst_f", [P, ETP])
        sF = sb("src_f", [P, ETP])
        wF = sb("w_f", [P, 3, ET])
        wp = sb("w_parts", [P, ETP, 4], bf16)
        dr = sb("dst_rows", [80, 4, P], i32)
        mm = sb("tile_minmax", [80, 2, 4])
        mb = sb("minmax_b", [NW, 2, ET])
        ov = sb("overlap", [NW, 3, ET])
        tl = sb("win_limits", [NW, 8])
        ti = sb("win_ints", [NW, 4], i32)
        tf = sb("win_tab", [NW, 4], i32)
        tab = sb("win_row", [1, NW * 4], i32)
        ioi = sb("iota_i", [P, N], i32)
        io16 = sb("iota16", [P, N + WIN], fp16)
        iot = sb("iota_t", [NW, ET])
        sel = sb("sel_parts", [128, 64])
        ohs = sb("onehot_src", [P, SLOTS, N], bf16)
        ohd = sb("onehot_dst", [P, SLOTS, 4 * WIN], bf16)
        stage = sb("stage", [128, 2, N])
        ps = k.ps

        edges_in, consts_in, minmax_in, tab_in = (sem(n) for n in ("edges_in", "consts_in", "minmax_in", "tab_in"))
        steps, minmax_ready, iota_done = sem("table_steps"), sem("minmax_ready"), sem("iota_done")
        lens_ready, before_ready, table_ready = sem("lens_ready"), sem("before_ready"), sem("table_ready")

        with nc.Block() as block:
            @block.sync
            def _(sp):
                sp.dma_start(dr[:, :, :], dst_rows).then_inc(edges_in, 16)
                sp.dma_start(ei[:, 0, :], src_pt).then_inc(edges_in, 16)
                sp.dma_start(ei[:, 1, :], dst_pt).then_inc(edges_in, 16)
                sp.dma_start(wF[:, 0, :], w_pt).then_inc(edges_in, 16)
                sp.dma_start(sel[:, :], k.c_sel).then_inc(consts_in, 16)
                sp.dma_start(tl[:, 0:2], k.c_win).then_inc(consts_in, 16)
                sp.wait_ge(minmax_ready, 2)
                sp.dma_start(scr_minmax.rearrange("m (p q) -> p m q", q=4), mm[:, :, :]).then_inc(minmax_in, 16)
                sp.wait_ge(minmax_in, 16)
                sp.dma_start(mb[:, :, :], scr_minmax.partition_broadcast(NW)).then_inc(minmax_in, 16)
                sp.wait_ge(table_ready, 4)
                sp.dma_start(scr_tab, tf[:, :]).then_inc(tab_in, 16)
                sp.wait_ge(tab_in, 16)
                sp.dma_start(tab[:, :], scr_tab.rearrange("(o w) c -> o (w c)", o=1)).then_inc(tab_in, 16)
                sp.wait_ge(tab_in, 32)

            @block.gpsimd
            def _(pool):
                pool.iota(ioi[:, :], [[1, N]], base=0, channel_multiplier=0).then_inc(iota_done, 1)
                pool.iota(iot[:, :], [[1, ET]], base=0, channel_multiplier=0,
                          allow_small_or_imprecise_dtypes=True).then_inc(iota_done, 1)

            @block.tensor
            def _(pe):
                pe.wait_ge(lens_ready, 1)
                pe.matmul(ps[0:NW, 0, 0:1], k.tri[0:NW, 0:NW], tl[:, 6:7], start=True, stop=True)\
                    .then_inc(before_ready, 1)

            @block.vector
            def _(v):
                v.wait_ge(edges_in, 64)
                v.tensor_reduce(mm[:, 0, :], dr[:, :, :], AX.X, ALU.min).then_inc(minmax_ready, 1)
                v.tensor_reduce(mm[:, 1, :], dr[:, :, :], AX.X, ALU.max).then_inc(minmax_ready, 1)
                s = Steps(v, steps)
                s.did(v.memset(dF[:, ET:ETP], -1.0))
                s.did(v.memset(sF[:, ET:ETP], 0.0))
                s.did(v.memset(tf[:, 3:4], 0))
                s.did(v.memset(wp[:, :, :], 0.0))
                s.wait()
                s.did(v.memset(wp[:, 0:ET, 0:1], 1.0))
                s.did(v.tensor_copy(sF[:, 0:ET], ei[:, 0, :]))
                s.did(v.tensor_copy(dF[:, 0:ET], ei[:, 1, :]))
                s.did(v.tensor_copy(wp[:, 0:ET, 1], wF[:, 0, :]))
                s.wait()
                s.did(v.tensor_tensor(wF[:, 1, :], wF[:, 0, :], wp[:, 0:ET, 1], ALU.subtract))
                s.wait()
                s.did(v.tensor_copy(wp[:, 0:ET, 2], wF[:, 1, :]))
                s.wait()
                s.did(v.tensor_tensor(wF[:, 2, :], wF[:, 1, :], wp[:, 0:ET, 2], ALU.subtract))
                s.wait()
                s.did(v.tensor_copy(wp[:, 0:ET, 3], wF[:, 2, :]))
                v.wait_ge(iota_done, 2)
                s.did(v.memset(io16[:, N:], 2000.0))
                s.did(v.tensor_copy(io16[:, 0:N], ioi[:, :]))
                v.wait_ge(minmax_in, 32)
                v.wait_ge(consts_in, 32)
                s.did(v.tensor_scalar(ov[:, 0, :], mb[:, 0, :], tl[:, 1:2], None, ALU.is_le))
                s.wait()
                s.did(v.scalar_tensor_tensor(ov[:, 1, :], mb[:, 1, :], tl[:, 0:1], ov[:, 0, :],
                                             ALU.is_ge, ALU.mult))
                s.wait()
                s.did(v.scalar_tensor_tensor(ov[:, 2, :], ov[:, 1, :], -1000.0, iot[:, :], ALU.mult, ALU.add))
                s.did(v.scalar_tensor_tensor(ov[:, 0, :], iot[:, :], 1.0, ov[:, 1, :], ALU.add, ALU.mult))
                s.wait()
                s.did(v.tensor_reduce(tl[:, 2:3], ov[:, 2, :], AX.X, ALU.min))
                s.did(v.tensor_reduce(tl[:, 3:4], ov[:, 0, :], AX.X, ALU.max))
                s.wait()
                s.did(v.tensor_scalar(tl[:, 4:5], tl[:, 2:3], 1000.0, float(ET - 1), ALU.add, ALU.min))
                s.wait()
                s.did(v.tensor_tensor(tl[:, 5:6], tl[:, 3:4], tl[:, 4:5], ALU.subtract))
                s.wait()
                s.did(v.tensor_scalar(ti[:, 0:1], tl[:, 5:6], 1.0, float(RUN - 2), ALU.max, ALU.add))
                s.wait()
                s.did(v.tensor_scalar(ti[:, 1:2], ti[:, 0:1], RUN.bit_length() - 1, None, ALU.arith_shift_right))
                s.wait()
                v.tensor_scalar(tf[:, 1:2], ti[:, 1:2], 1.0, None, ALU.max).then_inc(table_ready, 1)
                v.tensor_copy(tf[:, 0:1], tl[:, 4:5]).then_inc(table_ready, 1)
                v.wait_ge(table_ready, 2)
                v.tensor_scalar(tl[:, 6:7], tf[:, 1:2], float(RUN), 1.0, ALU.mult, ALU.add).then_inc(lens_ready, 1)
                v.wait_ge(before_ready, 1)
                v.tensor_copy(tf[:, 2:3], ps[0:NW, 0, 0:1]).then_inc(table_ready, 1)
                v.wait_ge(table_ready, 3)
                s.did(v.tensor_scalar(ti[:, 2:3], tf[:, 2:3], 17, None, ALU.logical_shift_left))
                s.did(v.tensor_scalar(ti[:, 3:4], tf[:, 0:1], 8, None, ALU.logical_shift_left))
                s.wait()
                s.did(v.tensor_tensor(ti[:, 2:3], ti[:, 2:3], ti[:, 3:4], ALU.bitwise_or))
                s.wait()
                v.tensor_tensor(tf[:, 3:4], ti[:, 2:3], tf[:, 1:2], ALU.bitwise_or).then_inc(table_ready, 1)

        onehots_ready, onehots_used = sem("onehots_ready"), sem("onehots_used")
        window_summed, window_staged = sem("window_summed"), sem("window_staged")
        parts_added, parts_out = sem("parts_added"), sem("parts_out")
        SPLIT = ((0, 5), (5, 5))

        def window(eng, w):
            entry = eng.snap(eng.value_load(tab[0:1, bass.ds(w * 4 + 3, 1)], min_val=0, max_val=2 ** 31 - 1))
            known = "a window's entry holds numbers in these ranges"
            return (nc.s_assert_within(eng.snap((entry >> 8) & 511), 0, ET - 1,
                                       skip_runtime_bounds_check_because=known),
                    nc.s_assert_within(eng.snap(entry & 255), 1, ET // RUN, skip_runtime_bounds_check_because=known),
                    nc.s_assert_within(eng.snap(entry >> 17), 0, NW * (ET + 1),
                                       skip_runtime_bounds_check_because=known))

        with nc.Block() as block:
            @block.sync
            def _(sp):
                beside(sp)

            @block.vector
            def _(v):
                def onehots(tile, nth, base):
                    slot = bass.ds(nth % SLOTS, 1)
                    tile = nc.s_assert_within(tile, 0, ETP - 1,
                                              skip_runtime_bounds_check_because="a run starts at tile ET at the latest")
                    v.wait_ge(onehots_used, nth + 1)
                    v.tensor_scalar(ohs[:, slot, :].rearrange("p o n -> p (o n)"), io16[:, 0:N], sF[:, bass.ds(tile, 1)], None, ALU.is_equal)
                    v.scalar_tensor_tensor(
                        ohd[:, slot, :].rearrange("p o (a b) -> p (o a) b", a=4),
                        io16[:, bass.ds(base, WIN)].unsqueeze(1).broadcast_to([P, 4, WIN]),
                        dF[:, bass.ds(tile, 1)],
                        wp[:, bass.ds(tile, 1), :].rearrange("p o f -> p (o f)").unsqueeze(2).broadcast_to([P, 4, WIN]),
                        ALU.is_equal, ALU.mult).then_inc(onehots_ready, 1)

                with v.Fori(0, T) as i:
                    for j in range(WPT):
                        first, runs, before = window(v, i * WPT + j)
                        base = i * P + j * WIN
                        onehots(first, before, base)
                        with v.Fori(0, runs) as q:
                            for h in range(RUN):
                                onehots(first + RUN * q + (1 + h), before + RUN * q + (1 + h), base)

            @block.tensor
            def _(pe):
                pe.sem_inc(onehots_used, SLOTS)

                def add_tile(half, nth, start):
                    slot = bass.ds(nth % SLOTS, 1)
                    pe.wait_ge(onehots_ready, nth + 1)
                    for c, (c0, cn) in enumerate(CH):
                        mm_ = pe.matmul(ps[:, 3 * half + c, 0:cn], ohd[:, slot, :].rearrange("p o n -> p (o n)"),
                                        ohs[:, slot, c0:c0 + cn].rearrange("p o n -> p (o n)"), start=start, stop=True, skip_group_check=True)
                    mm_.then_inc(onehots_used, 1)

                def add_parts(i, j):
                    w = i * WPT + j
                    pe.wait_ge(window_staged, w + 3)
                    pe.wait_ge(parts_out, w * 4 + 4)
                    for b, (s0, sn) in enumerate(SPLIT):
                        for s_ in range(sn):
                            t = s0 + s_
                            mm_ = pe.matmul(ps[0:P, 6 + b, 64 * s_:64 * s_ + 64],
                                            stage[:, j % 2, P * t:P * t + P], sel[:, :], start=True, stop=True,
                                            skip_group_check=True)
                    mm_.then_inc(parts_added, 1)

                with pe.Fori(0, T) as i:
                    for j in range(WPT):
                        w = i * WPT + j
                        first, runs, before = window(pe, w)
                        pe.wait_ge(window_staged, w + 1)
                        add_tile(j % 2, before, True)
                        with pe.Fori(0, runs) as q:
                            for h in range(RUN):
                                add_tile(j % 2, before + RUN * q + (1 + h), False)
                        pe.drain().then_inc(window_summed, 1)
                        if j:
                            add_parts(i, j - 1)
                    add_parts(i, WPT - 1)

            @block.scalar
            def _(act):
                act.sem_inc(window_staged, 2)
                act.sem_inc(parts_out, 4)

                def stage_window(i, j):
                    act.wait_ge(window_summed, i * WPT + j + 1)
                    h = j % 2
                    act.activation(stage[:, h, 0:1000].rearrange("p (c n) -> p c n", c=2),
                                   ps[:, 3 * h:3 * h + 2, 0:500], ACT.Copy)
                    act.activation(stage[:, h, 1000:N], ps[:, 3 * h + 2, 0:250], ACT.Copy).then_inc(window_staged, 1)

                def parts_to_columns(i, j):
                    act.wait_ge(parts_added, i * WPT + j + 1)
                    n = min(WIN, P - j * WIN)
                    for b, (s0, sn) in enumerate(SPLIT):
                        for half, mat in enumerate((CT, WT)):
                            act.activation(mat[:, s0:s0 + sn, bass.ds(i * P + j * WIN, n)],
                                           ps[0:P, 6 + b, 0:64 * sn].rearrange("p (s n) -> p s n", n=64)
                                           [:, :, WIN * half:WIN * half + n], ACT.Copy).then_inc(parts_out, 1)

                with act.Fori(0, T) as i:
                    for j in range(WPT):
                        stage_window(i, j)
                        if j:
                            parts_to_columns(i, j - 1)
                    parts_to_columns(i, WPT - 1)


class Kit:

    def __init__(self):
        self.names = 0
        self.used_semaphores = []
        self.lasting = None

    def name(self, base):
        self.names += 1
        return f"{base}_{self.names}"


    def gpsimd_dma_semaphore(self, nc, name):
        return self.lasting.enter_context(nc.semaphore(self.name(name)))

    @contextmanager
    def semaphore(self, nc, name):
        with nc.semaphore(name) as s:
            yield s
        self.used_semaphores.append(s)

    def clear_semaphores(self, nc):
        todo, self.used_semaphores = self.used_semaphores, []
        with nc.Block() as block:
            @block.gpsimd
            def _(pool):
                for s in todo:
                    pool.sem_clear(s)
def loads_beside(block, sem, pairs):
    if pairs:
        @block.sync
        def _(sp):
            for dst, src in pairs:
                sp.dma_start(dst, src).then_inc(sem, 16)
            sp.wait_ge(sem, 16 * len(pairs))


def in_two(dst, src):
    return [(dst[0:120], src[0:120]), (dst[120:P], src[120:P])]


def norm_rows(nc, k, x, xn, xT=None, affine=None, eps=1e-5, beside=(), have_stats=False):
    with ExitStack() as ctx:
        def sb(name, shape, dt=fp32):
            return ctx.enter_context(nc.sbuf_tensor(k.name(name), shape, dt))

        def sem(name):
            return ctx.enter_context(k.semaphore(nc, k.name(name)))

        st = k.stats
        mv = sb("mean_var", [P, T, 2])
        sd = sb("std", [P, T])
        rs = sb("rstd", [P, T])
        stats, var_ready, std_ready, inv_ready = sem("stats"), sem("var_ready"), sem("std_ready"), sem("inv_ready")
        rows_ready, transposed, copied = sem("rows_ready"), sem("transposed"), sem("copied")
        loaded = sem("loaded")
        with nc.Block() as block:
            loads_beside(block, loaded, beside)

            @block.vector
            def _(v):
                if not have_stats:
                    for i in range(T):
                        v.bn_stats(st[:, i, :], x[:, i, :]).then_inc(stats, 1)
                    v.wait_ge(stats, T)
                for i in range(T):
                    v.bn_aggr(mv[:, i, :], st[:, i, :]).then_inc(stats, 1)
                v.wait_ge(stats, T if have_stats else 2 * T)
                v.tensor_scalar(sd[:, :], mv[:, :, 1], eps, None, ALU.add).then_inc(var_ready, 1)
                v.wait_ge(std_ready, 1)
                v.reciprocal(rs[:, :], sd[:, :]).then_inc(inv_ready, 1)
                v.wait_ge(inv_ready, 1)
                for i in range(T):
                    v.tensor_scalar(xn[:, i, :], x[:, i, :], mv[:, i, 0:1], rs[:, i:i + 1], ALU.subtract, ALU.mult)\
                        .then_inc(rows_ready, 1)

            @block.scalar
            def _(act):
                act.wait_ge(var_ready, 1)
                act.activation(sd[:, :], sd[:, :], ACT.Sqrt).then_inc(std_ready, 1)
                if xT is not None:
                    copy_transposed(act, k, xT, transposed, copied, affine)

            if xT is not None:
                @block.tensor
                def _(pe):
                    transpose_rows(pe, k, xn, transposed, copied, rows_ready)


def transpose_rows(pe, k, xn, transposed, copied, rows_ready=None):
    g = 0
    for c0, cn in CH:
        if rows_ready is not None:
            pe.wait_ge(rows_ready, (c0 + cn) // P)
        for c in range(C):
            if g >= 8:
                pe.wait_ge(copied, g - 7)
            for t in range(c0 // P, (c0 + cn) // P):
                mm = pe.transpose(k.ps[:, g % 8, P * t - c0:P * t - c0 + P], xn[:, t, 128 * c:128 * c + 128],
                                  k.ident[0:P, 0:P])
            mm.then_inc(transposed, 1)
            g += 1


def copy_transposed(act, k, xT, transposed, copied, affine=None):
    g = 0
    for c0, cn in CH:
        for c in range(C):
            act.wait_ge(transposed, g + 1)
            if affine is None:
                act.activation(xT[:, c, c0:c0 + cn], k.ps[:, g % 8, 0:cn], ACT.Copy).then_inc(copied, 1)
            else:
                act.activation(xT[:, c, c0:c0 + cn], k.ps[:, g % 8, 0:cn], ACT.Identity,
                               bias=affine[1][:, c:c + 1], scale=affine[0][:, c:c + 1]).then_inc(copied, 1)
            g += 1


def transpose_only(nc, k, xn, xT, beside=()):
    with k.semaphore(nc, k.name("loaded")) as loaded, k.semaphore(nc, k.name("transposed")) as transposed, \
            k.semaphore(nc, k.name("copied")) as copied:
        with nc.Block() as block:
            loads_beside(block, loaded, beside)

            @block.tensor
            def _(pe):
                transpose_rows(pe, k, xn, transposed, copied)

            @block.scalar
            def _(act):
                copy_transposed(act, k, xT, transposed, copied)


def load(nc, k, pairs):
    with k.semaphore(nc, k.name("loaded")) as loaded:
        with nc.Block() as block:
            @block.sync
            def _(sp):
                for dst, src in pairs:
                    sp.dma_start(dst, src).then_inc(loaded, 16)
                sp.wait_ge(loaded, 16 * len(pairs))


def stats_behind(v, k, x, i, done):
    if i:
        v.wait_ge(done, i)
        v.bn_stats(k.stats[:, i - 1, :], x[:, i - 1, :])


def rows_product(nc, k, terms, bias, finish, stats_of=None, biased=None):
    (engine, take), = finish.items()
    with k.semaphore(nc, k.name("summed")) as summed, k.semaphore(nc, k.name("taken")) as taken, \
            k.semaphore(nc, k.name("bias_added")) as bias_added:
        with nc.Block() as block:
            @block.tensor
            def _(pe):
                for i in range(T):
                    if i >= 8:
                        pe.wait_ge(taken, i - 7)
                    todo = [(lhsT[:, c, P * i:P * i + P], rhs[:, c, :]) for lhsT, rhs, n in terms for c in range(n)]
                    for n, (l, r) in enumerate(todo):
                        mm = pe.matmul(k.ps[0:P, i % 8, :], l, r, start=(n == 0), stop=(n == len(todo) - 1))
                    mm.then_inc(summed, 1)

            def takes(eng):
                for i in range(T):
                    eng.wait_ge(summed, i + 1)
                    psum = k.ps[0:P, i % 8, :]
                    if bias is not None:
                        eng.tensor_tensor(biased[:, i % 2, :], psum, bias[:, :], ALU.add).then_inc(bias_added, 1)
                        eng.wait_ge(bias_added, i + 1)
                        psum = biased[:, i % 2, :]
                    take(eng, i, psum).then_inc(taken, 1)
                    if stats_of is not None:
                        stats_behind(eng, k, stats_of, i, taken)
                if stats_of is not None:
                    stats_behind(eng, k, stats_of, T, taken)

            if engine == "scalar":
                block.scalar(takes)
            else:
                block.vector(takes)


def columns_product(nc, k, terms, mchunks, take, reuse=None, beside=(), vector=None):
    with k.semaphore(nc, k.name("summed")) as summed, k.semaphore(nc, k.name("taken")) as taken, \
            k.semaphore(nc, k.name("loaded")) as loaded:
        with nc.Block() as block:
            loads_beside(block, loaded, beside)

            @block.tensor
            def _(pe):
                g = 0
                for m in range(mchunks):
                    for c0, cn in CH:
                        if g >= 8:
                            pe.wait_ge(taken, g - 7)
                        todo = [(lhsT[:, c, 128 * m:128 * m + 128], rhs[:, c, c0:c0 + cn])
                                for lhsT, rhs, chunks in terms for c in range(chunks)]
                        for i, (l, r) in enumerate(todo):
                            mm = pe.matmul(k.ps[:, g % 8, 0:cn], l, r, start=(i == 0), stop=(i == len(todo) - 1))
                        mm.then_inc(summed, 1)
                        g += 1

            if vector is not None:
                @block.vector
                def _(v):
                    vector(v)

            @block.scalar
            def _(act):
                g = 0
                for m in range(mchunks):
                    for n, (c0, cn) in enumerate(CH):
                        if reuse is not None and g >= reuse:
                            act.wait_ge(taken, g - reuse + 1)
                        act.wait_ge(summed, g + 1)
                        take(act, m, (c0, cn), n, k.ps[:, g % 8, 0:cn]).then_inc(taken, 1)
                        g += 1


def copy_rows(out, func=None):
    return {"scalar": lambda act, i, psum: act.activation(out[:, i, :], psum, func or ACT.Copy)}


def add_rows(out, base=None):
    return {"vector": lambda v, i, psum: v.tensor_tensor(out[:, i, :], (out if base is None else base)[:, i, :],
                                                         psum, ALU.add)}


def split(nc, k, pairs):
    with k.semaphore(nc, k.name("hi")) as hi_done:
        with nc.Block() as block:
            @block.scalar
            def _(act):
                for x, hi, lo in pairs:
                    for c in range(x.shape[1]):
                        act.activation(hi[:, c, :], x[:, c, :], ACT.Copy).then_inc(hi_done, 1)

            @block.vector
            def _(v):
                n = 0
                for x, hi, lo in pairs:
                    for c in range(x.shape[1]):
                        n += 1
                        v.wait_ge(hi_done, n)
                        v.tensor_tensor(lo[:, c, :], x[:, c, :], hi[:, c, :].bitcast(fp32), ALU.subtract)


def three_terms(l, r, chunks):
    return [(l[0], r[0], chunks), (l[0], r[1], chunks), (l[1], r[0], chunks)]


def matrix_slabs(view):
    S = T * D // N
    return view[:, :, :].rearrange("p t d -> p (t d)")[:, 0:S * N].rearrange("p (s n) -> p s n", s=S)


def linear_split(nc, k, lhsT, w, bias, y, matrix=None, beside=()):
    with ExitStack() as ctx:
        def sem(name):
            return ctx.enter_context(k.semaphore(nc, k.name(name)))
        summed, y_hi, taken, loaded = sem("summed"), sem("y_hi"), sem("taken"), sem("loaded")
        g_hi, slab_used, bias_added = sem("g_hi"), sem("slab_used"), sem("bias_added")

        def full(i):
            return k.ps[0:P, i % 8, :] if bias is None else bias[1][:, i % 2, :]
        if matrix is not None:
            dram, G, slabs = matrix
            S = slabs.shape[1]
            slab_in = [sem("slab_in") for _ in range(S)]
        with nc.Block() as block:
            @block.sync
            def _(sp):
                if matrix is not None:
                    for t in range(T):
                        if t >= S:
                            sp.wait_ge(slab_used, t - S + 1)
                        for r0, r1 in ((0, 120), (120, P)):
                            sp.dma_start(slabs[r0:r1, t % S, :], dram[P * t + r0:P * t + r1, :])\
                                .then_inc(slab_in[t % S], 16)
                for dst, src in beside:
                    sp.dma_start(dst, src).then_inc(loaded, 16)
                if beside:
                    sp.wait_ge(loaded, 16 * len(beside))

            @block.tensor
            def _(pe):
                for i in range(T):
                    if i >= 8:
                        pe.wait_ge(taken, i - 7)
                    for c in range(C):
                        mm = pe.matmul(k.ps[0:P, i % 8, :], lhsT[:, c, P * i:P * i + P], w[:, c, :], start=(c == 0),
                                       stop=(c == C - 1))
                    mm.then_inc(summed, 1)

            @block.scalar
            def _(act):
                for i in range(T):
                    if matrix is not None:
                        act.wait_ge(slab_in[i % S], 32 * (i // S + 1))
                        act.activation(G[0][:, i, :], slabs[:, i % S, :], ACT.Copy).then_inc(g_hi, 1)
                    act.wait_ge(summed if bias is None else bias_added, i + 1)
                    act.activation(y[0][:, i, :], full(i), ACT.Copy).then_inc(y_hi, 1)

            @block.vector
            def _(v):
                for i in range(T):
                    if matrix is not None:
                        v.wait_ge(g_hi, i + 1)
                        v.tensor_tensor(G[1][:, i, :], slabs[:, i % S, :], G[0][:, i, :].bitcast(fp32), ALU.subtract)\
                            .then_inc(slab_used, 1)
                    if bias is not None:
                        v.wait_ge(summed, i + 1)
                        v.tensor_tensor(full(i), k.ps[0:P, i % 8, :], bias[0][:, :], ALU.add).then_inc(bias_added, 1)
                    v.wait_ge(y_hi, i + 1)
                    v.tensor_tensor(y[1][:, i, :], full(i), y[0][:, i, :].bitcast(fp32), ALU.subtract)\
                        .then_inc(taken, 1)


def values(nc, k, x1, wraw, braw, V):
    with ExitStack() as ctx:
        def sb(name, shape, dt=fp32):
            return ctx.enter_context(nc.sbuf_tensor(k.name(name), shape, dt))
        wp = sb("wv_hi", [128, C, D], f32r), sb("wv_lo", [128, C, D], f32r)
        terms, parts = three_terms(x1, wp, C), [(wraw, *wp)]
        if braw is not None:
            bp = sb("bv_hi", [1, 1, D], f32r), sb("bv_lo", [1, 1, D], f32r)
            one = sb("one_v", [1, 1, N], f32r)
            terms += [(one, bp[0], 1), (one, bp[1], 1)]
            parts.append((braw, *bp))
        split(nc, k, parts)
        if braw is not None:
            with nc.Block() as block:
                @block.vector
                def _(v):
                    v.memset(one[:, :, :].bitcast(fp32), 1.0)
        rows_product(nc, k, terms, None, copy_rows(V))


def attention(nc, k, x1, w_qk, b_qk, Vall, ctxT, room):
    H, DH = 8, 64
    HALF, PIECE = 5, 250
    SCALE = DH ** -0.5
    with ExitStack() as ctx:
        def sb(name, shape, dt=fp32):
            return ctx.enter_context(nc.sbuf_tensor(k.name(name), shape, dt))

        def sem(name):
            return ctx.enter_context(k.semaphore(nc, k.name(name)))

        def pair(name, shape):
            return sb(name + "_hi", shape, f32r), sb(name + "_lo", shape, f32r)

        wraw = room(128, (C, 128))
        wph, wpl = pair("w", [128, C, 128])
        braw = sb("b_raw", [1, 128])
        bh, bl = pair("b", [1, 128])
        one = sb("one_r", [1, 500], f32r)
        QT, KT = pair("QT", [DH + 1, 2, N]), pair("KT", [DH + 1, 2, N])
        V = sb("V", [P, T, 128])
        PT = sb("probs", [P, 2, N])
        cu = room(128, (N,))
        inv = room(DH, (2, PIECE))
        mx, mr, negm = sb("mx", [P, T, 3]), sb("mr", [P, T]), sb("negm", [P, T])
        w_in, w_hi, w_split, ones_set = sem("w_in"), sem("w_hi"), sem("w_split"), sem("ones_set")
        proj_done, v_in, s_done, row_done = sem("proj_done"), sem("v_in"), sem("s_done"), sem("row_done")
        st_done, pv_done, qk_hi, row_hi = (sem(n) for n in ("st_done", "pv_done", "qk_hi", "row_hi"))
        s_out, p_out, qk_lo, ctx_out = (sem(n) for n in ("s_out", "p_out", "qk_lo", "ctx_out"))
        row_lo, negm_ready, inv_ready, norm_out = (sem(n) for n in ("row_lo", "negm_ready", "inv_ready",
                                                                    "norm_out"))
        max_steps = sem("max_steps")
        ps = k.ps
        ACC, ST, SQ = 0, 3, 6
        ROW = [ps[DH:DH + 1, SQ, 0:500], ps[DH:DH + 1, SQ + 1, 0:500], ps[0:1, SQ, 0:250]]
        bias = b_qk is not None
        LOADS = 32 if bias else 16

        def three(pe, out, l, r, start, stop):
            pe.matmul(out, l[0], r[0], start=start, stop=False)
            pe.matmul(out, l[0], r[1], start=False, stop=False)
            return pe.matmul(out, l[1], r[0], start=False, stop=stop)

        def schedule(eng, tiles, between):
            first, second = range(HALF), range(HALF, T)
            tiles(0, 0, first, True, True)
            with eng.Fori(0, H // 2 - 1) as i:
                for j in range(2):
                    tiles(i * 2 + j, j, second, True, True)
                    between(i * 2 + j, j, bass.ds(i, 1), True, True)
                    tiles(i * 2 + (j + 1), 1 - j, first, True, True)
            tiles(H - 2, 0, second, True, False)
            between(H - 2, 0, slice(H // 2 - 1, H // 2), True, False)
            tiles(H - 1, 1, first, False, False)
            tiles(H - 1, 1, second, False, False)
            between(H - 1, 1, slice(H // 2 - 1, H // 2), False, False)

        with nc.Block() as block:
            @block.sync
            def _(sp):
                def load_weights(h, wait):
                    sp.wait_ge(w_split, wait)
                    sp.dma_start(wraw[:, :, :], w_qk[bass.ds(h, 1)].rearrange("o p c n -> p (o c) n"))\
                        .then_inc(w_in, 16)
                    if bias:
                        sp.dma_start(braw[:, :], b_qk[bass.ds(h, 1), :]).then_inc(w_in, 16)
                load_weights(0, 1)
                with sp.Fori(1, H) as h:
                    load_weights(h, h + 1)

            @block.tensor
            def _(pe):
                pe.sem_inc(pv_done, 1)
                pe.wait_ge(ones_set, 4)

                def project(h, between=lambda: None):
                    pe.wait_ge(w_split, h + 2)
                    for n, (c0, cn) in enumerate(CH):
                        o = ps[:, ST + n, 0:cn]
                        for c in range(C):
                            mm = three(pe, o, (wph[:, c, :], wpl[:, c, :]), [x[:, c, c0:c0 + cn] for x in x1],
                                       c == 0, c == C - 1 and not bias)
                            if c == C - 1 and not bias:
                                mm.then_inc(proj_done, 1)
                            between()
                        if bias:
                            pe.matmul(o, bh[:, :], one[0:1, 0:cn], start=False, stop=False)
                            pe.matmul(o, bl[:, :], one[0:1, 0:cn], start=False, stop=True).then_inc(proj_done, 1)

                def score(h, j, cc):
                    t, (c0, cn) = cc // 3, CH[cc % 3]
                    if cc >= 2:
                        pe.wait_ge(s_out, h * 30 + (cc - 1))
                    pe.matmul(ps[0:P, SQ + cc % 2, 0:cn], QT[0][0:DH, j, P * t:P * t + P],
                              KT[0][0:DH, j, c0:c0 + cn], start=True, stop=True).then_inc(s_done, 1)

                def score_t(h, j, t, n):
                    c0, cn = CH[n]
                    if t >= 1:
                        pe.wait_ge(p_out, h * 30 + (3 * t + n - 2))
                    three(pe, ps[0:P, ST + n, 0:cn], [x[:, j, P * t:P * t + P] for x in KT],
                          [x[:, j, c0:c0 + cn] for x in QT], True, True).then_inc(st_done, 1)

                def times_v(h, t, n):
                    c0, cn = CH[n]
                    if n == 0:
                        pe.wait_ge(p_out, h * 30 + (3 * t + 3))
                    mm = pe.matmul(ps[:, ACC + n, 0:cn], V[:, t, :], PT[:, t % 2, c0:c0 + cn],
                                   start=(t == 0), stop=(t == T - 1))
                    if n == 2:
                        mm.then_inc(pv_done, 1)

                def minus_max(h):
                    pe.wait_ge(negm_ready, h + 1)
                    for n, (c0, cn) in enumerate(CH):
                        for t in range(c0 // P, (c0 + cn) // P):
                            mm = pe.matmul(ROW[n][:, P * t - c0:P * t - c0 + P], negm[:, t:t + 1],
                                           k.ident[0:P, 0:P], start=True, stop=True)
                        mm.then_inc(row_done, 1)

                def tiles(h, j, those, has_next, has_second):
                    for t in those:
                        if t == 0:
                            ready = h * 6 + 12 if has_next else H * 6
                            pe.wait_ge(qk_hi, ready)
                            pe.wait_ge(qk_lo, ready)
                            pe.wait_ge(row_hi, h * 3 + 3)
                            pe.wait_ge(row_lo, h * 3 + 3)
                        for n in range(3):
                            score_t(h, j, t, n)
                            if has_next and n < 2:
                                score(h + 1, 1 - j, 3 * t + n)
                        if t == 1:
                            pe.wait_ge(ctx_out, h * 3 + 1)
                            pe.wait_ge(v_in, h + 1)
                        for n in range(3):
                            if t:
                                times_v(h, t - 1, n)
                            if has_next and n == 0:
                                score(h + 1, 1 - j, 3 * t + 2)

                def between(h, j, chunk, has_next, has_second):
                    for n in range(3):
                        times_v(h, T - 1, n)
                    if has_next:
                        minus_max(h + 1)
                    if has_second:
                        project(h + 2)

                project(0)
                pe.wait_ge(qk_hi, 6)
                pe.wait_ge(qk_lo, 6)
                todo = iter(range(3 * T))

                def next_scores(n=2):
                    for _ in range(n):
                        score(0, 0, next(todo))
                next_scores(3 * T - 2 * len(CH) * C)
                project(1, next_scores)
                minus_max(0)
                schedule(pe, tiles, between)

            @block.scalar
            def _(act):
                act.sem_inc(ctx_out, 1)

                def split_hi(h, through):
                    if through is not None:
                        act.wait_ge(proj_done, through)
                    act.wait_ge(w_in, h * LOADS + LOADS)
                    act.activation(wph[:, :, :], wraw[:, :, :], ACT.Copy).then_inc(w_hi, 1)
                    if bias:
                        act.activation(bh[:, :], braw[:, :], ACT.Copy).then_inc(w_hi, 1)

                def take_projections(h, j):
                    for n, (c0, cn) in enumerate(CH):
                        act.wait_ge(proj_done, h * 3 + (n + 1))
                        act.activation(QT[0][0:DH, j, c0:c0 + cn], ps[0:DH, ST + n, 0:cn], ACT.Copy)\
                            .then_inc(qk_hi, 1)
                        act.activation(KT[0][0:DH, j, c0:c0 + cn], ps[DH:128, ST + n, 0:cn], ACT.Copy)\
                            .then_inc(qk_hi, 1)

                def take_row(h, j):
                    for n, (c0, cn) in enumerate(CH):
                        act.wait_ge(row_done, h * 3 + (n + 1))
                        act.activation(QT[0][DH:DH + 1, j, c0:c0 + cn], ROW[n], ACT.Copy).then_inc(row_hi, 1)

                def tiles(h, j, those, has_next, has_second):
                    for t in those:
                        act.wait_ge(pv_done, h * T + (max(t - 1, 0) + 1))
                        for n, (c0, cn) in enumerate(CH):
                            act.wait_ge(st_done, h * 30 + (3 * t + n + 1))
                            act.activation(PT[:, t % 2, c0:c0 + cn], ps[0:P, ST + n, 0:cn], ACT.Exp,
                                           scale=SCALE).then_inc(p_out, 1)
                        if t == HALF and has_second:
                            split_hi(h + 2, h * 3 + 6)

                def between(h, j, chunk, has_next, has_second):
                    act.wait_ge(norm_out, h * HALF + 1)
                    act.wait_ge(pv_done, h * T + (T + 1))
                    for n, (c0, cn) in enumerate(CH):
                        act.activation(cu[:, c0:c0 + cn], ps[:, ACC + n, 0:cn], ACT.Copy).then_inc(ctx_out, 1)
                    if has_next:
                        take_row(h + 1, 1 - j)
                    if has_second:
                        take_projections(h + 2, j)

                for h in range(2):
                    split_hi(h, 3 if h else None)
                    take_projections(h, h)
                take_row(0, 0)
                schedule(act, tiles, between)

            @block.vector
            def _(v):
                v.sem_inc(w_split, 1)
                v.sem_inc(norm_out, 1)
                v.memset(KT[0][DH:DH + 1, :, :].bitcast(fp32), 1.0).then_inc(ones_set, 1)
                v.memset(KT[1][DH:DH + 1, :, :].bitcast(fp32), 0.0).then_inc(ones_set, 1)
                v.memset(V[:, :, DH:128], 1.0).then_inc(ones_set, 1)
                v.memset(one[:, :].bitcast(fp32), 1.0).then_inc(ones_set, 1)

                def take_projections(h, j):
                    for n, (c0, cn) in enumerate(CH):
                        v.wait_ge(qk_hi, h * 6 + (2 * n + 2))
                        v.tensor_tensor(QT[1][0:DH, j, c0:c0 + cn], ps[0:DH, ST + n, 0:cn],
                                        QT[0][0:DH, j, c0:c0 + cn].bitcast(fp32), ALU.subtract).then_inc(qk_lo, 1)
                        v.tensor_tensor(KT[1][0:DH, j, c0:c0 + cn], ps[DH:128, ST + n, 0:cn],
                                        KT[0][0:DH, j, c0:c0 + cn].bitcast(fp32), ALU.subtract).then_inc(qk_lo, 1)

                def split_lo(h):
                    parts = 2 if bias else 1
                    v.wait_ge(w_hi, h * parts + parts)
                    if bias:
                        v.tensor_tensor(bl[:, :], braw[:, :], bh[:, :].bitcast(fp32), ALU.subtract)
                    v.tensor_tensor(wpl[:, :, :], wraw[:, :, :], wph[:, :, :].bitcast(fp32), ALU.subtract)\
                        .then_inc(w_split, 1)

                def take_v(h):
                    v.tensor_copy(V[:, :, 0:DH], Vall[:, :, bass.ds(h * DH, DH)]).then_inc(v_in, 1)

                def maxima(h, t):
                    for n, (c0, cn) in enumerate(CH):
                        cc = 3 * t + n
                        v.wait_ge(s_done, h * 30 + (cc + 1))
                        v.tensor_reduce(mx[:, t, n:n + 1], ps[0:P, SQ + cc % 2, 0:cn], AX.X, ALU.max)\
                            .then_inc(s_out, 1)

                def negate(h):
                    v.wait_ge(s_out, h * 30 + 30)
                    v.tensor_reduce(mr[:, :], mx[:, :, :], AX.X, ALU.max).then_inc(max_steps, 1)
                    v.wait_ge(max_steps, h + 1)
                    v.tensor_scalar(negm[:, :], mr[:, :], -1.0, None, ALU.mult).then_inc(negm_ready, 1)

                def take_row(h, j):
                    for n, (c0, cn) in enumerate(CH):
                        v.wait_ge(row_hi, h * 3 + (n + 1))
                        v.tensor_tensor(QT[1][DH:DH + 1, j, c0:c0 + cn], ROW[n],
                                        QT[0][DH:DH + 1, j, c0:c0 + cn].bitcast(fp32), ALU.subtract)\
                            .then_inc(row_lo, 1)

                def finish(h, j, chunk, m):
                    if m == 0:
                        v.wait_ge(ctx_out, h * 3 + 4)
                    c0 = PIECE * m
                    v.reciprocal(inv[:, m % 2, :], cu[DH:128, c0:c0 + PIECE]).then_inc(inv_ready, 1)
                    v.wait_ge(inv_ready, h * HALF + (m + 1))
                    v.tensor_tensor(ctxT[DH * j:DH * j + DH, chunk, c0:c0 + PIECE].rearrange("p o n -> p (o n)"),
                                    cu[0:DH, c0:c0 + PIECE], inv[:, m % 2, :], ALU.mult).then_inc(norm_out, 1)

                last = []

                def tiles(h, j, those, has_next, has_second):
                    for t in those:
                        if has_next:
                            maxima(h + 1, t)
                        if last and t < HALF:
                            finish(*last[0], t)
                        if t == HALF and has_second:
                            split_lo(h + 2)

                def between(h, j, chunk, has_next, has_second):
                    if has_next:
                        negate(h + 1)
                        v.wait_ge(pv_done, h * T + (T + 1))
                        take_v(h + 1)
                        take_row(h + 1, 1 - j)
                    if has_second:
                        take_projections(h + 2, j)
                    last[:] = [(h, j, chunk)]

                take_v(0)
                split_lo(0)
                take_projections(0, 0)
                split_lo(1)
                for t in range(T):
                    maxima(0, t)
                negate(0)
                take_projections(1, 1)
                take_row(0, 0)
                schedule(v, tiles, between)
                for m in range(HALF):
                    finish(*last[0], m)
def route(nc, k, yT, wr, br, E_, topk, cap, keep_last, r):
    with ExitStack() as ctx:
        def sb(name, shape, dt=fp32):
            return ctx.enter_context(nc.sbuf_tensor(k.name(name), shape, dt))

        def sem(name):
            return ctx.enter_context(k.semaphore(nc, k.name(name)))

        L = sb("logits", [P, T, E_])
        W = sb("work", [P, T, E_])
        PR = sb("probs", [P, T, E_])
        OH = sb("onehot", [P, 2, T, E_])
        M16 = sb("mask16", [P, T, E_], bf16)
        POS = sb("pos", [P, T, E_])
        G = sb("gates_by_expert", [P, T, E_])
        m1 = sb("m1", [P, T])
        top = sb("top", [P, T, 8])
        idx = sb("idx", [P, T, 8], u32)
        ix = sb("ix", [P, 2, T])
        pk = sb("pk", [P, 2, T])
        keep = sb("keep", [P, 2, T])
        tmp = sb("tmp", [P, 4, T])
        spare = sb("spare", [P, 2, T])
        ioE = sb("iota_e", [P, E_])
        cnt = sb("cnt", [P, E_])
        cnti = sb("cnt_i", [P, 2, E_], i32)
        blk = sb("blk", [P, 3, E_])
        ps = k.ps
        iotas, logit_done, logit_out = sem("iotas"), sem("logit_done"), sem("logit_out")
        steps, shifted, exps, masks = sem("route_steps"), sem("shifted"), sem("exps"), sem("masks")
        pos_done, gates_ready, gT_done, gT_out = sem("pos_done"), sem("gates_ready"), sem("gT_done"), sem("gT_out")
        PB = T // 2

        def two(bank):
            return [(ps[0:P, bank + b, 0:PB * E_].rearrange("p (t e) -> p t e", e=E_), slice(PB * b, PB * b + PB))
                    for b in range(2)]

        def over_e(ap):
            return ap.unsqueeze(2).broadcast_to([P, T, E_])

        with nc.Block() as block:
            @block.gpsimd
            def _(pool):
                pool.iota(ioE[:, :], [[1, E_]], base=0, channel_multiplier=0,
                          allow_small_or_imprecise_dtypes=True).then_inc(iotas, 1)
                for c in range(topk):
                    pool.iota(spare[:, c, :], [[topk * P, T]], base=c + r.spare0, channel_multiplier=topk,
                              allow_small_or_imprecise_dtypes=True).then_inc(iotas, 1)

            @block.tensor
            def _(pe):
                for t in range(T):
                    o = ps[0:P, t // PB, E_ * (t % PB):E_ * (t % PB) + E_]
                    for c in range(C):
                        mm = pe.matmul(o, yT[:, c, P * t:P * t + P], wr[:, c, :], start=(c == 0),
                                       stop=(c == C - 1 and br is None))
                    if br is not None:
                        mm = pe.matmul(o, k.ones[0:1, 0:P], br, start=False, stop=True)
                mm.then_inc(logit_done, 1)
                pe.wait_ge(masks, 1)
                for t in range(T):
                    o = ps[0:P, 2 + t // PB, E_ * (t % PB):E_ * (t % PB) + E_]
                    for u in range(t):
                        pe.matmul(o, k.ones16[0:P, 0:P], M16[:, u, :], start=(u == 0), stop=False)
                    mm = pe.matmul(o, k.tri16[0:P, 0:P], M16[:, t, :], start=(t == 0), stop=True)
                if cap is None:
                    for u in range(T):
                        mm = pe.matmul(ps[0:P, 4, 0:E_], k.ones16[0:P, 0:P], M16[:, u, :], start=(u == 0),
                                       stop=(u == T - 1))
                mm.then_inc(pos_done, 1)
                pe.wait_ge(gates_ready, 1)
                for n, (c0, cn) in enumerate(CH):
                    for t in range(c0 // P, (c0 + cn) // P):
                        mm = pe.transpose(ps[0:E_, 5 + n, P * t - c0:P * t - c0 + P], G[:, t, :], k.ident[0:P, 0:P])
                mm.then_inc(gT_done, 1)

            @block.scalar
            def _(act):
                act.wait_ge(shifted, 1)
                act.activation(W[:, :, :], L[:, :, :], ACT.Exp).then_inc(exps, 1)
                act.wait_ge(gT_done, 1)
                for n, (c0, cn) in enumerate(CH):
                    act.activation(r.gateT[:, c0:c0 + cn], ps[0:E_, 5 + n, 0:cn], ACT.Copy).then_inc(gT_out, 1)

            @block.vector
            def _(v):
                s = Steps(v, steps)
                v.wait_ge(iotas, 1 + topk)
                v.wait_ge(logit_done, 1)
                for part, tt in two(0):
                    s.did(v.tensor_copy(POS[:, tt, :], part))
                s.wait()
                s.did(v.tensor_reduce(m1[:, :], POS[:, :, :], AX.X, ALU.max))
                s.wait()
                v.tensor_tensor(L[:, :, :], POS[:, :, :], over_e(m1[:, :]), ALU.subtract).then_inc(shifted, 1)
                v.wait_ge(exps, 1)
                s.did(v.tensor_reduce(m1[:, :], W[:, :, :], AX.X, ALU.add))
                s.wait()
                s.did(v.reciprocal(tmp[:, 0, :], m1[:, :]))
                s.wait()
                s.did(v.tensor_tensor(PR[:, :, :], W[:, :, :], over_e(tmp[:, 0, :]), ALU.mult))
                s.wait()
                for t in range(T):
                    s.did(v.max(top[:, t, :], PR[:, t, :]))
                s.wait()
                for t in range(T):
                    s.did(v.max_index(idx[:, t, :], top[:, t, :], PR[:, t, :]))
                s.wait()
                for c in range(topk):
                    s.did(v.tensor_copy(ix[:, c, :], idx[:, :, c]))
                s.wait()
                for c in range(topk):
                    s.did(v.tensor_tensor(OH[:, c, :, :], ioE[:, :].unsqueeze(1).broadcast_to([P, T, E_]),
                                          over_e(ix[:, c, :]), ALU.is_equal))
                s.wait()
                if topk == 2:
                    v.tensor_tensor(M16[:, :, :], OH[:, 0, :, :], OH[:, 1, :, :], ALU.add).then_inc(masks, 1)
                else:
                    v.tensor_copy(M16[:, :, :], OH[:, 0, :, :]).then_inc(masks, 1)
                v.wait_ge(pos_done, 1)
                for part, tt in two(2):
                    s.did(v.tensor_copy(POS[:, tt, :], part))
                s.wait()
                if cap is None:
                    s.did(v.tensor_copy(cnt[:, :], ps[0:P, 4, 0:E_]))
                    s.wait()
                    s.did(v.memset(blk[:, 0, :], 1.0))
                    s.wait()
                    for b in range(1, N // (2 * P)):
                        s.did(v.scalar_tensor_tensor(blk[:, 0, :], cnt[:, :], float(2 * P * b), blk[:, 0, :],
                                                     ALU.is_gt, ALU.add))
                        s.wait()
                    s.did(v.memset(blk[:, 1, :], 0.0))
                    s.did(v.memset(blk[:, 2, 0:1], 0.0))
                    s.wait()
                    for e in range(1, E_):
                        s.did(v.tensor_tensor(blk[:, 2, e:e + 1], blk[:, 2, e - 1:e], blk[:, 0, e - 1:e], ALU.add))
                        s.wait()
                    s.did(v.tensor_copy(r.tab[:, 0, :], blk[0:1, 0, :]))
                    s.did(v.tensor_copy(r.tab[:, 1, :], blk[0:1, 2, :]))
                    s.did(v.tensor_scalar(blk[:, 1, :], blk[:, 2, :], float(2 * P), None, ALU.mult))
                    s.wait()
                    s.did(v.tensor_tensor(POS[:, :, :], POS[:, :, :],
                                          blk[:, 1, :].unsqueeze(1).broadcast_to([P, T, E_]), ALU.add))
                    s.wait()
                for c in range(topk):
                    s.did(v.tensor_tensor(W[:, :, :], OH[:, c, :, :], POS[:, :, :], ALU.mult))
                    s.wait()
                    s.did(v.tensor_reduce(pk[:, c, :], W[:, :, :], AX.X, ALU.add))
                    s.wait()
                if cap is None:
                    s.did(v.tensor_copy(r.put[:, 0, :], pk[:, 0, :]))
                    s.did(v.tensor_copy(r.get[:, 0, :], pk[:, 0, :]))
                    s.did(v.tensor_copy(r.gate[:, 0, :], top[:, :, 0]))
                    s.wait()
                else:
                    for c in range(2):
                        s.did(v.tensor_scalar(keep[:, c, :], pk[:, c, :], float(cap), None, ALU.is_lt))
                        s.did(v.tensor_scalar(tmp[:, c, :], pk[:, c, :], float(cap - 1), None, ALU.min))
                    s.wait()
                    for c in range(2):
                        s.did(v.scalar_tensor_tensor(tmp[:, 2 + c, :], ix[:, c, :], float(cap), tmp[:, c, :],
                                                     ALU.mult, ALU.add))
                    s.wait()
                    for c in range(2):
                        s.did(v.tensor_copy(r.get[:, c, :], tmp[:, 2 + c, :]))
                        s.did(v.tensor_tensor(tmp[:, c, :], tmp[:, 2 + c, :], spare[:, c, :], ALU.subtract))
                    s.wait()
                    for c in range(2):
                        s.did(v.tensor_tensor(tmp[:, c, :], tmp[:, c, :], keep[:, c, :], ALU.mult))
                    s.wait()
                    for c in range(2):
                        s.did(v.tensor_tensor(r.put[:, c, :], tmp[:, c, :], spare[:, c, :], ALU.add))
                    s.wait()
                    if keep_last:
                        s.did(v.tensor_tensor(tmp[:, 0, :], ix[:, 1, :], ix[:, 0, :], ALU.is_gt))
                        s.did(v.tensor_tensor(tmp[:, 1, :], ix[:, 0, :], ix[:, 1, :], ALU.is_gt))
                        s.wait()
                        for c in range(2):
                            s.did(v.tensor_tensor(tmp[:, c, :], tmp[:, c, :], keep[:, 1 - c, :], ALU.mult))
                        s.wait()
                        for c in range(2):
                            s.did(v.tensor_scalar(tmp[:, c, :], tmp[:, c, :], -1.0, 1.0, ALU.mult, ALU.add))
                        s.wait()
                    else:
                        s.did(v.tensor_tensor(m1[:, :], top[:, :, 0], top[:, :, 1], ALU.add))
                        s.wait()
                        s.did(v.reciprocal(tmp[:, 2, :], m1[:, :]))
                        s.wait()
                        for c in range(2):
                            s.did(v.tensor_tensor(tmp[:, c, :], tmp[:, 2, :], top[:, :, c], ALU.mult))
                        s.wait()
                    for c in range(2):
                        s.did(v.tensor_tensor(r.gate[:, c, :], tmp[:, c, :], keep[:, c, :], ALU.mult))
                    s.wait()
                if topk == 2:
                    s.did(v.tensor_tensor(W[:, :, :], OH[:, 0, :, :], over_e(r.gate[:, 0, :]), ALU.mult))
                    s.did(v.tensor_tensor(PR[:, :, :], OH[:, 1, :, :], over_e(r.gate[:, 1, :]), ALU.mult))
                    s.wait()
                    v.tensor_tensor(G[:, :, :], W[:, :, :], PR[:, :, :], ALU.add).then_inc(gates_ready, 1)
                else:
                    v.tensor_tensor(G[:, :, :], OH[:, 0, :, :], over_e(r.gate[:, 0, :]), ALU.mult)\
                        .then_inc(gates_ready, 1)


def experts(nc, k, r, rows_in, E_, F, R, tiles, func, w1, b1, w2, affine, buf, ybuf, dynamic, room=None, residual=None):
    FC = F // 128
    EPG = 2 if tiles == 1 else 1
    RING = 4
    ROUNDS = E_ // (RING * EPG)
    with ExitStack() as ctx:
        def sb(name, shape, dt=fp32):
            return ctx.enter_context(nc.sbuf_tensor(k.name(name), shape, dt))

        def sem(name):
            return ctx.enter_context(k.semaphore(nc, k.name(name)))

        if room is None:
            w1s = sb("w1s", [128, RING * EPG, C, F])
        else:
            w1s = room(128, (RING * EPG * C, F)).rearrange("p (e c) f -> p e c f", c=C)
        w2s = sb("w2s", [128, RING * EPG, FC, D])
        b1s = sb("b1s", [128, RING * EPG, FC])
        xb = sb("xb", [R, 2, D])
        xbT = sb("xbT", [128, 2, 2, C, R])
        hT = sb("hT", [128, 2, FC, R])
        yb = sb("yb", [R, 2, D])
        put_done = k.gpsimd_dma_semaphore(nc, "put_done")
        stored = [k.gpsimd_dma_semaphore(nc, "stored") for _ in range(2)]
        w_in, w_used = [sem(f"w_in{g}") for g in range(RING)], [sem(f"w_used{g}") for g in range(RING)]
        rows_loaded, turned = [sem("rows0"), sem("rows1")], [sem("turned0"), sem("turned1")]
        xT_out, h_done, h_out = [[sem(n + "0"), sem(n + "1")] for n in ("xT_out", "h_done", "h_out")]
        yb_free = [sem("yb_free0"), sem("yb_free1")]
        y_done, y_out = [[sem(n + "0"), sem(n + "1")] for n in ("y_done", "y_out")]
        ps = k.ps

        def group(eng, i, g, body):
            e = i * RING + g
            if dynamic:
                n = eng.snap(eng.value_load(r.tab[0:1, 0, bass.ds(e, 1)], min_val=1, max_val=N // (2 * P)))
                first = eng.snap(eng.value_load(r.tab[0:1, 1, bass.ds(e, 1)], min_val=0, max_val=r.max_blocks))
                with eng.Fori(0, n) as q:
                    body(i, first + q, g)
            else:
                body(i, e, g)

        def run(eng, body, after=None):
            with eng.Fori(0, ROUNDS) as i:
                for g in range(RING):
                    group(eng, i, g, body)
                    if after is not None:
                        after(g)

        def run_ahead(eng, ahead, body, after=None):
            if dynamic:
                def both(i, u, g):
                    ahead(u, 0, True)
                    body(i, u, g, 0)
                run(eng, both, after)
                return

            def steps(i, g, last):
                u = i * RING + g
                if not last:
                    ahead(u + 1, (g + 1) % 2, True)
                body(i, u, g, g % 2)
                if after is not None:
                    after(g)
            ahead(0, 0, False)
            with eng.Fori(0, ROUNDS - 1) as i:
                for g in range(RING):
                    steps(i, g, False)
            for g in range(RING):
                steps(ROUNDS - 1, g, g == RING - 1)

        def rows_of(u, s):
            return bass.ds(nc.s_assert_within(u * (2 * R) + s * R, 0, r.rows - R,
                                              skip_runtime_bounds_check_because="the blocks fit the buffer"), R)

        def second(s):
            return s if EPG == 2 else 0

        with nc.Block() as block:
            @block.sync
            def _(sp):
                def rows(i, u, g):
                    for s in range(2):
                        sp.wait_ge(turned[s], u + 1)
                        sp.dma_start(xb[:, s, :], buf[rows_of(u, s), :]).then_inc(rows_loaded[s], 16)

                sp.wait_ge(put_done, 16 * r.topk * T)
                run(sp, rows)

            @block.gpsimd
            def _(pool):
                for c in range(r.topk):
                    for t in range(T):
                        pool.indirect_dma_start(buf, bass.IndirectOffsetOnAxis(ap=r.put[:, c, t:t + 1], axis=0),
                                                rows_in[:, t, :], None).then_inc(put_done, 16)
                pool.sem_inc(yb_free[0], 1)
                pool.sem_inc(yb_free[1], 1)

                def store(i, u, g):
                    for s in range(2):
                        pool.wait_ge(y_out[s], u + 2)
                        pool.dma_start(ybuf[rows_of(u, s), :], yb[:, s, :]).then_inc(stored[s], 16)
                    for s in range(2):
                        pool.wait_ge(stored[s], u * 16 + 16)
                        pool.sem_inc(yb_free[s], 1)
                run(pool, store)

            @block.tensor
            def _(pe):
                for g in range(RING):
                    pe.sem_inc(w_used[g], 1)
                for s in range(2):
                    pe.sem_inc(turned[s], 1)

                    pe.sem_inc(xT_out[s], 1)

                def turn(u, parity, used):
                    for s in range(2):
                        if used:
                            pe.wait_ge(xT_out[s], u + 1)
                        pe.wait_ge(rows_loaded[s], u * 16 + 16)
                        for c in range(C):
                            mm = pe.transpose(ps[:, 4 * s, R * c:R * c + R], xb[:, s, 128 * c:128 * c + 128],
                                              k.ident[0:R, 0:R])
                        mm.then_inc(turned[s], 1)

                def products(i, u, g, parity):
                    pe.wait_ge(w_in[g], (i + 1) * (48 * EPG))
                    for s in range(2):
                        w = g * EPG + second(s)
                        pe.wait_ge(xT_out[s], u + 2)
                        for m in range(FC):
                            for c in range(C):
                                mm = pe.matmul(ps[:, 4 * s + 1, R * m:R * m + R],
                                               w1s[:, w, c, 128 * m:128 * m + 128],
                                               xbT[:, s, parity, c, :], start=(c == 0), stop=(c == C - 1))
                        mm.then_inc(h_done[s], 1)
                    for s in range(2):
                        w = g * EPG + second(s)
                        pe.wait_ge(h_out[s], u * FC + FC)
                        pe.wait_ge(y_out[s], u + 1)
                        for m in range(FC):
                            mm = pe.matmul(ps[0:R, 4 * s + 2, :], hT[:, s, m, :], w2s[:, w, m, :],
                                           start=(m == 0), stop=(m == FC - 1))
                        mm.then_inc(y_done[s], 1)

                run_ahead(pe, turn, products, after=lambda g: pe.drain().then_inc(w_used[g], 1))

            @block.scalar
            def _(act):
                def weights(i, g):
                    act.wait_ge(w_used[g], i + 1)
                    for x_ in range(EPG):
                        e = (i * RING + g) * EPG + x_
                        act.dma_start(w1s[:, g * EPG + x_, :, :], w1[bass.ds(e, 1)].rearrange("o p c f -> p (o c) f"))\
                            .then_inc(w_in[g], 16)
                        act.dma_start(w2s[:, g * EPG + x_, :, :],
                                     w2[bass.ds(e, 1)].rearrange("o (c p) n -> p (o c) n", p=128))\
                            .then_inc(w_in[g], 16)
                        act.dma_start(b1s[:, g * EPG + x_, :], b1[bass.ds(e, 1)].rearrange("o p f -> p (o f)"))\
                            .then_inc(w_in[g], 16)

                def hidden(i, u, g):
                    for s in range(2):
                        act.wait_ge(h_done[s], u + 1)
                        for m in range(FC):
                            act.activation(hT[:, s, m, :], ps[:, 4 * s + 1, R * m:R * m + R], func,
                                           bias=b1s[:, g * EPG + second(s), m:m + 1]).then_inc(h_out[s], 1)

                weights(0, 0)
                act.wait_ge(put_done, 16 * r.topk * T)
                for g in range(1, RING - 1):
                    weights(0, g)
                with act.Fori(0, ROUNDS - 1) as i:
                    for g in range(RING):
                        weights(i + (1 if g else 0), (g + RING - 1) % RING)
                        group(act, i, g, hidden)
                weights(ROUNDS - 1, RING - 1)
                for g in range(RING):
                    group(act, ROUNDS - 1, g, hidden)

            @block.vector
            def _(v):
                v.sem_inc(y_out[0], 1)
                v.sem_inc(y_out[1], 1)
                if residual is not None:
                    x, res = residual
                    v.tensor_tensor(x[:, :, :], x[:, :, :], res[:, :, :], ALU.add)

                def affine_rows(u, parity, used):
                    for s in range(2):
                        v.wait_ge(turned[s], u + 2)
                        if affine is None:
                            v.tensor_copy(xbT[:, s, parity, :, :], ps[:, 4 * s, 0:C * R].rearrange("p (c r) -> p c r", c=C))\
                                .then_inc(xT_out[s], 1)
                        else:
                            for c in range(C):
                                last = v.tensor_scalar(xbT[:, s, parity, c, :], ps[:, 4 * s, R * c:R * c + R],
                                                       affine[0][:, c:c + 1], affine[1][:, c:c + 1], ALU.mult,
                                                       ALU.add)
                            last.then_inc(xT_out[s], 1)

                def take(i, u, g, parity):
                    for s in range(2):
                        v.wait_ge(y_done[s], u + 1)
                        v.wait_ge(yb_free[s], u + 1)
                        v.tensor_copy(yb[:, s, :], ps[0:R, 4 * s + 2, :]).then_inc(y_out[s], 1)
                run_ahead(v, affine_rows, take)


def combine(nc, k, r, x, b2, ybuf, E_, out=None):
    with ExitStack() as ctx:
        Y = ctx.enter_context(nc.sbuf_tensor(k.name("Y"), [P, 4, D], fp32))
        got = [k.gpsimd_dma_semaphore(nc, "got") for _ in range(4)]
        used, summed, taken, stored = (ctx.enter_context(k.semaphore(nc, k.name(n)))
                                       for n in ("y_used", "summed", "taken", "stored"))
        K_ = r.topk
        with nc.Block() as block:
            if out is not None:
                @block.sync
                def _(sp):
                    for t in range(T):
                        sp.wait_ge(used, K_ * (t + 1))
                        sp.dma_start(out[P * t:P * t + P, :], x[:, t, :]).then_inc(stored, 16)
                    sp.wait_ge(stored, 16 * T)

            @block.gpsimd
            def _(pool):
                for n in range(K_ * T):
                    t, c = n // K_, n % K_
                    if n >= 4:
                        pool.wait_ge(used, n - 3)
                    pool.indirect_dma_start(Y[:, n % 4, :], None, ybuf,
                                            bass.IndirectOffsetOnAxis(ap=r.get[:, c, t:t + 1], axis=0))\
                        .then_inc(got[n % 4], 16)

            @block.tensor
            def _(pe):
                for t in range(T):
                    if t >= 8:
                        pe.wait_ge(taken, t - 7)
                    pe.matmul(k.ps[0:P, t % 8, :], r.gateT[:, P * t:P * t + P], b2, start=True, stop=True)\
                        .then_inc(summed, 1)

            @block.vector
            def _(v):
                for t in range(T):
                    v.wait_ge(summed, t + 1)
                    v.tensor_tensor(x[:, t, :], x[:, t, :], k.ps[0:P, t % 8, :], ALU.add).then_inc(taken, 1)
                    v.wait_ge(taken, t + 1)
                    for c in range(K_):
                        n = t * K_ + c
                        v.wait_ge(got[n % 4], 16 * (n // 4 + 1))
                        v.scalar_tensor_tensor(x[:, t, :], Y[:, n % 4, :], r.gate[:, c, t:t + 1], x[:, t, :],
                                               ALU.mult, ALU.add).then_inc(used, 1)
                        v.wait_ge(used, n + 1)
class Routing:

    def __init__(self, nc, k, ctx, E_, topk, cap):
        self.topk = topk
        blocks = None if cap else E_ + N // (2 * P) - 1
        self.max_blocks = blocks
        self.rows = E_ * cap if cap else blocks * 2 * P
        self.spare0 = self.rows
        self.put = ctx.enter_context(nc.sbuf_tensor(k.name("put"), [P, 2, T], u32))
        self.get = ctx.enter_context(nc.sbuf_tensor(k.name("get"), [P, 2, T], u32))
        self.gate = ctx.enter_context(nc.sbuf_tensor(k.name("gate"), [P, 2, T], fp32))
        self.gateT = ctx.enter_context(nc.sbuf_tensor(k.name("gateT"), [E_, N], fp32))
        self.tab = ctx.enter_context(nc.sbuf_tensor(k.name("tab"), [1, 2, E_], i32))


class Room:

    def __init__(self, tile):
        self.flat, self.used = tile[:, :, :].rearrange("p a b -> p (a b)"), 0

    def __call__(self, partitions, shape):
        size = int(np.prod(shape))
        piece = self.flat[0:partitions, self.used:self.used + size]
        self.used += size
        assert self.used <= self.flat.shape[1]
        return piece if len(shape) == 1 else piece.rearrange("p (a b) -> p a b", a=shape[0])


def rowtiles(ap):
    return ap.rearrange("(t p) n -> p t n", p=P)


def kchunks(ap):
    return ap.rearrange("(c p) n -> p c n", p=128)


def row(ap):
    return ap.rearrange("(o n) -> o n", o=1)


def pair_of(nc, k, ctx, name, shape):
    return [ctx.enter_context(nc.sbuf_tensor(k.name(name + part), shape, f32r)) for part in ("_hi", "_lo")]


def l0_gnn(nc, k, a, x, matrix):
    with ExitStack() as ctx:
        def sb(name, shape):
            return ctx.enter_context(nc.sbuf_tensor(k.name(name), shape, fp32))
        hT = sb("hT", [128, C, N])
        wl, wr, bl = sb("wl", [128, C, D]), sb("wr", [128, C, D]), sb("bl", [P, D])
        biased = sb("biased", [P, 2, D])
        G, u = pair_of(nc, k, ctx, "G", [P, T, N]), pair_of(nc, k, ctx, "u", [P, T, D])

        def weights(l):
            return [(wl[:, :, :], kchunks(a[f"L0_gnn_Wl{l}T"])), (wr[:, :, :], kchunks(a[f"L0_gnn_Wr{l}T"])),
                    (bl[:, :], a[f"L0_gnn_bl{l}"].partition_broadcast(P))]
        norm_rows(nc, k, x, x, hT, beside=weights(0))
        linear_split(nc, k, hT, wl, None, u, (matrix, G, matrix_slabs(x)))
        rows_product(nc, k, three_terms(G, u, T) + [(hT, wr, C)], bl, relu_rows(x), biased=biased)
        transpose_only(nc, k, x, hT, beside=weights(1))
        linear_split(nc, k, hT, wl, None, u, beside=in_two(x, rowtiles(a["x"])))
        rows_product(nc, k, three_terms(G, u, T) + [(hT, wr, C)], bl, add_relu(x), x, biased)


def relu_rows(x):
    return {"vector": lambda v, i, total: v.tensor_scalar(x[:, i, :], total, 0.0, None, ALU.max)}


def add_relu(x):
    return {"vector": lambda v, i, psum: v.scalar_tensor_tensor(x[:, i, :], psum, 0.0, x[:, i, :], ALU.max, ALU.add)}


def transformer(nc, k, a, x, pre, E_, F, cap, func, keep_last, buf, ybuf, out=None):
    with ExitStack() as ctx:
        def sb(c_, name, shape):
            return c_.enter_context(nc.sbuf_tensor(k.name(name), shape, fp32))
        Gf = sb(ctx, "room", [128, T, N])
        res = sb(ctx, "res", [P, T, D])
        g1, b1, g2, b2 = (sb(ctx, n, [128, C]) for n in ("g1", "b1", "g2", "b2"))
        norm_rows(nc, k, x, res, have_stats=True, beside=[(g1[:, :], a[pre + "ln1_g_c"]), (b1[:, :], a[pre + "ln1_b_c"]),
                                         (g2[:, :], a[pre + "ln2_g_c"]), (b2[:, :], a[pre + "ln2_b_c"])])
        bias = pre + "bo" in a
        with ExitStack() as c2:
            room = Room(Gf)
            ctxT, Vplace = room(128, (C, N)), room(128, (T, D))
            wv, bv = Vplace[:, 0:C, :], Vplace[0:1, C:C + 1, :] if bias else None
            pair = pair_of(nc, k, c2, "x", [128, C, N])
            wo, bo, biased = sb(c2, "wo", [128, C, D]), sb(c2, "bo", [P, D]), sb(c2, "biased", [P, 2, D])
            with ExitStack() as c3:
                xn = sb(c3, "xn", [P, T, D])
                norm_rows(nc, k, res, xn, ctxT, (g1, b1),
                          beside=[(wv, kchunks(a[pre + "wv"])), (wo[:, :, :], kchunks(a[pre + "wo"]))]
                          + ([(bv[:, 0, :], row(a[pre + "bv"])), (bo[:, :], a[pre + "bo"].partition_broadcast(P))]
                             if bias else []))
            split(nc, k, [(ctxT, *pair)])
            values(nc, k, pair, wv, bv, Vplace[0:P])
            attention(nc, k, pair, a[pre + "wqk"], a[pre + "bqk"] if bias else None, Vplace[0:P], ctxT, room)
            rows_product(nc, k, [(ctxT, wo, C)], bo if bias else None, add_rows(res), res, biased)
        yn, xnT = sb(ctx, "yn", [P, T, D]), sb(ctx, "xnT", [128, C, N])
        b2r, wr, br = sb(ctx, "b2r", [E_, D]), sb(ctx, "wr", [128, C, E_]), sb(ctx, "br", [1, E_])
        norm_rows(nc, k, res, yn, xnT, (g2, b2), have_stats=True,
                  beside=[(b2r[:, :], a[pre + "b2"]), (wr[:, :, :], kchunks(a[pre + ("router_w" if bias else "wr")]))]
                  + ([(br[:, :], row(a[pre + "router_b"]))] if bias else []))
        r = Routing(nc, k, ctx, E_, 2, cap)
        route(nc, k, xnT, wr, br[:, :] if bias else None, E_, 2, cap, keep_last, r)
        R = 78 if cap == 78 else P
        experts(nc, k, r, yn, E_, F, R, 1 if R == cap else 2, func, a[pre + "w1_p"], a[pre + "b1_p"], a[pre + "w2"],
                (g2, b2), buf, ybuf, False, Room(Gf), (x, res))
        combine(nc, k, r, x, b2r[:, :], ybuf, E_, out)


def graph_layer(nc, k, x, w_dram, b_dram, matrix, inner_bias, finish):
    with ExitStack() as ctx:
        def sb(name, shape):
            return ctx.enter_context(nc.sbuf_tensor(k.name(name), shape, fp32))
        xT, w, b = sb("xT", [128, C, N]), sb("w", [128, C, D]), sb("b", [P, D])
        with nc.sbuf_tensor(k.name("xn"), [P, T, D], fp32) as xn:
            norm_rows(nc, k, x, xn, xT, beside=[(w[:, :, :], kchunks(w_dram)), (b[:, :], b_dram.partition_broadcast(P))])
        G, y = pair_of(nc, k, ctx, "G", [P, T, N]), pair_of(nc, k, ctx, "y", [P, T, D])
        if inner_bias:
            with nc.sbuf_tensor(k.name("slabs"), [P, 1, N], fp32) as slabs, \
                    nc.sbuf_tensor(k.name("biased"), [P, 2, D], fp32) as biased:
                linear_split(nc, k, xT, w, (b, biased), y, (matrix, G, slabs))
            rows_product(nc, k, three_terms(G, y, T), None, finish, x)
        else:
            slabs = sb("slabs", [P, 2, N])
            linear_split(nc, k, xT, w, None, y, (matrix, G, slabs))
            rows_product(nc, k, three_terms(G, y, T), b, finish, x, slabs[:, :, 0:D])


def l2_gnn(nc, k, a, x, matrix):
    with ExitStack() as ctx:
        def sb(name, shape):
            return ctx.enter_context(nc.sbuf_tensor(k.name(name), shape, fp32))

        def sem(name):
            return ctx.enter_context(k.semaphore(nc, k.name(name)))
        xT, w = sb("xT", [128, C, N]), sb("w", [128, C, D])
        cols = sb("bgb", [128, 3, 3, C])
        st, mv = sb("bn_parts", [128, C, 3, 6]), sb("mean_var", [128, C, 2])
        sc, sh = sb("scale", [128, C]), sb("shift", [128, C])


        def weights(l):
            return [(w[:, :, :], kchunks(a["L2_gnn_WT"][l]))]
        with nc.sbuf_tensor(k.name("xn"), [P, T, D], fp32) as xn:
            norm_rows(nc, k, x, xn, xT, beside=weights(0) + [(cols[:, :, :, :], a["L2_gnn_bgb"])])
        G, h = pair_of(nc, k, ctx, "G", [P, T, N]), pair_of(nc, k, ctx, "h", [P, T, D])
        slabs = sb("slabs", [P, 2, N])
        for l in range(3):
            steps, var_ready, std_ready, scale_ready = sem("steps"), sem("var"), sem("std"), sem("scale_ready")
            linear_split(nc, k, xT, w, None, h, (matrix, G, slabs) if l == 0 else None)
            columns_product(nc, k, three_terms(h, G, T), C, lambda act, m, ch, n, psum:
                            act.activation(xT[:, m, ch[0]:ch[0] + ch[1]], psum, ACT.Identity,
                                           bias=cols[:, 0, l, m:m + 1]),
                            beside=weights(l + 1) if l < 2 else ())
            with nc.Block() as block:
                @block.vector
                def _(v):
                    s = Steps(v, steps)
                    for m in range(C):
                        for n, (c0, cn) in enumerate(CH):
                            s.did(v.bn_stats(st[:, m, n, :], xT[:, m, c0:c0 + cn]))
                    s.wait()
                    for m in range(C):
                        s.did(v.bn_aggr(mv[:, m, :], st[:, m, :, :].rearrange("p a b -> p (a b)")))
                    s.wait()
                    v.tensor_scalar(sc[:, :], mv[:, :, 1], 1e-5, None, ALU.add).then_inc(var_ready, 1)
                    v.wait_ge(std_ready, 1)
                    s.did(v.reciprocal(sh[:, :], sc[:, :]))
                    s.wait()
                    s.did(v.tensor_tensor(sc[:, :], sh[:, :], cols[:, 1, l, :], ALU.mult))
                    s.wait()
                    s.did(v.tensor_tensor(sh[:, :], mv[:, :, 0], sc[:, :], ALU.mult))
                    s.wait()
                    v.tensor_tensor(sh[:, :], cols[:, 2, l, :], sh[:, :], ALU.subtract).then_inc(scale_ready, 1)

                @block.scalar
                def _(act):
                    act.wait_ge(var_ready, 1)
                    act.activation(sc[:, :], sc[:, :], ACT.Sqrt).then_inc(std_ready, 1)
                    act.wait_ge(scale_ready, 1)
                    for m in range(C):
                        act.activation(xT[:, m, :], xT[:, m, :], ACT.Relu, bias=sh[:, m:m + 1],
                                       scale=sc[:, m:m + 1])
        turned, taken = sem("turned"), sem("taken")
        with nc.Block() as block:
            @block.tensor
            def _(pe):
                for i in range(T):
                    if i >= 8:
                        pe.wait_ge(taken, i - 7)
                    for c in range(C):
                        mm = pe.transpose(k.ps[0:P, i % 8, 128 * c:128 * c + 128], xT[:, c, P * i:P * i + P],
                                          k.ident[:, :])
                    mm.then_inc(turned, 1)

            @block.vector
            def _(v):
                for i in range(T):
                    v.wait_ge(turned, i + 1)
                    v.tensor_tensor(x[:, i, :], x[:, i, :], k.ps[0:P, i % 8, :], ALU.add).then_inc(taken, 1)
                    stats_behind(v, k, x, i, taken)
                stats_behind(v, k, x, T, taken)


def l2_ffn(nc, k, a, x, buf, ybuf):
    E_, F = 8, 512
    with ExitStack() as ctx:
        def sb(c_, name, shape):
            return c_.enter_context(nc.sbuf_tensor(k.name(name), shape, fp32))
        xn, xT = sb(ctx, "xn", [P, T, D]), sb(ctx, "xT", [128, C, N])
        b2r, wr, br = sb(ctx, "b2r", [E_, D]), sb(ctx, "wr", [128, C, E_]), sb(ctx, "br", [1, E_])
        norm_rows(nc, k, x, xn, xT, have_stats=True, beside=[(wr[:, :, :], kchunks(a["L2_ffn_Wr"])), (br[:, :], row(a["L2_ffn_br"])),
                                            (b2r[:, :], a["L2_ffn_b2"])])
        r = Routing(nc, k, ctx, E_, 1, None)
        route(nc, k, xT, wr, br[:, :], E_, 1, None, False, r)
        experts(nc, k, r, xn, E_, F, P, 2, ACT.Relu, a["L2_ffn_w1_p"], a["L2_ffn_b1_p"], a["L2_ffn_W2"], None, buf, ybuf, True)
        combine(nc, k, r, x, b2r[:, :], ybuf, E_)


def l1_ffn(nc, k, a, x):
    E_, F, FC = 8, 256, 2
    with ExitStack() as ctx:
        def sb(c_, name, shape):
            return c_.enter_context(nc.sbuf_tensor(k.name(name), shape, fp32))

        def sem(name):
            return ctx.enter_context(k.semaphore(nc, k.name(name)))
        xn, xT, hT = sb(ctx, "xn", [P, T, D]), sb(ctx, "xT", [128, C, N]), sb(ctx, "hT", [128, FC, N])
        W1m, W2m = sb(ctx, "W1m", [128, C, F]), sb(ctx, "W2m", [128, FC, D])
        biased = sb(ctx, "biased", [P, 2, D])
        b1m, b2b, lngb, lnbb = (sb(ctx, "b1m", [128, FC]), sb(ctx, "b2b", [P, D]), sb(ctx, "lngb", [P, D]),
                                sb(ctx, "lnbb", [P, D]))
        with ExitStack() as c2:
            gw, gb = sb(c2, "gfc1", [128, C, D]), sb(c2, "gfc1_b", [128, C])
            g2w, g2b, g2c = sb(c2, "gfc2", [128, C, E_]), sb(c2, "gfc2_b", [128, E_]), sb(c2, "gfc2_bc", [E_, 1])
            tv1, tv2 = sb(c2, "tv1", [128, E_, C * F]), sb(c2, "tv2", [128, E_, FC * D])
            tb1, tb2 = sb(c2, "tb1", [E_, F]), sb(c2, "tb2", [E_, D])
            tg, tb, lg8, lb8 = (sb(c2, n, [E_, D]) for n in ("tg", "tb", "lg8", "lb8"))
            b1c, rows3 = sb(c2, "b1c", [128, FC]), sb(c2, "rows3", [1, 3, D])
            gh, ghs, ghb = sb(c2, "gh", [128, 4, 500]), sb(c2, "gh_sum", [128, C, 3]), sb(c2, "ghb", [128, C, 128])
            ghm, gB, gC = sb(c2, "gh_mean", [128, C]), sb(c2, "g_all", [128, E_]), sb(c2, "g_col", [E_, 1])
            norm_rows(nc, k, x, xn, xT, have_stats=True, beside=[
                         (gw[:, :, :], kchunks(a["L1_ffn_gfc1_wT"])), (gb[:, :], a["L1_ffn_gfc1_b_c"]),
                         (g2w[:, :, :], kchunks(a["L1_ffn_gfc2_wT"])),
                         (g2b[:, :], a["L1_ffn_gfc2_b"].partition_broadcast(128)),
                         (g2c[:, :], a["L1_ffn_gfc2_b"].rearrange("(p o) -> p o", o=1)),
                         (tv1[:, :, :], a["L1_ffn_tv_W1_p"]), (tv2[:, :, :], a["L1_ffn_tv_W2_p"]),
                         (W1m[:, :, :], kchunks(a["L1_ffn_W1T"])), (W2m[:, :, :], kchunks(a["L1_ffn_W2T"])),
                         (tb1[:, :], a["L1_ffn_tv_b1"]), (tb2[:, :], a["L1_ffn_tv_b2"]),
                         (tg[:, :], a["L1_ffn_tv_ln_g"]), (tb[:, :], a["L1_ffn_tv_ln_b"]),
                         (lg8[:, :], a["L1_ffn_ln_g"].partition_broadcast(E_)),
                         (lb8[:, :], a["L1_ffn_ln_b"].partition_broadcast(E_)),
                         (b1c[:, :], a["L1_ffn_b1_c"]), (rows3[:, 0, :], row(a["L1_ffn_b2"])),
                         (rows3[:, 1, :], row(a["L1_ffn_ln_g"])), (rows3[:, 2, :], row(a["L1_ffn_ln_b"]))])
            columns_product(nc, k, [(gw, xT, C)], C, lambda act, m, ch, n, psum:
                            act.activation(gh[:, (3 * m + n) % 4, 0:ch[1]], psum, ACT.Relu, bias=gb[:, m:m + 1],
                                           accum_out=ghs[:, m, n:n + 1]), reuse=4)
            steps, mean_ready, g_done, g_out = sem("steps"), sem("mean_ready"), sem("g_done"), sem("g_out")
            rows_ready, sums_done, accs = sem("rows_ready"), sem("sums_done"), sem("accs")
            with nc.Block() as block:
                @block.tensor
                def _(pe):
                    pe.wait_ge(mean_ready, C)
                    for c in range(C):
                        pe.matmul(k.ps[:, 0, 0:E_], ghb[:, c, :], g2w[:, c, :], start=(c == 0), stop=(c == C - 1))
                    for c in range(C):
                        mm = pe.matmul(k.ps[0:E_, 1, 0:1], g2w[:, c, :], ghm[:, c:c + 1], start=(c == 0),
                                       stop=(c == C - 1))
                    mm.then_inc(g_done, 1)
                    pe.wait_ge(rows_ready, 4)
                    for n, t_ in enumerate((tb2, tg, tb)):
                        pe.matmul(k.ps[0:P, 2 + n, :], k.ones[0:E_, 0:P], t_[:, :], start=True, stop=False)
                        pe.matmul(k.ps[0:P, 2 + n, :], k.ones[0:1, 0:P], rows3[:, n, :], start=False, stop=True)
                    for m in range(FC):
                        mm = pe.matmul(k.ps[:, 5, m:m + 1], tb1[:, 128 * m:128 * m + 128], gC[:, :], start=True,
                                       stop=True, skip_group_check=True)
                    mm.then_inc(sums_done, 1)

                @block.scalar
                def _(act):
                    act.wait_ge(sums_done, 1)
                    for n, o in enumerate((b2b, lngb, lnbb)):
                        act.activation(o[:, :], k.ps[0:P, 2 + n, :], ACT.Copy)

                @block.vector
                def _(v):
                    s = Steps(v, steps)
                    s.did(v.tensor_reduce(ghm[:, :], ghs[:, :, :], AX.X, ALU.add))
                    s.wait()
                    s.did(v.tensor_scalar(ghm[:, :], ghm[:, :], 1.0 / N, None, ALU.mult))
                    s.wait()
                    for c in range(C):
                        v.tensor_scalar(ghb[:, c, :], k.ones[:, :], ghm[:, c:c + 1], None, ALU.mult)\
                            .then_inc(mean_ready, 1)
                    s.did(v.tensor_tensor(tg[:, :], tg[:, :], lg8[:, :], ALU.subtract))
                    s.did(v.tensor_tensor(tb[:, :], tb[:, :], lb8[:, :], ALU.subtract))
                    s.wait()
                    v.tensor_scalar(tg[:, :], tg[:, :], 0.03, None, ALU.mult).then_inc(rows_ready, 1)
                    v.tensor_scalar(tb[:, :], tb[:, :], 0.03, None, ALU.mult).then_inc(rows_ready, 1)
                    v.wait_ge(g_done, 1)
                    s.did(v.tensor_tensor(gB[:, :], g2b[:, :], k.ps[:, 0, 0:E_], ALU.add))
                    v.tensor_tensor(gC[:, :], g2c[:, :], k.ps[0:E_, 1, 0:1], ALU.add).then_inc(rows_ready, 1)
                    v.wait_ge(rows_ready, 3)
                    s.wait()
                    v.tensor_scalar(tb2[:, :], tb2[:, :], gC[:, 0:1], None, ALU.mult).then_inc(rows_ready, 1)
                    W1f = W1m[:, :, :].rearrange("p c f -> p (c f)")
                    W2f = W2m[:, :, :].rearrange("p c f -> p (c f)")
                    for e in range(E_):
                        if e:
                            v.wait_ge(accs, 2 * e)
                        v.scalar_tensor_tensor(W1f, tv1[:, e, :], gB[:, e:e + 1], W1f, ALU.mult, ALU.add)\
                            .then_inc(accs, 1)
                        v.scalar_tensor_tensor(W2f, tv2[:, e, :], gB[:, e:e + 1], W2f, ALU.mult, ALU.add)\
                            .then_inc(accs, 1)
                    v.wait_ge(sums_done, 1)
                    v.tensor_tensor(b1m[:, :], b1c[:, :], k.ps[:, 5, 0:FC], ALU.add)
        columns_product(nc, k, [(W1m, xT, C)], FC, lambda act, m, ch, n, psum:
                        act.activation(hT[:, m, ch[0]:ch[0] + ch[1]], psum, ACT.Relu, bias=b1m[:, m:m + 1]),
                        vector=lambda v: v.tensor_tensor(x[:, :, :], x[:, :, :],
                                                         lnbb[:, :].unsqueeze(1).broadcast_to([P, T, D]), ALU.add))
        rows_product(nc, k, [(hT, W2m, FC)], b2b, add_rows(xn), xn, biased)
        steps = sem("steps")
        norm_rows(nc, k, xn, xn, have_stats=True)
        with nc.Block() as block:
            @block.vector
            def _(v):
                s = Steps(v, steps)
                s.did(v.tensor_tensor(xn[:, :, :], xn[:, :, :], lngb[:, :].unsqueeze(1).broadcast_to([P, T, D]),
                                      ALU.mult))
                s.wait()
                s.did(v.tensor_tensor(x[:, :, :], x[:, :, :], xn[:, :, :], ALU.add))


def finish_graph(nc, k, CT, WT, W, w_spill, ah_spill, mean_spill):
    with ExitStack() as ctx:
        def sb(name, shape):
            return ctx.enter_context(nc.sbuf_tensor(k.name(name), shape, fp32))

        def sem(name):
            return ctx.enter_context(k.semaphore(nc, k.name(name)))
        rc, dr, part = sb("inv_deg_row", [P, N]), sb("dinv_row", [P, N]), sb("parts", [P, N])
        dc, mc, cols = sb("dinv_col", [P, T]), sb("inv_deg_col", [P, T]), sb("cols", [P, 3, T])
        turned, taken, deg_done, steps = sem("turned"), sem("taken"), sem("deg_done"), sem("steps")
        deg1, root_done, spilled, cols_ready = sem("deg1"), sem("root_done"), sem("spilled"), sem("cols_ready")
        parts_summed = sem("parts_summed")
        rows_done, scaled, normed, averaged = sem("rows_done"), sem("scaled"), sem("normed"), sem("averaged")
        with nc.Block() as block:
            @block.sync
            def _(sp):
                sp.wait_ge(taken, 3 * T)
                spill_rows(sp, rowtiles(w_spill), W, spilled)

            @block.tensor
            def _(pe):
                g = 0
                for d in range(T):
                    for c0, cn in CH:
                        if g >= 5:
                            pe.wait_ge(taken, g - 4)
                        for s_ in range(c0 // P, (c0 + cn) // P):
                            mm = pe.transpose(k.ps[0:P, g % 5, P * s_ - c0:P * s_ - c0 + P],
                                              WT[:, s_, P * d:P * d + P], k.ident[0:P, 0:P])
                        mm.then_inc(turned, 1)
                        g += 1
                pe.wait_ge(parts_summed, 1)
                for d in range(T):
                    mm = pe.matmul(k.ps[0:P, 5, d:d + 1], part[:, P * d:P * d + P], k.ones[0:P, 0:1], start=True,
                                   stop=True, skip_group_check=True)
                mm.then_inc(deg_done, 1)
                pe.wait_ge(cols_ready, 2)
                pe.wait_ge(taken, g)
                for bank, col in ((5, dc), (0, mc)):
                    for n, (c0, cn) in enumerate(CH):
                        for t in range(c0 // P, (c0 + cn) // P):
                            mm = pe.matmul(k.ps[0:P, bank + n, P * t - c0:P * t - c0 + P],
                                           col[:, t:t + 1].broadcast_to([P, P]), k.ident[0:P, 0:P], start=True,
                                           stop=True)
                        mm.then_inc(rows_done, 1)

            @block.scalar
            def _(act):
                g = 0
                for d in range(T):
                    for c0, cn in CH:
                        act.wait_ge(turned, g + 1)
                        act.activation(W[:, d, c0:c0 + cn], k.ps[0:P, g % 5, 0:cn], ACT.Copy).then_inc(taken, 1)
                        g += 1
                act.wait_ge(deg1, 1)
                act.activation(cols[:, 1, :], cols[:, 0, :], ACT.Sqrt).then_inc(root_done, 1)
                g = 0
                for bank, out in ((5, dr), (0, rc)):
                    for n, (c0, cn) in enumerate(CH):
                        g += 1
                        act.wait_ge(rows_done, g)
                        act.activation(out[:, c0:c0 + cn], k.ps[0:P, bank + n, 0:cn], ACT.Copy)

            @block.vector
            def _(v):
                s = Steps(v, steps)
                v.tensor_reduce(part[:, :], CT[:, :, :].rearrange("p t n -> p n t"), AX.X, ALU.add)\
                    .then_inc(parts_summed, 1)
                v.wait_ge(deg_done, 1)
                v.tensor_scalar(cols[:, 0, :], k.ps[0:P, 5, 0:T], 1.0, None, ALU.add).then_inc(deg1, 1)
                s.did(v.tensor_scalar(cols[:, 2, :], k.ps[0:P, 5, 0:T], 1.0, None, ALU.max))
                s.wait()
                v.reciprocal(mc[:, :], cols[:, 2, :]).then_inc(cols_ready, 1)
                v.wait_ge(root_done, 1)
                v.reciprocal(dc[:, :], cols[:, 1, :]).then_inc(cols_ready, 1)
        diag = sb("diag", [P, T, P])
        PIECE = 2
        with nc.Block() as block:
            @block.sync
            def _(sp):
                for t0 in range(0, T, PIECE):
                    t1 = t0 + PIECE
                    sp.wait_ge(normed, t1)
                    spill_rows(sp, rowtiles(ah_spill)[:, t0:t1], WT[:, t0:t1], spilled)
                    sp.wait_ge(averaged, t1)
                    spill_rows(sp, rowtiles(mean_spill)[:, t0:t1], CT[:, t0:t1], spilled)
                sp.wait_ge(spilled, 32 + 64 * (T // PIECE))

            @block.vector
            def _(v):
                s = Steps(v, steps, 1)
                s.did(v.tensor_tensor(diag[:, :, :], dr[:, :].rearrange("p (t n) -> p t n", n=P),
                                      k.ident[0:P, 0:P].unsqueeze(1).broadcast_to([P, T, P]), ALU.mult))
                s.wait()
                s.did(v.tensor_tensor(diag[:, :, :], diag[:, :, :], dc[:, :].unsqueeze(2).broadcast_to([P, T, P]),
                                      ALU.mult))
                s.wait()
                for t0 in range(0, T, PIECE):
                    for t in range(t0, t0 + PIECE):
                        v.scalar_tensor_tensor(WT[:, t, :], CT[:, t, :], dc[:, t:t + 1], dr[:, :], ALU.mult, ALU.mult)\
                            .then_inc(scaled, 1)
                    v.wait_ge(scaled, t0 + PIECE)
                    for t in range(t0, t0 + PIECE):
                        v.tensor_tensor(WT[:, t, P * t:P * t + P], WT[:, t, P * t:P * t + P], diag[:, t, :], ALU.add)\
                            .then_inc(normed, 1)
                    for t in range(t0, t0 + PIECE):
                        v.tensor_tensor(CT[:, t, :], CT[:, t, :], rc[:, :], ALU.mult).then_inc(averaged, 1)


def spill_rows(sp, dram, sbuf, sem):
    sp.dma_start(dram[0:120], sbuf[0:120]).then_inc(sem, 16)
    sp.dma_start(dram[120:P], sbuf[120:P]).then_inc(sem, 16)




def program(nc, a, out):
    k = Kit()
    with ExitStack() as ctx:
        k.lasting = ctx
        k.ps = ctx.enter_context(nc.psum_tensor("ps", [128, 8, 512], fp32))
        k.stats = ctx.enter_context(nc.sbuf_tensor("row_stats", [P, T, 6], fp32))
        k.ident = ctx.enter_context(nc.sbuf_tensor("ident", [128, 128], fp32))
        k.ones = ctx.enter_context(nc.sbuf_tensor("ones", [128, 128], fp32))
        k.tri = ctx.enter_context(nc.sbuf_tensor("tri", [128, 128], fp32))
        k.ones16 = ctx.enter_context(nc.sbuf_tensor("ones16", [128, 128], bf16))
        k.tri16 = ctx.enter_context(nc.sbuf_tensor("tri16", [128, 128], bf16))
        k.c_sel, k.c_win = a["c_sel"], a["c_win"]
        x = ctx.enter_context(nc.sbuf_tensor("x", [P, T, D], fp32))
        start_done = ctx.enter_context(k.semaphore(nc, "start_done"))

        def scratch(name, shape, dt=fp32):
            return nc.dram_tensor(name, shape, dt).ap()
        w_spill, ah_spill, mean_spill = (scratch(n, (N, N)) for n in ("w_spill", "ah_spill", "mean_spill"))
        NB0, NB3 = 64 * 78, 8 * 250
        NB2 = 12 * 250
        buf0, buf3, buf2 = (scratch("buf0", (NB0 + 2 * N, D)), scratch("buf3", (NB3 + 2 * N, D)),
                            scratch("buf2", (NB2, D)))
        yb0, yb3 = scratch("yb0", (NB0, D)), scratch("yb3", (NB3, D))
        scr1, scr2 = scratch("scr_minmax", (2, ET)), scratch("scr_tab", (NW, 4), i32)

        load(nc, k, [(k.ident[:, :], a["c_ident"]), (k.tri[:, :], a["c_tri"])])
        with nc.Block() as block:
            @block.vector
            def _(v):
                v.memset(k.ones[:, :], 1.0)
                v.memset(k.ones16[:, :], 1.0)
                v.tensor_copy(k.tri16[:, :], k.tri[:, :])
        with ExitStack() as c2:
            zeros = c2.enter_context(nc.sbuf_tensor("zeros", [128, 2 * D], fp32))
            with nc.Block() as block:
                @block.vector
                def _(v):
                    v.memset(zeros[:, :], 0.0)

            def beside(sp):
                spill_rows(sp, x, rowtiles(a["x"]), start_done)
                n = 32
                for b, rows in ((buf0, NB0), (buf3, NB3), (buf2, NB2)):
                    for r0 in range(0, rows, 256):
                        m = min(256, rows - r0) // 2
                        sp.dma_start(b[r0:r0 + 2 * m, :].rearrange("(p q) n -> p q n", q=2),
                                     zeros[0:m, :].rearrange("p (q n) -> p q n", q=2)).then_inc(start_done, 16)
                        n += 16
                sp.wait_ge(start_done, n)
            CT = c2.enter_context(nc.sbuf_tensor("CT", [P, T, N], fp32))
            WT = c2.enter_context(nc.sbuf_tensor("WT", [P, T, N], fp32))
            build_graph(nc, k, CT, WT, a["src_pt"], a["dst_pt"], a["w_pt"], a["dst_rows"], scr1, scr2, beside)
            W = c2.enter_context(nc.sbuf_tensor("W", [P, T, N], fp32))
            finish_graph(nc, k, CT, WT, W, w_spill, ah_spill, mean_spill)

        k.clear_semaphores(nc)
        l0_gnn(nc, k, a, x, mean_spill)
        k.clear_semaphores(nc)
        transformer(nc, k, a, x, "L0_ffn_", 64, 256, 78, ACT.Gelu_apprx_tanh, False, buf0, yb0)
        k.clear_semaphores(nc)
        graph_layer(nc, k, x, a["L1_gnn_weight"], a["L1_gnn_bias"], w_spill, False, add_rows(x))
        l1_ffn(nc, k, a, x)
        k.clear_semaphores(nc)
        l2_gnn(nc, k, a, x, ah_spill)
        k.clear_semaphores(nc)
        l2_ffn(nc, k, a, x, buf2, buf2)
        k.clear_semaphores(nc)
        graph_layer(nc, k, x, a["L3_gnn_W"], a["L3_gnn_b"], ah_spill, True, add_relu(x))
        k.clear_semaphores(nc)
        transformer(nc, k, a, x, "L3_ffn_", 8, 256, 250, ACT.Gelu, True, buf3, yb3, out)


def layouts(inputs):
    import numpy as _np

    a = {n: _np.asarray(v) for n, v in inputs.items()}

    def heads(w):
        return w.reshape(C, 128, 8, 64).transpose(2, 1, 0, 3)

    def columns(b):
        return b.reshape(-1, 128).T

    w = _np.arange(NW)
    base = P * (w // WPT) + WIN * (w % WPT)
    p = _np.arange(128)
    sel = _np.zeros((128, 2 * WIN), _np.float32)
    sel[p[:WIN], p[:WIN]] = 1
    for m in (1, 2, 3):
        sel[WIN * m + p[:WIN], WIN + p[:WIN]] = 1
    o = {"c_sel": sel, "c_win": _np.stack([base, base + WIN - 1], 1).astype(_np.float32),
         "c_tri": (p[:, None] < p[None, :]).astype(_np.float32), "c_ident": _np.eye(128, dtype=_np.float32),
         "x": a["x"], "src_pt": a["src"].reshape(ET, P).T, "dst_pt": a["dst"].reshape(ET, P).T,
         "w_pt": a["edge_weight"].reshape(ET, P).T, "dst_rows": a["dst"].reshape(80, 4, P)}
    for l in range(2):
        o[f"L0_gnn_Wl{l}T"], o[f"L0_gnn_Wr{l}T"] = a[f"L0_gnn_Wl{l}"].T, a[f"L0_gnn_Wr{l}"].T
        o[f"L0_gnn_bl{l}"] = a[f"L0_gnn_bl{l}"]
    for pre, names in (("L0_ffn_", ("wv", "wo", "wr", "w2", "b2")),
                       ("L3_ffn_", ("wv", "wo", "bo", "bv", "router_w", "router_b", "w2", "b2"))):
        for n in names:
            o[pre + n] = a[pre + n]
        o[pre + "wqk"] = _np.concatenate([heads(a[pre + "wq"]), heads(a[pre + "wk"])], 3)
        for n in ("ln1_g", "ln1_b", "ln2_g", "ln2_b"):
            o[pre + n + "_c"] = columns(a[pre + n])
        e, d, f = a[pre + "w1"].shape
        o[pre + "w1_p"] = a[pre + "w1"].reshape(e, C, 128, f).transpose(0, 2, 1, 3)
        o[pre + "b1_p"] = a[pre + "b1"].reshape(e, f // 128, 128).transpose(0, 2, 1)
    o["L3_ffn_bqk"] = _np.concatenate([a["L3_ffn_bq"].reshape(8, 64), a["L3_ffn_bk"].reshape(8, 64)], 1)
    for n in ("L1_gnn_weight", "L1_gnn_bias", "L3_gnn_W", "L3_gnn_b", "L2_ffn_Wr", "L2_ffn_br", "L2_ffn_W2",
              "L2_ffn_b2", "L1_ffn_gfc2_b", "L1_ffn_tv_b1", "L1_ffn_tv_b2", "L1_ffn_tv_ln_g", "L1_ffn_tv_ln_b",
              "L1_ffn_ln_g", "L1_ffn_ln_b", "L1_ffn_b2"):
        o[n] = a[n]
    o["L2_ffn_w1_p"] = a["L2_ffn_W1"].reshape(8, C, 128, 512).transpose(0, 2, 1, 3)
    o["L2_ffn_b1_p"] = a["L2_ffn_b1"].reshape(8, 4, 128).transpose(0, 2, 1)
    o["L2_gnn_WT"] = a["L2_gnn_W"].transpose(0, 2, 1)
    o["L2_gnn_bgb"] = _np.stack([a["L2_gnn_" + n].reshape(3, C, 128).transpose(2, 0, 1)
                                 for n in ("b", "gamma", "beta")], 1)
    o["L1_ffn_gfc1_wT"], o["L1_ffn_gfc2_wT"] = a["L1_ffn_gfc1_w"].T, a["L1_ffn_gfc2_w"].T
    o["L1_ffn_gfc1_b_c"], o["L1_ffn_b1_c"] = columns(a["L1_ffn_gfc1_b"]), columns(a["L1_ffn_b1"])
    o["L1_ffn_W1T"], o["L1_ffn_W2T"] = a["L1_ffn_W1"].T, a["L1_ffn_W2"].T
    o["L1_ffn_tv_W1_p"] = a["L1_ffn_tv_W1"].reshape(8, 256, C, 128).transpose(3, 0, 2, 1).reshape(128, 8, C * 256)
    o["L1_ffn_tv_W2_p"] = a["L1_ffn_tv_W2"].reshape(8, D, 2, 128).transpose(3, 0, 2, 1).reshape(128, 8, 2 * D)
    return {"in_" + n: _np.ascontiguousarray(v) for n, v in o.items()}


def kernel(**inputs):
    import concourse.bacc as _bacc
    from concourse import mybir as _mybir
    from concourse.bass_utils import run_bass_kernel_spmd as _run

    nc = _bacc.Bacc("TRN2", target_bir_lowering=False, num_devices=1)
    arrays = layouts(inputs)
    a = {n[3:]: nc.dram_tensor(n, v.shape, _mybir.dt.from_np(v.dtype), kind="ExternalInput").ap()
         for n, v in arrays.items()}
    out = nc.dram_tensor("out_x", (N, D), _mybir.dt.float32, kind="ExternalOutput").ap()
    program(nc, a, out)
    r = _run(nc, [arrays], core_ids=[0])
    return r.results[0]["out_x"]
```
